# Optimizing a Trainium2 kernel written in Bass

```python
import numpy as np
import jax
import jax.numpy as jnp

def _softmax(x, axis=-1):
    return jax.nn.softmax(x, axis=axis)

def _gelu(x):
    return jax.nn.gelu(x, approximate=True)

def _silu(x):
    return jax.nn.silu(x)

def _sigmoid(x):
    return jax.nn.sigmoid(x)

def _layernorm(x, axis=-1, eps=1e-05):
    m = jnp.mean(x, axis=axis, keepdims=True)
    v = jnp.var(x, axis=axis, keepdims=True)
    return (x - m) / jnp.sqrt(v + eps)

def _scatter_add(tgt, idx, src, axis=0):
    return tgt.at[idx].add(src)

def _segment_sum(src, seg, n):
    return jax.ops.segment_sum(src, seg, n)
kernel_name = 'mk_seq_preln_d2_jaxref_r8_7820ed'

def setup_inputs(seed: int=0):
    np.random.seed(seed)
    _w = jnp.asarray

    def _L0_attn_setup():
        import math
        import jax, jax.numpy as jnp
        import numpy as np
        B, T, C = (2, 256, 128)
        H = 16
        D = C // H

        def alibi_slopes(n_heads):

            def pow2_slopes(n):
                start = 2.0 ** (-2.0 ** (-(math.log2(n) - 3)))
                return [start * start ** i for i in range(n)]
            if n_heads & n_heads - 1 == 0:
                s = pow2_slopes(n_heads)
            else:
                cp2 = 2 ** math.floor(math.log2(n_heads))
                s = pow2_slopes(cp2)
                extra_base = 2.0 ** (-2.0 ** (-(math.log2(2 * cp2) - 3)))
                s.extend([extra_base * extra_base ** i for i in range(n_heads - cp2)])
                s = s[:n_heads]
            return jnp.asarray(s, dtype=jnp.float32)
        key = jax.random.key(seed)
        k1, k2, k3 = jax.random.split(key, 3)
        x = jax.random.normal(k1, (B, T, C), dtype=jnp.float32)
        W_attn = jax.random.normal(k2, (3 * C, C), dtype=jnp.float32) * 0.02
        W_proj = jax.random.normal(k3, (C, C), dtype=jnp.float32) * 0.02
        return {'x': x, 'W_attn': W_attn, 'W_proj': W_proj}
    _L0_attn_in = _L0_attn_setup()

    def _L0_ffn_setup():
        import jax, jax.numpy as jnp
        import numpy as np
        B, S, HID, DFF, E, K = (4, 256, 128, 512, 8, 256)
        key = jax.random.key(seed)
        ks = jax.random.split(key, 4)
        sc_h = 1.0 / np.sqrt(HID)
        sc_f = 1.0 / np.sqrt(DFF)
        return {'x': jax.random.normal(ks[0], (B, S, HID), jnp.float32), 'router_w': jax.random.normal(ks[1], (HID, E), jnp.float32) * sc_h, 'router_b': jnp.zeros((E,), jnp.float32), 'w1': jax.random.normal(ks[2], (E, HID, DFF), jnp.float32) * sc_h, 'b1': jnp.zeros((E, DFF), jnp.float32), 'w2': jax.random.normal(ks[3], (E, DFF, HID), jnp.float32) * sc_f, 'b2': jnp.zeros((E, HID), jnp.float32)}
    _L0_ffn_in = _L0_ffn_setup()

    def _L1_attn_setup():
        import jax, jax.numpy as jnp
        import numpy as np
        from jax import lax
        D = 128
        K = 3
        LN_EPS = 1e-05

        def _dwconv(v, conv_w, conv_b):
            vt = jnp.transpose(v, (0, 2, 1))
            out = lax.conv_general_dilated(vt, conv_w, window_strides=(1,), padding=[(K // 2, K // 2)], dimension_numbers=('NCH', 'OIH', 'NCH'), feature_group_count=D)
            out = out + conv_b[None, :, None]
            return jnp.transpose(out, (0, 2, 1))
        key = jax.random.key(seed)
        ks = jax.random.split(key, 8)
        B, T = (8, 512)
        x = jax.random.normal(ks[0], (B, T, D), dtype=jnp.float32)
        s = 1.0 / np.sqrt(D)
        in_proj_w = jax.random.uniform(ks[1], (D, 2 * D), jnp.float32, -s, s)
        in_proj_b = jax.random.uniform(ks[2], (2 * D,), jnp.float32, -s, s)
        conv_w = jax.random.uniform(ks[3], (D, 1, K), jnp.float32, -1.0 / np.sqrt(K), 1.0 / np.sqrt(K))
        conv_b = jax.random.uniform(ks[4], (D,), jnp.float32, -1.0 / np.sqrt(K), 1.0 / np.sqrt(K))
        logit_a = jnp.zeros((D,), jnp.float32)
        ssm_b = jnp.full((D,), 0.1, jnp.float32)
        ssm_c = jnp.ones((D,), jnp.float32)
        ssm_d = jnp.zeros((D,), jnp.float32)
        out_proj_w = jax.random.uniform(ks[5], (D, D), jnp.float32, -s, s)
        out_proj_b = jax.random.uniform(ks[6], (D,), jnp.float32, -s, s)
        ln_w = jnp.ones((D,), jnp.float32)
        ln_b = jnp.zeros((D,), jnp.float32)
        return {'x': x, 'in_proj_w': in_proj_w, 'in_proj_b': in_proj_b, 'conv_w': conv_w, 'conv_b': conv_b, 'logit_a': logit_a, 'ssm_b': ssm_b, 'ssm_c': ssm_c, 'ssm_d': ssm_d, 'out_proj_w': out_proj_w, 'out_proj_b': out_proj_b, 'ln_w': ln_w, 'ln_b': ln_b}
    _L1_attn_in = _L1_attn_setup()

    def _L1_ffn_setup():
        import jax, jax.numpy as jnp
        import numpy as np
        E, K = (8, 2)
        DM, DE = (128, 352)
        B, S = (1, 256)
        EPS = 1e-06

        def _rmsnorm(x, w):
            var = jnp.mean(jnp.square(x), axis=-1, keepdims=True)
            return x * jax.lax.rsqrt(var + EPS) * w
        key = jax.random.key(seed)
        kx, kg, k1, k2, k3 = jax.random.split(key, 5)

        def kaiming_uniform(k, shape, fan_in):
            bound = 1.0 / np.sqrt(fan_in)
            return jax.random.uniform(k, shape, jnp.float32, -bound, bound)
        return {'x': jax.random.normal(kx, (B, S, DM), jnp.float32), 'gate_w': kaiming_uniform(kg, (E, DM), DM), 'rms_w': jnp.ones((DM,), jnp.float32), 'W1': kaiming_uniform(k1, (E, DE, DM), DE * DM), 'W2': kaiming_uniform(k2, (E, DE, DM), DE * DM), 'W3': kaiming_uniform(k3, (E, DM, DE), DM * DE)}
    _L1_ffn_in = _L1_ffn_setup()
    _d = {'L0_attn_x': _L0_attn_in['x'], 'L0_attn_W_attn': _L0_attn_in['W_attn'], 'L0_attn_W_proj': _L0_attn_in['W_proj'], 'L0_ffn_router_w': _L0_ffn_in['router_w'], 'L0_ffn_router_b': _L0_ffn_in['router_b'], 'L0_ffn_w1': _L0_ffn_in['w1'], 'L0_ffn_b1': _L0_ffn_in['b1'], 'L0_ffn_w2': _L0_ffn_in['w2'], 'L0_ffn_b2': _L0_ffn_in['b2'], 'L1_attn_in_proj_w': _L1_attn_in['in_proj_w'], 'L1_attn_in_proj_b': _L1_attn_in['in_proj_b'], 'L1_attn_conv_w': _L1_attn_in['conv_w'], 'L1_attn_conv_b': _L1_attn_in['conv_b'], 'L1_attn_logit_a': _L1_attn_in['logit_a'], 'L1_attn_ssm_b': _L1_attn_in['ssm_b'], 'L1_attn_ssm_c': _L1_attn_in['ssm_c'], 'L1_attn_ssm_d': _L1_attn_in['ssm_d'], 'L1_attn_out_proj_w': _L1_attn_in['out_proj_w'], 'L1_attn_out_proj_b': _L1_attn_in['out_proj_b'], 'L1_attn_ln_w': _L1_attn_in['ln_w'], 'L1_attn_ln_b': _L1_attn_in['ln_b'], 'L1_ffn_gate_w': _L1_ffn_in['gate_w'], 'L1_ffn_rms_w': _L1_ffn_in['rms_w'], 'L1_ffn_W1': _L1_ffn_in['W1'], 'L1_ffn_W2': _L1_ffn_in['W2'], 'L1_ffn_W3': _L1_ffn_in['W3']}
    _x0 = _d['L0_attn_x']
    _d['L0_attn_x'] = jax.random.normal(jax.random.fold_in(jax.random.key(seed), 1), (16, 512, 128), dtype=_x0.dtype)
    del _x0
    return _d

def reference(L0_attn_x, L0_attn_W_attn, L0_attn_W_proj, L0_ffn_router_w, L0_ffn_router_b, L0_ffn_w1, L0_ffn_b1, L0_ffn_w2, L0_ffn_b2, L1_attn_in_proj_w, L1_attn_in_proj_b, L1_attn_conv_w, L1_attn_conv_b, L1_attn_logit_a, L1_attn_ssm_b, L1_attn_ssm_c, L1_attn_ssm_d, L1_attn_out_proj_w, L1_attn_out_proj_b, L1_attn_ln_w, L1_attn_ln_b, L1_ffn_gate_w, L1_ffn_rms_w, L1_ffn_W1, L1_ffn_W2, L1_ffn_W3):

    def _L0_attn_ref(x, W_attn, W_proj):
        import math
        import jax, jax.numpy as jnp
        import numpy as np
        B, T, C = (2, 256, 128)
        H = 16
        D = C // H

        def alibi_slopes(n_heads):

            def pow2_slopes(n):
                start = 2.0 ** (-2.0 ** (-(math.log2(n) - 3)))
                return [start * start ** i for i in range(n)]
            if n_heads & n_heads - 1 == 0:
                s = pow2_slopes(n_heads)
            else:
                cp2 = 2 ** math.floor(math.log2(n_heads))
                s = pow2_slopes(cp2)
                extra_base = 2.0 ** (-2.0 ** (-(math.log2(2 * cp2) - 3)))
                s.extend([extra_base * extra_base ** i for i in range(n_heads - cp2)])
                s = s[:n_heads]
            return jnp.asarray(s, dtype=jnp.float32)
        b, t, c = x.shape
        slopes = alibi_slopes(H)
        qkv = jnp.einsum('btc,fc->btf', x, W_attn)
        q, k, v = jnp.split(qkv, 3, axis=-1)
        q = q.reshape(b, t, H, D).transpose(0, 2, 1, 3)
        k = k.reshape(b, t, H, D).transpose(0, 2, 1, 3)
        v = v.reshape(b, t, H, D).transpose(0, 2, 1, 3)
        scale = 1.0 / math.sqrt(D)
        scores = jnp.einsum('bhqd,bhkd->bhqk', q, k) * scale
        pos = jnp.arange(t, dtype=jnp.float32)
        rel = pos[None, :] - pos[:, None]
        causal = pos[None, :] <= pos[:, None]
        bias = slopes[:, None, None] * rel[None, :, :]
        bias = jnp.where(causal[None, :, :], bias, -jnp.inf)
        scores = scores + bias[None]
        att = jax.nn.softmax(scores, axis=-1)
        y = jnp.einsum('bhqk,bhkd->bhqd', att, v)
        y = y.transpose(0, 2, 1, 3).reshape(b, t, c)
        y = jnp.einsum('btc,oc->bto', y, W_proj)
        return y

    def _L0_ffn_ref(x, router_w, router_b, w1, b1, w2, b2):
        import jax, jax.numpy as jnp
        import numpy as np
        B, S, HID, DFF, E, K = (4, 256, 128, 512, 8, 256)
        b, s, h = x.shape
        xf = x.reshape(-1, h)
        logits = xf @ router_w + router_b
        scores = jax.nn.softmax(logits, axis=-1)
        G, idx = jax.lax.top_k(scores.T, K)
        toks = xf[idx]
        h1 = jax.nn.relu(jnp.einsum('ekh,ehf->ekf', toks, w1) + b1[:, None, :])
        eo = jnp.einsum('ekf,efh->ekh', h1, w2) + b2[:, None, :]
        contrib = (eo * G[..., None]).reshape(-1, h)
        y = jnp.zeros_like(xf).at[idx.reshape(-1)].add(contrib)
        return y.reshape(b, s, h)

    def _L1_attn_ref(x, in_proj_w, in_proj_b, conv_w, conv_b, logit_a, ssm_b, ssm_c, ssm_d, out_proj_w, out_proj_b, ln_w, ln_b):
        import jax, jax.numpy as jnp
        import numpy as np
        from jax import lax
        D = 128
        K = 3
        LN_EPS = 1e-05

        def _dwconv(v, conv_w, conv_b):
            vt = jnp.transpose(v, (0, 2, 1))
            out = lax.conv_general_dilated(vt, conv_w, window_strides=(1,), padding=[(K // 2, K // 2)], dimension_numbers=('NCH', 'OIH', 'NCH'), feature_group_count=D)
            out = out + conv_b[None, :, None]
            return jnp.transpose(out, (0, 2, 1))
        B, T, _ = x.shape
        residual = x
        uv = x @ in_proj_w + in_proj_b
        u, v = (uv[..., :D], uv[..., D:])
        v = jax.nn.silu(v)
        v_local = _dwconv(v, conv_w, conv_b)
        a = jax.nn.sigmoid(logit_a).astype(v_local.dtype)

        def step(h, vt):
            h = a * h + ssm_b * vt
            return (h, ssm_c * h + ssm_d * vt)
        h0 = jnp.zeros((B, D), v_local.dtype)
        _, y_seq = lax.scan(step, h0, jnp.transpose(v_local, (1, 0, 2)))
        y_seq = jnp.transpose(y_seq, (1, 0, 2))
        out = u * jax.nn.silu(y_seq)
        out = out @ out_proj_w + out_proj_b
        h = out + residual
        mu = jnp.mean(h, axis=-1, keepdims=True)
        var = jnp.mean(jnp.square(h - mu), axis=-1, keepdims=True)
        return (h - mu) * lax.rsqrt(var + LN_EPS) * ln_w + ln_b

    def _L1_ffn_ref(x, gate_w, rms_w, W1, W2, W3):
        import jax, jax.numpy as jnp
        import numpy as np
        E, K = (8, 2)
        DM, DE = (128, 352)
        B, S = (1, 256)
        EPS = 1e-06

        def _rmsnorm(x, w):
            var = jnp.mean(jnp.square(x), axis=-1, keepdims=True)
            return x * jax.lax.rsqrt(var + EPS) * w
        y = _rmsnorm(x, rms_w)
        logits = jnp.einsum('bsd,ed->bse', y, gate_w)
        vals, idx = jax.lax.top_k(logits, K)
        w = jax.nn.softmax(vals, axis=-1)
        w_full = jnp.einsum('bsk,bske->bse', w, jax.nn.one_hot(idx, E, dtype=x.dtype))
        up = jnp.einsum('bsd,end->bsen', y, W1)
        gate = jnp.einsum('bsd,end->bsen', y, W2)
        h = jax.nn.silu(up) * gate
        out = jnp.einsum('bsen,emn->bsem', h, W3)
        comb = jnp.einsum('bsem,bse->bsm', out, w_full)
        return x + comb
    x = L0_attn_x
    x = x + _L0_attn_ref(_layernorm(x, axis=-1), L0_attn_W_attn, L0_attn_W_proj)
    x = x + _L0_ffn_ref(_layernorm(x, axis=-1), L0_ffn_router_w, L0_ffn_router_b, L0_ffn_w1, L0_ffn_b1, L0_ffn_w2, L0_ffn_b2)
    x = x + _L1_attn_ref(_layernorm(x, axis=-1), L1_attn_in_proj_w, L1_attn_in_proj_b, L1_attn_conv_w, L1_attn_conv_b, L1_attn_logit_a, L1_attn_ssm_b, L1_attn_ssm_c, L1_attn_ssm_d, L1_attn_out_proj_w, L1_attn_out_proj_b, L1_attn_ln_w, L1_attn_ln_b)
    x = x + _L1_ffn_ref(_layernorm(x, axis=-1), L1_ffn_gate_w, L1_ffn_rms_w, L1_ffn_W1, L1_ffn_W2, L1_ffn_W3)
    return x

_drawn_inputs = setup_inputs


def setup_inputs(seed=0):
    import zlib

    import numpy as np

    out = dict(_drawn_inputs(seed))
    spreads = {'L0_ffn_router_b': (0.0, 0.1),
     'L0_ffn_b1': (0.0, 0.44),
     'L0_ffn_b2': (0.0, 0.315),
     'L1_attn_logit_a': (0.0, 0.8),
     'L1_attn_ssm_b': (0.10000000149011612, 0.6),
     'L1_attn_ssm_c': (1.0, 0.6),
     'L1_attn_ssm_d': (0.0, 0.8),
     'L1_attn_ln_w': (1.0, 0.2),
     'L1_attn_ln_b': (0.0, 0.1),
     'L1_ffn_rms_w': (1.0, 0.6)}
    factors = {'L1_attn_in_proj_w': 8.0,
     'L1_attn_in_proj_b': 8.0,
     'L1_attn_conv_w': 8.0,
     'L1_attn_conv_b': 8.0,
     'L1_attn_out_proj_w': 8.0,
     'L1_ffn_gate_w': 51.352,
     'L1_ffn_W1': 48.978,
     'L1_ffn_W2': 48.242,
     'L1_ffn_W3': 48.102,
     'L1_attn_out_proj_b': 37.22}
    for name, (base, spread) in spreads.items():
        noise = np.random.default_rng([zlib.crc32(name.encode()), seed]).standard_normal(out[name].shape)
        drawn = base * np.exp(spread * noise) if base else spread * noise
        out[name] = jnp.asarray(drawn.astype(out[name].dtype))
    for name, factor in factors.items():
        out[name] = (out[name] * factor).astype(out[name].dtype)
    return out
```

```python
from contextlib import ExitStack

import numpy as np
import concourse.bass as bass
from concourse import mybir

F32 = mybir.dt.float32
BF16 = mybir.dt.bfloat16
F16 = mybir.dt.float16
I32 = mybir.dt.int32
ALU = mybir.AluOpType
ACT = mybir.ActivationFunctionType
AX = mybir.AxisListType.X

P = 128
C = 128
T = 512
NB = 16
TT = T // P
EPS = 1e-5

H = 16
D = C // H
G = 4
HG = H // G
TERMS = [(0, 0), (0, 1), (0, 2), (1, 0), (1, 1), (2, 0)]
ROW_ALIBI = 8 * len(TERMS)
ROW_MAX = 96
W = [T - P * j for j in range(TT)]

E = 8
KTOP = 256
BITS = 30
DE = 352
FC = [128, 128, 96]


def attention(nc, x_all, ident, x_in, w_attnT, qkv_scr, max_scr, y_scr, c_ident, c_identb, c_maskq, c_maskk, c_rows, nb=NB):
    with ExitStack() as ctx:
        def sb(name, shape, dt):
            return ctx.enter_context(nc.sbuf_tensor(name, shape, dt))

        def sem(name):
            return ctx.enter_context(nc.semaphore(name))

        qop = [sb(f"qop{i}", [P, H, T], BF16) for i in range(2)]
        kop = [sb(f"kop{i}", [P, H, T], BF16) for i in range(2)]
        vaug = [sb(f"vaug{i}", [P, TT, H, 32], F32) for i in range(2)]
        probs = [[sb(f"probs{i}_{j}", [P, HG, W[j]], F32) for j in range(TT)] for i in range(2)]
        ysb = [sb(f"ysb{i}", [P, T], F32) for i in range(2)]
        identb = sb("identb", [P, P], BF16)
        maskq = sb("maskq", [P, HG, P], BF16)
        maskk = sb("maskk", [P, HG, P], BF16)
        wT = sb("wT", [P, 3, C], F32)
        stats = sb("stats", [P, TT, 6], F32)
        sync6 = sb("sync6", [P, 6], F32)
        mv = sb("mv", [P, TT, 2], F32)
        veps = sb("veps", [P, TT], F32)
        rstd = sb("rstd", [P, TT], F32)
        mhalf = sb("mhalf", [P, TT], F32)
        zeros = sb("zeros", [P, T], F32)
        warm = sb("warm", [P, 1], F32)
        xn = sb("xn", [P, TT, C], F32)
        xT = sb("xT", [P, T], F32)
        parts = [sb(f"parts{n}", [P, 3, T], BF16) for n in range(2)]
        rest = sb("rest", [P, T], F32)
        mx = sb("mx", [P, TT, HG], F32)
        mhl = sb("mhl", [P, TT, 2, HG], BF16)
        mT = sb("mT", [2 * HG, T], BF16)
        psS = [ctx.enter_context(nc.psum_tensor(f"psS{i}", [P, T], F32)) for i in range(2)]
        psE = [ctx.enter_context(nc.psum_tensor(f"psE{i}", [P, 2, T], F32)) for i in range(2)]
        psY = ctx.enter_context(nc.psum_tensor("psY", [P, T], F32))
        psM = ctx.enter_context(nc.psum_tensor("psM", [P, T], F32))
        psMb = psM[:].bitcast(BF16)

        s_first = sem("x_first")
        s_rest = sem("x_rest")
        s_init = sem("init")
        s_vinit = sem("vinit")
        s_rows = sem("rows")
        s_stat = sem("stat")
        s_rstd = sem("rstd_ready")
        s_xn = sem("xn_ready")
        s_mr = sem("misc_ready")
        s_mf = sem("misc_free")
        s_hi = sem("hi_ready")
        s_mid = sem("mid_ready")
        s_lo = sem("lo_ready")
        s_pw = sem("parts_written")
        s_op = sem("operands")
        s_sr = sem("scores_ready")
        s_su = sem("scores_used")
        s_hl = sem("max_parts")
        s_mw = sem("max_written")
        s_mrow = sem("max_rows")
        s_er = sem("exp_in_ready")
        s_ex = sem("exp_done")
        s_pv = sem("pv_done")
        s_yc = sem("y_copied")
        s_yw = sem("y_written")

        UN = 11
        EN = 6
        s_units = []
        for j in range(TT):
            n = [4, 2, 1, 1][j]
            s_units += [(j, h, n) for h in range(0, HG, n)]
        e_units = [(0, 0, 2), (0, 2, 2), (1, 0, 2), (1, 2, 2), (2, 0, 4), (3, 0, 4)]
        ORDER = ["E0", "E1", "S0", "S1", "S2", "E2", "S3", "E3", "S4", "S5", "M", "V0", "S6", "E4", "S7", "V1", "S8",
                 "E5", "S9", "V2", "S10", "V3"]
        REST = 16 * (nb // 2 - 1)
        MISC0 = 4
        MISC = 8

        def muse(g, last):
            return g if last else 2 * g + 1

        QUSE = {0: 0, 1: 2, 2: 4, 3: 6}

        block = ctx.enter_context(nc.Block())

        @block.sync
        def _(sp):
            for dst, src in ((x_all[:, 0:2 * TT, :], x_in[:, 0:2 * TT, :]), (ident[:], c_ident), (identb[:], c_identb),
                             (maskq[:], c_maskq), (maskk[:], c_maskk),
                             (wT[:], w_attnT.rearrange("c (s f) -> c s f", s=3))):
                sp.dma_start(dst, src).then_inc(s_first, 16)
            for n in range(2):
                sp.wait_ge(s_init, n + 1)
                for dst, a, b in ((kop[n][ROW_ALIBI:ROW_ALIBI + 3], 0, 3), (qop[n][ROW_ALIBI:ROW_ALIBI + 3], 3, 6),
                                  (kop[n][ROW_MAX:ROW_MAX + 2], 6, 8)):
                    sp.dma_start(dst.rearrange("p h q -> p (h q)"), c_rows[a:b]).then_inc(s_rows, 16)
            for b in range(1, nb // 2):
                sp.dma_start(x_all[:, 2 * TT * b:2 * TT * b + 2 * TT, :], x_in[:, 2 * TT * b:2 * TT * b + 2 * TT, :]).then_inc(s_rest, 16)

            def place(n, b):
                if not (isinstance(b, int) and b == 0):
                    sp.wait_ge(s_op, 16 * 12 * (b - 1))
                for s in range(2):
                    sp.wait_ge(s_lo, 2 * b + s + 1)
                    sp.dma_start(qkv_scr[n, s], parts[s][:]).then_inc(s_pw, 16)
                for s, op in ((0, qop[n]), (1, kop[n])):
                    sp.wait_ge(s_pw, 32 * b + 32)
                    for i, t in enumerate(TERMS):
                        sp.dma_start(op[8 * i:8 * i + 8], qkv_scr[n, s, :, t[s]].rearrange("(h d) q -> d h q", d=D))\
                            .then_inc(s_op, 16)

            place(0, 0)

            def body(n, b, last):
                for st in range(7):
                    if 1 <= st <= 4:
                        g = st - 1
                        sp.wait_ge(s_mf, MISC0 + MISC * b + muse(g, last) + 1)
                        sp.wait_ge(s_mrow, 16 * (4 * b + g))
                        sp.dma_start(max_scr[g], mT[:]).then_inc(s_mw, 16)
                        sp.wait_ge(s_mw, 16 * (4 * b + g + 1))
                        sp.dma_start(qop[n][ROW_MAX:ROW_MAX + 2, HG * g:HG * g + HG],
                                     max_scr[g].rearrange("(p h) q -> p h q", p=2)).then_inc(s_mrow, 16)
                    if 3 <= st <= 6:
                        g = st - 3
                        sp.wait_ge(s_yc, 4 * b + g + 2)
                        for h in range(HG):
                            sp.dma_start(y_scr[bass.ds(b, 1), :, HG * g + h, :].rearrange("b r q -> (b r) q"),
                                         ysb[g % 2][32 * h:32 * h + 2 * D]).then_inc(s_yw, 16)
                    if st == 4 and not last:
                        place(1 - n, b + 1)

            with sp.Fori(0, nb // 2 - 1) as i:
                for n in range(2):
                    body(n, 2 * i + n, False)
            for b in (nb - 2, nb - 1):
                body(b % 2, b, b == nb - 1)
            sp.wait_ge(s_yw, 64 * 4 * nb)
            sp.wait_ge(s_rest, REST)

        @block.gpsimd
        def _(pool):
            for n in range(2):
                pool.memset(qop[n][:], 0.0)
                pool.memset(kop[n][:], 0.0).then_inc(s_init, 1)
            for n in range(2):
                pool.memset(vaug[n][:], 0.0).then_inc(s_vinit, 1)
            pool.memset(mhalf[:], -0.5).then_inc(s_vinit, 1)
            pool.memset(zeros[:], 0.0).then_inc(s_vinit, 1)
            pool.wait_ge(s_vinit, 4)
            for n in range(2):
                pool.memset(vaug[n][:, :, :, D:2 * D], 1.0).then_inc(s_vinit, 1)

            def prepare(b, first=False):
                pool.wait_ge(s_xn, b)
                pool.wait_ge(s_stat, 3 * b + 3)
                pool.tensor_tensor(rstd[:], veps[:], mhalf[:], ALU.pow).then_inc(s_rstd, 1)
                for s in range(2):
                    pool.wait_ge(s_mf, s + 2 if first else MISC0 + MISC * (b - 1) + 2 * s + 3)
                    pool.tensor_tensor(parts[s][:, 1], rest[:], zeros[:], ALU.add).then_inc(s_mid, 1)
                    pool.wait_ge(s_mid, 2 * b + s + 1)
                    pool.tensor_tensor(parts[s][:, 2], rest[:], parts[s][:, 1], ALU.subtract).then_inc(s_lo, 1)

            prepare(0, True)
            if nb > 2:
                with pool.Fori(1, nb - 1) as b:
                    prepare(b)
            prepare(nb - 1)

        @block.tensor
        def _(pe):
            pe.wait_ge(s_first, 96)

            def x_transposes(b, use):
                pe.wait_ge(s_xn, b + 1)
                if not (use is None):
                    pe.wait_ge(s_mf, use)
                for t in range(TT):
                    mm = pe.transpose(psM[:, P * t:P * t + P], xn[:, t], ident[:])
                mm.then_inc(s_mr, 1)

            def project(which, use):
                pe.wait_ge(s_mf, use)
                if which < 2:
                    pe.matmul(psM[:], wT[:, which], xT[:], start=True, stop=True).then_inc(s_mr, 1)
                else:
                    for t in range(TT):
                        mm = pe.matmul(psM[:, P * t:P * t + P], xT[:, P * t:P * t + P], wT[:, 2], start=True, stop=True)
                    mm.then_inc(s_mr, 1)

            x_transposes(0, None)
            for s in range(3):
                if s == 0:
                    pe.wait_ge(s_yc, 1)
                project(s, s + 1)

            def body(n, b, last):
                ub = MISC0 + MISC * b
                for st in range(6):
                    g, e = st, st - 2
                    if st == 0:
                        pe.wait_ge(s_op, 16 * 12 * (b + 1))
                        pe.wait_ge(s_rows, 96)
                    if 0 <= e < G:
                        pe.wait_ge(s_mrow, 16 * (4 * b + e + 1))
                    for what in ORDER:
                        k = int(what[1:]) if len(what) > 1 else 0
                        if what[0] == "S" and g < G:
                            j, h0, nh = s_units[k]
                            w = P * (j + 1)
                            u = UN * g + k
                            bank = psS[u % 2]
                            pe.wait_ge(s_su, UN * G * b + u)
                            out = bank[:, 0:nh * w].rearrange("p (h k) -> p h k", h=nh)
                            pe.matmul(out[:, :, P * j:w], identb[:], maskq[:, 0:nh, :], start=True, stop=False, skip_group_check=True)
                            for h in range(nh):
                                hh = HG * g + h0 + h
                                mm = pe.matmul(out[:, h, :], qop[n][0:96, hh, P * j:P * j + P], kop[n][0:96, hh, 0:w],
                                               start=False, stop=(h == nh - 1), skip_group_check=True)
                            mm.then_inc(s_sr, 1)
                        if what[0] == "E" and 0 <= e < G:
                            j, h0, nh = e_units[k]
                            u = EN * e + k
                            bank = psE[u % 2]
                            per = nh // 2 if j < 3 else 4
                            pe.wait_ge(s_ex, EN * G * b + u)
                            for h in range(0, nh, per):
                                out = bank[:, h // per, 0:per * W[j]].rearrange("p (h q) -> p h q", h=per)
                                pe.matmul(out[:, :, 0:P], identb[:], maskk[:, 0:per, :], start=True, stop=False, skip_group_check=True)
                                for a in range(per):
                                    hh = HG * e + h0 + h + a
                                    mm = pe.matmul(out[:, a, :], kop[n][:, hh, P * j:P * j + P], qop[n][:, hh, P * j:T],
                                                   start=False, stop=(a == per - 1), skip_group_check=True)
                            mm.then_inc(s_er, 1)
                        if what[0] == "V" and 0 <= e < G:
                            pe.wait_ge(s_ex, 1 + EN * G * b + EN * e + [2, 4, 5, 6][k])
                            if k == 0:
                                pe.wait_ge(s_yc, 4 * b + e + 1)
                            for h in range(HG):
                                mm = pe.matmul(psY[32 * h:32 * h + 32, P * k:T], vaug[n][:, k, HG * e + h, :], probs[e % 2][k][:, h, :],
                                               start=(k == 0), stop=(k == TT - 1), skip_group_check=True)
                            if k == TT - 1:
                                mm.then_inc(s_pv, 1)
                        if what[0] == "M" and 1 <= st <= 4:
                            m = g - 1
                            pe.wait_ge(s_hl, 2 * (4 * b + m + 1))
                            pe.wait_ge(s_mf, ub + muse(m, last))
                            for t in range(TT):
                                mm = pe.transpose(psMb[0:2 * HG, P * t:P * t + P],
                                                  mhl[:, t].rearrange("p a h -> p (a h)"), identb[:])
                            mm.then_inc(s_mr, 1)
                    if not last and st < 4:
                        if st == 0:
                            x_transposes(b + 1, ub)
                        else:
                            project(st - 1, ub + QUSE[st])

            with pe.Fori(0, nb // 2 - 1) as i:
                for n in range(2):
                    body(n, 2 * i + n, False)
            for b in (nb - 2, nb - 1):
                body(b % 2, b, b == nb - 1)

        @block.vector
        def _(dve):
            def norm_stats(b):
                for t in range(TT):
                    bn = dve.bn_stats(stats[:, t], x_all[:, bass.ds(TT * b + t, 1), :].rearrange("p a c -> p (a c)"))
                bn.then_inc(s_stat, 1)
                dve.wait_ge(s_stat, 3 * b + 1)
                dve.tensor_copy(sync6[:], stats[:, TT - 1])
                for t in range(TT):
                    bn = dve.bn_aggr(mv[:, t], stats[:, t])
                bn.then_inc(s_stat, 1)
                dve.wait_ge(s_stat, 3 * b + 2)
                dve.tensor_scalar(veps[:], mv[:, :, 1], EPS, None, ALU.add).then_inc(s_stat, 1)

            def norm_apply(b, used):
                dve.wait_ge(s_rstd, b + 1)
                dve.wait_ge(s_mr, used)
                for t in range(TT):
                    i = dve.tensor_scalar(xn[:, t], x_all[:, bass.ds(TT * b + t, 1), :].rearrange("p a c -> p (a c)"),
                                          mv[:, t, 0:1], rstd[:, t:t + 1], ALU.subtract, ALU.mult)
                i.then_inc(s_xn, 1)

            dve.wait_ge(s_first, 96)
            norm_stats(0)
            norm_apply(0, 0)
            dve.memset(sync6[:], 0.0).then_inc(s_su, 1)
            dve.tensor_scalar(wT[:, 0], wT[:, 0], D ** -0.5, None, ALU.mult).then_inc(s_yc, 1)

            def split(b, s):
                dve.wait_ge(s_hi, 2 * b + s + 1)
                dve.wait_ge(s_lo, 2 * b + s)
                dve.tensor_tensor(rest[:], psM[:], parts[s][:, 0], ALU.subtract).then_inc(s_mf, 1)

            for s in range(2):
                split(0, s)

            def body(n, b, last):
                ub = MISC0 + MISC * b
                for st in range(5):
                    g = st
                    if st == 0 and not last:
                        if n == 1:
                            dve.wait_ge(s_rest, REST)
                        norm_stats(b + 1)
                    if g < G:
                        dve.wait_ge(s_hl, 2 * (4 * b + g))
                    for k in range(UN):
                        if k == 6:
                            if st == 0 and not last:
                                norm_apply(b + 1, ub)
                            if st >= 1:
                                copy_max(b, st - 1, ub + muse(st - 1, last))
                        if g < G:
                            j, h0, nh = s_units[k]
                            u = UN * g + k
                            w = P * (j + 1)
                            dve.wait_ge(s_sr, UN * G * b + u + 1)
                            dve.tensor_reduce(mx[:, j, h0:h0 + nh], psS[u % 2][:, 0:nh * w].rearrange("p (h k) -> p h k", h=nh),
                                              AX, ALU.max).then_inc(s_su, 1)
                    if g < G:
                        dve.wait_ge(s_su, 1 + UN * G * b + UN * (g + 1))
                        dve.wait_ge(s_mr, ub + muse(g - 1, last) + 1 if g else ub)
                        dve.tensor_copy(mhl[:, :, 0], mx[:]).then_inc(s_hl, 1)
                        dve.wait_ge(s_hl, 2 * (4 * b + g) + 1)
                        dve.tensor_tensor(mhl[:, :, 1], mx[:], mhl[:, :, 0], ALU.subtract).then_inc(s_hl, 1)
                    if st in (1, 2) and not last:
                        split(b + 1, st - 1)

            def copy_max(b, g, use):
                dve.wait_ge(s_mr, use + 1)
                dve.wait_ge(s_mw, 16 * (4 * b + g))
                dve.tensor_copy(mT[:], psMb[0:2 * HG, 0:T]).then_inc(s_mf, 1)

            with dve.Fori(0, nb // 2 - 1) as i:
                for n in range(2):
                    body(n, 2 * i + n, False)
            for b in (nb - 2, nb - 1):
                body(b % 2, b, b == nb - 1)

        @block.scalar
        def _(act):
            def copy_x(use):
                act.wait_ge(s_mr, use + 1)
                act.activation(xT[:], psM[:], ACT.Copy).then_inc(s_mf, 1)

            def hi_part(b, s, use):
                act.wait_ge(s_mr, use + 1)
                act.wait_ge(s_pw, 32 * b)
                act.activation(parts[s][:, 0], psM[:], ACT.Copy).then_inc(s_hi, 1)

            def copy_v(n, use):
                act.wait_ge(s_mr, use + 1)
                act.activation(vaug[n][:, :, :, 0:D], psM[:].rearrange("p (t h d) -> p t h d", t=TT, h=H), ACT.Copy)\
                   .then_inc(s_mf, 1)

            copy_x(0)
            for s in range(2):
                hi_part(0, s, s + 1)
            act.wait_ge(s_vinit, 6)
            copy_v(0, 3)
            act.activation(warm[:], ident[:, 0:1], ACT.Exp).then_inc(s_ex, 1)

            def copy_y(b, g):
                act.wait_ge(s_pv, 4 * b + g + 1)
                act.wait_ge(s_yw, 64 * (4 * b + g))
                act.activation(ysb[g % 2][:], psY[:], ACT.Copy).then_inc(s_yc, 1)

            def body(n, b, last):
                ub = MISC0 + MISC * b
                for st in range(7):
                    e = st - 2
                    if 0 <= e < G:
                        act.wait_ge(s_pv, 4 * b + max(e - 1, 0))
                        for k in range(EN):
                            j, h0, nh = e_units[k]
                            u = EN * e + k
                            act.wait_ge(s_er, EN * G * b + u + 1)
                            pr = probs[e % 2][j]
                            if j < 2:
                                src, dst = psE[u % 2][:, :, 0:W[j]], pr[:, h0:h0 + 2, :]
                            elif j == 2:
                                src, dst = psE[u % 2][:], pr[:].rearrange("p (a h) q -> p a (h q)", a=2)
                            else:
                                src, dst = psE[u % 2][:, 0], pr[:].rearrange("p h q -> p (h q)")
                            act.activation(dst, src, ACT.Exp).then_inc(s_ex, 1)
                            if k == 1 and e > 0:
                                copy_y(b, e - 1)
                    if st == 6:
                        copy_y(b, 3)
                    if not last:
                        if st == 0:
                            copy_x(ub)
                        if st in (1, 2):
                            hi_part(b + 1, st - 1, ub + QUSE[st])
                        if st == 3:
                            copy_v(1 - n, ub + QUSE[3])

            with act.Fori(0, nb // 2 - 1) as i:
                for n in range(2):
                    body(n, 2 * i + n, False)
            for b in (nb - 2, nb - 1):
                body(b % 2, b, b == nb - 1)

PAIR = [None]


def half(b, n):
    return b // 2 if isinstance(b, int) else PAIR[0]


def pairs(eng, count, fn):
    if count > 2:
        with eng.Fori(0, count // 2 - 1) as i:
            PAIR[0] = i
            for n in range(2):
                fn(n, 2 * i + n, False)
    for b in (count - 2, count - 1):
        fn(b % 2, b, b == count - 1)


class Norm:
    OPS = 8

    def __init__(self, sb):
        self.stats = sb("stats", [P, TT, 6], F32)
        self.carry = sb("carry", [P, 1], F32)
        self.a = sb("nrm_a", [P, TT], F32)
        self.b = sb("nrm_b", [P, TT], F32)
        self.c = sb("nrm_c", [P, TT], F32)
        self.mean = sb("nrm_mean", [P, TT], F32)
        self.var = sb("nrm_var", [P, TT], F32)
        self.veps = sb("nrm_veps", [P, TT], F32)

    def run(self, dve, src, s, b, eps=EPS):
        st, base = self.stats, self.OPS * b
        me, m2e, mo, m2o = (st[:, :, k] for k in (1, 2, 4, 5))
        dve.wait_ge(s, base)
        dve.memset(self.carry[:], 0.0)
        for t in range(TT):
            i = dve.bn_stats(st[:, t], src(t))
        i.then_inc(s, 1)
        dve.wait_ge(s, base + 1)
        dve.tensor_tensor(self.a[:], me, mo, ALU.subtract).then_inc(s, 1)
        dve.tensor_tensor(self.b[:], m2e, m2o, ALU.add).then_inc(s, 1)
        dve.tensor_tensor(self.mean[:], me, mo, ALU.add).then_inc(s, 1)
        dve.wait_ge(s, base + 4)
        dve.scalar_tensor_tensor(out=self.c[:], in0=self.a[:], scalar=C / 4.0, in1=self.a[:], op0=ALU.mult, op1=ALU.mult)\
            .then_inc(s, 1)
        dve.tensor_scalar(self.mean[:], self.mean[:], 0.5, None, ALU.mult).then_inc(s, 1)
        dve.wait_ge(s, base + 6)
        dve.tensor_tensor(self.var[:], self.b[:], self.c[:], ALU.add).then_inc(s, 1)
        dve.wait_ge(s, base + 7)
        dve.tensor_scalar(self.veps[:], self.var[:], 1.0 / C, eps, ALU.mult, ALU.add).then_inc(s, 1)


def project(nc, x_all, y_scr, w_projT, xbuf, mean_all, rstd_all, nb):
    with ExitStack() as ctx:
        sb = lambda name, shape, dt: ctx.enter_context(nc.sbuf_tensor("pj_" + name, shape, dt))
        sem = lambda name: ctx.enter_context(nc.semaphore("pj_" + name))
        num = [sb(f"num{i}", [P, T], F32) for i in range(2)]
        den = [sb(f"den{i}", [P, T], F32) for i in range(2)]
        rec = [sb(f"rec{i}", [P, T], F32) for i in range(2)]
        y = [sb(f"y{i}", [P, T], F32) for i in range(2)]
        wp = sb("wp", [P, C], F32)
        mhalf = sb("mhalf", [P, TT], F32)
        nrm = Norm(sb)
        ps = [ctx.enter_context(nc.psum_tensor(f"pj_psP{i}", [P, T], F32)) for i in range(2)]
        s_w, s_rec, s_y, s_pr, s_x1, s_chain, s_rs, s_st, s_mh, s_mn = (sem(n) for n in (
            "weights", "rec_ready", "y_ready", "proj_ready", "x1_ready", "chain", "rstd", "stored", "mhalf_set",
            "mean_stored"))
        s_ld = [sem(f"loaded{n}") for n in range(2)]
        block = ctx.enter_context(nc.Block())

        @block.sync
        def _(sp):
            sp.dma_start(wp[:], w_projT).then_inc(s_w, 16)

            for n in range(2):
                sp.dma_start(num[n][:], y_scr[n, 0:8].rearrange("r h q -> (r h) q")).then_inc(s_ld[n], 16)
                sp.dma_start(den[n][:], y_scr[n, 8:16].rearrange("r h q -> (r h) q")).then_inc(s_ld[n], 16)
            with sp.Fori(0, nb // 2 - 1) as i:
                for n in range(2):
                    sp.wait_ge(s_y, 2 * i + n + 1)
                    b = 2 * i + n + 2
                    sp.dma_start(num[n][:], y_scr[bass.ds(b, 1), 0:8].rearrange("b r h q -> (b r h) q")).then_inc(s_ld[n], 16)
                    sp.dma_start(den[n][:], y_scr[bass.ds(b, 1), 8:16].rearrange("b r h q -> (b r h) q")).then_inc(s_ld[n], 16)

        @block.gpsimd
        def _(pool):
            pool.memset(mhalf[:], -0.5).then_inc(s_mh, 1)
            pool.wait_ge(s_mh, 1)

            def body(n, b, last):
                pool.wait_ge(s_rec, b + 1)
                pool.wait_ge(s_pr, b)
                pool.tensor_tensor(y[n][:], num[n][:], rec[n][:], ALU.mult).then_inc(s_y, 1)
                pool.wait_ge(s_chain, Norm.OPS * (b + 1))
                pool.tensor_tensor(rstd_all[:, bass.ds(b * TT, TT)], nrm.veps[:], mhalf[:], ALU.pow).then_inc(s_rs, 1)
            pairs(pool, nb, body)

        @block.tensor
        def _(pe):
            pe.wait_ge(s_w, 16)

            def body(n, b, last):
                pe.wait_ge(s_y, b + 1)
                pe.wait_ge(s_x1, b)
                for t in range(TT):
                    i = pe.matmul(ps[n][:, P * t:P * t + P], y[n][:, P * t:P * t + P], wp[:], start=True, stop=True)
                i.then_inc(s_pr, 1)
            pairs(pe, nb, body)

        @block.vector
        def _(dve):
            dve.wait_ge(s_ld[0], 32)
            dve.reciprocal(rec[0][:], den[0][:]).then_inc(s_rec, 1)

            def body(n, b, last):
                if not last:
                    dve.wait_ge(s_ld[1 - n], 32 * (half(b, n) + n + 1))
                    dve.wait_ge(s_y, b)
                    dve.reciprocal(rec[1 - n][:], den[1 - n][:]).then_inc(s_rec, 1)
                dve.wait_ge(s_pr, b + 1)
                xb = x_all[:, bass.ds(TT * b, TT), :].rearrange("p t c -> p (t c)")
                dve.tensor_tensor(xb, ps[n][:], xb, ALU.add).then_inc(s_x1, 1)
                dve.wait_ge(s_x1, b + 1)
                dve.wait_ge(s_rs, b)
                dve.wait_ge(s_mn, b)
                nrm.run(dve, lambda t: x_all[:, bass.ds(TT * b + t, 1), :].rearrange("p a c -> p (a c)"), s_chain, b)
                dve.tensor_copy(mean_all[:, bass.ds(b * TT, TT)], nrm.mean[:]).then_inc(s_mn, 1)
            pairs(dve, nb, body)

        @block.scalar
        def _(act):
            def body(n, b, last):
                act.wait_ge(s_x1, b + 1)
                act.dma_start(xbuf[:, bass.ds(TT * b, TT), :], x_all[:, bass.ds(TT * b, TT), :]).then_inc(s_st, 16)
            pairs(act, nb, body)
            act.wait_ge(s_st, 16 * nb)


def router(nc, x_all, mean_all, rstd_all, rw, rb, tab, sctab, sc, ident, nb):
    nt = nb * TT
    with ExitStack() as ctx:
        sb = lambda name, shape, dt: ctx.enter_context(nc.sbuf_tensor("ro_" + name, shape, dt))
        sem = lambda name: ctx.enter_context(nc.semaphore("ro_" + name))
        rws = sb("rws", [P, E], F32)
        rbs = sb("rbs", [P, TT, E], F32)
        xn = [sb(f"xn{i}", [P, TT, C], F32) for i in range(2)]
        xT = [sb(f"xT{i}", [P, T], F32) for i in range(2)]
        lg = sb("lg", [P, nt, E], F32)
        ex = sb("ex", [P, nt, E], F32)
        top = sb("top", [P, nt], F32)
        tot = sb("tot", [P, nt], F32)
        psX = [ctx.enter_context(nc.psum_tensor(f"ro_psX{i}", [P, T], F32)) for i in range(2)]
        psL = [ctx.enter_context(nc.psum_tensor(f"ro_psL{i}", [P, TT, E], F32)) for i in range(2)]
        s_w, s_xn, s_tr, s_xT, s_lr, s_lg, s_c, s_ex, s_sc = (sem(n) for n in (
            "weights", "xn_ready", "transposed", "xT_ready", "logits_ready", "logits_kept", "chain",
            "exp_ready", "sc_stored"))
        s_st = [sem(f"stored{n}") for n in range(2)]
        block = ctx.enter_context(nc.Block())

        @block.sync
        def _(sp):
            sp.dma_start(rws[:], rw).then_inc(s_w, 16)
            for t in range(TT):
                sp.dma_start(rbs[:, t], rb.partition_broadcast(P)).then_inc(s_w, 16)

            def body(n, b, last):
                sp.wait_ge(s_xn, b + 1)
                sp.dma_start(tab[:, bass.ds(TT * b, TT), :], xn[n][:]).then_inc(s_st[n], 16)
            pairs(sp, nb, body)
            for n in range(2):
                sp.wait_ge(s_st[n], 8 * nb)
            sp.wait_ge(s_c, 5)
            sp.dma_start(sctab, sc[:]).then_inc(s_sc, 16)
            sp.wait_ge(s_sc, 16)

        @block.vector
        def _(dve):
            def keep(n, b):
                dve.wait_ge(s_lr, b + 1)
                dve.tensor_tensor(lg[:, bass.ds(TT * b, TT), :], psL[n][:], rbs[:], ALU.add).then_inc(s_lg, 1)

            def body(n, b, r):
                dve.wait_ge(s_st[n], 16 * r)
                dve.wait_ge(s_tr, 2 * r)
                for t in range(TT):
                    k = TT * b + t
                    i = dve.tensor_scalar(xn[n][:, t], x_all[:, bass.ds(k, 1), :].rearrange("p a c -> p (a c)"),
                                          mean_all[:, bass.ds(k, 1)], rstd_all[:, bass.ds(k, 1)], ALU.subtract, ALU.mult)
                i.then_inc(s_xn, 1)
            dve.wait_ge(s_w, 16 * 5)
            body(0, 0, 0)
            body(1, 1, 0)
            with dve.Fori(0, nb // 2 - 1) as i:
                for n in range(2):
                    keep(n, 2 * i + n)
                    body(n, 2 * i + n + 2, i + 1)
            for b in (nb - 2, nb - 1):
                keep(b % 2, b)
            dve.wait_ge(s_lg, nb)
            dve.tensor_reduce(top[:], lg[:], AX, ALU.max).then_inc(s_c, 1)
            dve.wait_ge(s_c, 1)
            dve.tensor_tensor(lg[:], lg[:], top[:].unsqueeze(2).to_broadcast([P, nt, E]), ALU.subtract).then_inc(s_c, 1)
            dve.wait_ge(s_ex, 1)
            dve.tensor_reduce(tot[:], ex[:], AX, ALU.add).then_inc(s_c, 1)
            dve.wait_ge(s_c, 3)
            dve.reciprocal(tot[:], tot[:]).then_inc(s_c, 1)
            dve.wait_ge(s_c, 4)
            dve.tensor_tensor(sc[:], ex[:], tot[:].unsqueeze(2).to_broadcast([P, nt, E]), ALU.mult).then_inc(s_c, 1)

        @block.tensor
        def _(pe):
            pe.wait_ge(s_w, 16 * 5)

            def turn(n, b):
                pe.wait_ge(s_xn, b + 1)
                pe.wait_ge(s_xT, b - 1) if not isinstance(b, int) or b > 1 else None
                for t in range(TT):
                    i = pe.transpose(psX[n][:, P * t:P * t + P], xn[n][:, t], ident[:])
                i.then_inc(s_tr, 1)

            def logits(n, b):
                pe.wait_ge(s_xT, b + 1)
                pe.wait_ge(s_lg, b - 1) if not isinstance(b, int) or b > 1 else None
                for t in range(TT):
                    i = pe.matmul(psL[n][:, t], xT[n][:, P * t:P * t + P], rws[:], start=True, stop=True)
                i.then_inc(s_lr, 1)
            turn(0, 0)
            turn(1, 1)
            with pe.Fori(0, nb // 2 - 1) as i:
                for n in range(2):
                    b = 2 * i + n
                    pe.wait_ge(s_xT, b + 1)
                    pe.wait_ge(s_lg, b if n == 0 else b)
                    for t in range(TT):
                        k = pe.matmul(psL[n][:, t], xT[n][:, P * t:P * t + P], rws[:], start=True, stop=True)
                    k.then_inc(s_lr, 1)
                    pe.wait_ge(s_xn, b + 3)
                    for t in range(TT):
                        k = pe.transpose(psX[n][:, P * t:P * t + P], xn[n][:, t], ident[:])
                    k.then_inc(s_tr, 1)
            for b in (nb - 2, nb - 1):
                logits(b % 2, b)

        @block.scalar
        def _(act):
            def body(n, b, last):
                act.wait_ge(s_tr, b + 1)
                act.wait_ge(s_lr, b)
                act.activation(xT[n][:], psX[n][:], ACT.Copy).then_inc(s_xT, 1)
            act.wait_ge(s_tr, 1)
            act.activation(xT[0][:], psX[0][:], ACT.Copy).then_inc(s_xT, 1)
            act.wait_ge(s_tr, 2)
            act.activation(xT[1][:], psX[1][:], ACT.Copy).then_inc(s_xT, 1)
            with act.Fori(0, nb // 2 - 1) as i:
                for n in range(2):
                    b = 2 * i + n + 2
                    act.wait_ge(s_tr, b + 1)
                    act.wait_ge(s_lr, b - 1)
                    act.activation(xT[n][:], psX[n][:], ACT.Copy).then_inc(s_xT, 1)
            act.wait_ge(s_c, 2)
            act.activation(ex[:], lg[:], ACT.Exp).then_inc(s_ex, 1)


def choose(nc, sc, ident, cst, idx, nb):
    nt = nb * TT
    nj = nt * E // P
    BITS = 30
    with ExitStack() as ctx:
        sb = lambda name, shape, dt: ctx.enter_context(nc.sbuf_tensor("ch_" + name, shape, dt))
        sem = lambda name: ctx.enter_context(nc.semaphore("ch_" + name))
        scT = sb("scT", [P, nj * P], F32)
        junk = sb("junk", [P, nj * P], BF16)
        junk2 = sb("junk2", [P, 2 * E, P], BF16)
        cnt = sb("cnt", [P, 1], F16)
        bitx = sb("bitx", [P, 1], I32)
        cand = sb("cand", [P, 1], I32)
        thrb = sb("thrb", [P, P], F32)
        thr = sb("thr", [P, E], F32)
        same = sb("same", [P, P], F16)
        tri = sb("tri", [P, P], BF16)
        ones = sb("ones", [P, P], BF16)
        strict = sb("strict", [nt, nt], BF16)
        pwf = sb("pwf", [P, BITS], F32)
        pwi = sb("pwi", [P, BITS], I32)
        iota = sb("iota", [nt, KTOP], F32)
        tileno = sb("tileno", [nt, E], BF16)
        slotno = sb("slotno", [P, 2 * E], F32)
        gt = sb("gt", [P, nt, E], BF16)
        eq = sb("eq", [P, nt, E], BF16)
        sel = sb("sel", [P, nt, E], BF16)
        cgt = sb("cgt", [P, E], F32)
        tots = sb("tots", [P, E, nt], F32)
        incl = sb("incl", [P, E, nt], F32)
        onesf = sb("onesf", [P, nt], F32)
        pe_ = sb("peq", [P, nt, E], F32)
        pin = sb("pin", [nt, E, P], BF16)
        pex2 = sb("pex2", [nt, E, 2], BF16)
        pex = sb("pex", [nt, E], F32)
        pinc = sb("pinc", [nt, E], F32)
        ge = sb("ge", [nt, E, KTOP], BF16)
        oh = sb("oh", [nt, E, KTOP], BF16)
        rr = sb("rr", [P, 2 * E], F32)
        cn = sb("cn", [P, 2 * E], F32)
        til = sb("til", [P, 2 * E], F32)
        psA = ctx.enter_context(nc.psum_tensor("ch_psA", [P, 512], F32))
        psB = ctx.enter_context(nc.psum_tensor("ch_psB", [P, 512], F32))
        psC = ctx.enter_context(nc.psum_tensor("ch_psC", [P, 512], F32))
        psL = ctx.enter_context(nc.psum_tensor("ch_psL", [P, 4, 512], F32))
        psR = ctx.enter_context(nc.psum_tensor("ch_psR", [P, 512], F32))
        s_cst, s_tr, s_cp, s_cnt, s_tot, s_thr, s_thrT, s_masks, s_pre, s_sel, s_pin, s_pinc, s_off, s_oh, s_look, s_c = (
            sem(n) for n in ("consts", "turned", "scT_ready", "counted", "total", "thr_ready", "thr_turned", "masks",
                             "prefixes", "selected", "pin_ready", "pin_copied", "offsets", "onehots", "looked", "chain"))
        block = ctx.enter_context(nc.Block())

        @block.sync
        def _(sp):
            for dst, name in ((same, "c_same"), (tri, "c_tri"), (ones, "c_ones"), (strict, "c_strict"), (pwf, "c_pwf"),
                              (pwi, "c_pwi"), (iota, "c_iota"), (tileno, "c_tileno"), (slotno, "c_slotno")):
                sp.dma_start(dst[:], cst[name][0:dst.shape[0], 0:dst.shape[1]]).then_inc(s_cst, 16)

        @block.tensor
        def _(pe):
            for j in range(nj):
                i = pe.transpose(psA[:, P * j:P * j + P], sc[:, 16 * j:16 * j + 16, :].rearrange("p t e -> p (t e)"), ident[:])
            i.then_inc(s_tr, 1)
            pe.wait_ge(s_cst, 16 * 9)
            with pe.Fori(0, BITS) as k:
                pe.wait_ge(s_cnt, k + 1)
                pe.matmul(psR[:, 0:1], same[:], cnt[:], start=True, stop=True).then_inc(s_tot, 1)
            pe.wait_ge(s_thr, 1)
            pe.transpose(psA[:, 0:P], thrb[:], ident[:]).then_inc(s_thrT, 1)
            pe.wait_ge(s_masks, 1)
            nn = nt * E
            pe.matmul(psA[:, 0:nn], ones[:], gt[:].rearrange("p t e -> p (t e)"), start=True, stop=True)
            pe.matmul(psB[:, 0:nn], tri[:], eq[:].rearrange("p t e -> p (t e)"), start=True, stop=True)
            pe.matmul(psC[:, 0:nn], ones[:], eq[:].rearrange("p t e -> p (t e)"), start=True, stop=True).then_inc(s_pre, 1)
            pe.wait_ge(s_sel, 1)
            for e in range(E):
                i = pe.matmul(psL[0:nt, e // 4, P * (e % 4):P * (e % 4) + P], sel[:, :, e], tri[:], start=True, stop=True)
            i.then_inc(s_pin, 1)
            pe.wait_ge(s_pinc, 1)
            pe.matmul(psR[0:nt, 0:E], strict[:], pin[:, :, P - 1], start=True, stop=True).then_inc(s_off, 1)
            pe.wait_ge(s_oh, 1)
            for k in range(2 * E):
                e, h = k // 2, k % 2
                ohk = oh[:, e, P * h:P * h + P]
                pe.matmul(psL[:, k // 4, P * (k % 4):P * (k % 4) + P], ohk, pin[:, e, :], start=True, stop=True)
                i = pe.matmul(psR[:, 2 * k:2 * k + 2], ohk, pex2[:, e, :], start=True, stop=True)
            i.then_inc(s_look, 1)

        @block.vector
        def _(dve):
            chain = [0]

            def link(ins):
                chain[0] += 1
                ins.then_inc(s_c, 1)
                dve.wait_ge(s_c, chain[0])

            dve.memset(cand[:], 1 << (BITS - 1))
            link(dve.memset(onesf[:], 1.0))
            dve.wait_ge(s_tr, 1)
            dve.tensor_copy(scT[:], psA[:, 0:nj * P]).then_inc(s_cp, 1)
            dve.wait_ge(s_cst, 16 * 9)
            dve.wait_ge(s_cp, 1)
            with dve.Fori(0, BITS) as k:
                dve.tensor_scalar(junk[:], scT[:], cand[:].bitcast(F32), 0.0, ALU.is_ge, ALU.add, accum_out=cnt[:]).then_inc(s_cnt, 1)
                dve.wait_ge(s_tot, k + 1)
                dve.tensor_scalar(bitx[:], psR[:, 0:1], KTOP - 0.5, pwf[:, bass.ds(k, 1)], ALU.is_lt, ALU.mult).then_inc(s_cp, 1)
                dve.wait_ge(s_cp, 2 * k + 2)
                dve.scalar_tensor_tensor(out=cand[:], in0=bitx[:], scalar=pwi[:, bass.ds(k, 1)], in1=cand[:],
                                         op0=ALU.bitwise_xor, op1=ALU.bitwise_xor).then_inc(s_cp, 1)
                dve.wait_ge(s_cp, 2 * k + 3)
            dve.tensor_copy(thrb[:], cand[:].bitcast(F32).to_broadcast([P, P])).then_inc(s_thr, 1)
            dve.wait_ge(s_thrT, 1)
            link(dve.tensor_copy(thr[:], psA[:, 0:E]))
            tb = thr[:].unsqueeze(1).to_broadcast([P, nt, E])
            dve.tensor_tensor(gt[:], sc[:], tb, ALU.is_gt)
            dve.tensor_tensor(eq[:], sc[:], tb, ALU.is_equal).then_inc(s_masks, 1)
            dve.wait_ge(s_pre, 1)
            nn = nt * E
            dve.tensor_reduce(cgt[:], psA[:, 0:nn].rearrange("p (t e) -> p e t", e=E), AX, ALU.add)
            link(dve.tensor_copy(tots[:], psC[:, 0:nn].rearrange("p (t e) -> p e t", e=E)))
            for e in range(E):
                i = dve.tensor_tensor_scan(incl[:, e], onesf[:], tots[:, e], 0.0, ALU.mult, ALU.add)
            link(i)
            link(dve.tensor_tensor(incl[:], incl[:], tots[:], ALU.subtract))
            link(dve.tensor_tensor(pe_[:], psB[:, 0:nn].rearrange("p (t e) -> p t e", e=E), incl[:].rearrange("p e t -> p t e"), ALU.add))
            link(dve.tensor_tensor(pe_[:], pe_[:], cgt[:].unsqueeze(1).to_broadcast([P, nt, E]), ALU.add))
            link(dve.scalar_tensor_tensor(out=pe_[:], in0=pe_[:], scalar=KTOP + 0.5, in1=eq[:], op0=ALU.is_lt, op1=ALU.mult))
            dve.tensor_tensor(sel[:], pe_[:], gt[:], ALU.add).then_inc(s_sel, 1)
            dve.wait_ge(s_pin, 1)
            dve.tensor_copy(pin[:], psL[0:nt, 0:2].rearrange("p a (e k) -> p (a e) k", e=4)).then_inc(s_pinc, 1)
            dve.wait_ge(s_off, 1)
            dve.tensor_copy(pex2[:, :, 0], psR[0:nt, 0:E])
            dve.tensor_copy(pex2[:, :, 1], tileno[:])
            dve.wait_ge(s_pinc, 1)
            dve.tensor_tensor(pinc[:], psR[0:nt, 0:E], pin[:, :, P - 1], ALU.add)
            link(dve.tensor_copy(pex[:], psR[0:nt, 0:E]))
            for e in range(E):
                i = dve.tensor_scalar(ge[:, e], iota[:], pex[:, e:e + 1], None, ALU.is_ge)
            link(i)
            for e in range(E):
                i = dve.scalar_tensor_tensor(out=oh[:, e], in0=iota[:], scalar=pinc[:, e:e + 1], in1=ge[:, e],
                                             op0=ALU.is_lt, op1=ALU.mult)
            i.then_inc(s_oh, 1)
            dve.wait_ge(s_look, 1)
            pr = psR[:, 0:4 * E].rearrange("p (k a) -> p k a", a=2)
            dve.tensor_copy(til[:], pr[:, :, 1])
            link(dve.tensor_tensor(rr[:], slotno[:], pr[:, :, 0], ALU.subtract))
            for k in range(2 * E):
                i = dve.tensor_scalar(junk2[:, k], psL[:, k // 4, P * (k % 4):P * (k % 4) + P], rr[:, k:k + 1], 0.0,
                                      ALU.is_le, ALU.add, accum_out=cn[:, k:k + 1])
            link(i)
            link(dve.scalar_tensor_tensor(out=idx[:], in0=cn[:], scalar=float(nt), in1=til[:], op0=ALU.mult, op1=ALU.add))


def expert_choice(nc, idx, tab, sctab, w1, b1, w2, b2, xbuf, ident, nb):
    nt = nb * TT
    FT = 4
    with ExitStack() as ctx:
        sb = lambda name, shape, dt: ctx.enter_context(nc.sbuf_tensor("ec_" + name, shape, dt))
        sem = lambda name: ctx.enter_context(nc.semaphore("ec_" + name))
        xg = sb("xg", [P, 2 * E, C], F32)
        gg = sb("gg", [P, 2 * E * E], F32)
        w1s = [sb(f"w1s{i}", [P, FT * P], F32) for i in range(2)]
        w2s = [sb(f"w2s{i}", [P, FT, C], F32) for i in range(2)]
        b1s = sb("b1s", [P, E, FT], F32)
        b2s = sb("b2s", [P, E, C], F32)
        xT = [sb(f"xgT{i}", [P, 2 * P], F32) for i in range(2)]
        hT = [sb(f"hT{i}", [P, FT, 2 * P], F32) for i in range(2)]
        ctr = sb("ctr", [P, 2 * E, C], F32)
        tmp = sb("tmp", [P, 2, C], F32)
        psX = [ctx.enter_context(nc.psum_tensor(f"ec_psX{i}", [P, 2 * P], F32)) for i in range(2)]
        psH = [ctx.enter_context(nc.psum_tensor(f"ec_psH{i}", [P, 2, 512], F32)) for i in range(2)]
        psO = [ctx.enter_context(nc.psum_tensor(f"ec_psO{i}", [P, 2, C], F32)) for i in range(2)]
        s_b, s_xg, s_gg, s_tr, s_xT, s_h, s_hT, s_o, s_t, s_ctr, s_sc = (sem(n) for n in (
            "biases", "gathered", "gates", "turned", "xT_ready", "h_ready", "hT_ready", "o_ready", "tmp_ready",
            "contrib", "scattered"))
        s_w = [sem(f"weights{n}") for n in range(2)]
        block = ctx.enter_context(nc.Block())
        tabr = tab.rearrange("p t c -> (p t) c")
        sctr = sctab.rearrange("p t e -> (p t) e")
        xr = xbuf.rearrange("p t c -> (p t) c")

        @block.gpsimd
        def _(pool):
            for k in range(2 * E):
                off = bass.IndirectOffsetOnAxis(ap=idx[:, k:k + 1], axis=0)
                pool.indirect_dma_start(xg[:, k, :], None, tabr, off).then_inc(s_xg, 16)
                if k % 2:
                    pool.wait_ge(s_xg, 16 * (k + 1))
            for k in range(2 * E):
                off = bass.IndirectOffsetOnAxis(ap=idx[:, k:k + 1], axis=0)
                pool.indirect_dma_start(gg[:, E * k:E * k + E], None, sctr, off).then_inc(s_gg, 16)
            pool.wait_ge(s_gg, 16 * 2 * E)
            for e in range(E):
                pool.wait_ge(s_ctr, e + 1)
                if e:
                    pool.wait_ge(s_sc, 32 * e)
                for k in (2 * e, 2 * e + 1):
                    off = bass.IndirectOffsetOnAxis(ap=idx[:, k:k + 1], axis=0)
                    pool.indirect_dma_start(xr, off, ctr[:, k, :], None, compute_op=ALU.add).then_inc(s_sc, 16)
            pool.wait_ge(s_sc, 32 * E)

        @block.sync
        def _(sp):
            sp.dma_start(b1s[:], b1).then_inc(s_b, 16)
            sp.dma_start(b2s[:], b2.partition_broadcast(P)).then_inc(s_b, 16)

            def load(n, e):
                sp.dma_start(w1s[n][:], w1[bass.ds(e, 1)].rearrange("e c f -> (e c) f")).then_inc(s_w[n], 16)
                sp.dma_start(w2s[n][:], w2[bass.ds(e, 1)].rearrange("e f t c -> (e f) t c")).then_inc(s_w[n], 16)
            load(0, 0)
            load(1, 1)
            with sp.Fori(0, E // 2 - 1) as i:
                for n in range(2):
                    sp.wait_ge(s_o, 2 * i + n + 1)
                    load(n, 2 * i + n + 2)

        @block.tensor
        def _(pe):
            def body(n, e, last):
                pe.wait_ge(s_xg, 32 * (e + 1))
                pe.wait_ge(s_xT, e)
                for h in range(2):
                    i = pe.transpose(psX[n][:, P * h:P * h + P], xg[:, bass.ds(2 * e + h, 1), :].rearrange("p a c -> p (a c)"), ident[:])
                i.then_inc(s_tr, 1)
                pe.wait_ge(s_xT, e + 1)
                pe.wait_ge(s_w[n], 32 * (half(e, n) + 1))
                pe.wait_ge(s_hT, e)
                for f in range(FT):
                    i = pe.matmul(psH[n][:, f // 2, 2 * P * (f % 2):2 * P * (f % 2) + 2 * P], w1s[n][:, P * f:P * f + P], xT[n][:],
                                  start=True, stop=True)
                i.then_inc(s_h, 1)
                pe.wait_ge(s_hT, e + 1)
                pe.wait_ge(s_ctr, e)
                for h in range(2):
                    for f in range(FT):
                        i = pe.matmul(psO[n][:, h], hT[n][:, f, P * h:P * h + P], w2s[n][:, f], start=(f == 0), stop=(f == FT - 1))
                i.then_inc(s_o, 1)
            for e in range(E):
                body(e % 2, e, e == E - 1)

        @block.scalar
        def _(act):
            act.wait_ge(s_b, 32)

            def body(n, e, last):
                act.wait_ge(s_tr, e + 1)
                act.activation(xT[n][:], psX[n][:], ACT.Copy).then_inc(s_xT, 1)
                act.wait_ge(s_h, e + 1)
                for f in range(FT):
                    i = act.activation(hT[n][:, f], psH[n][:, f // 2, 2 * P * (f % 2):2 * P * (f % 2) + 2 * P], ACT.Relu,
                                       bias=b1s[:, bass.ds(e, 1), f:f + 1].rearrange("p a b -> p (a b)"))
                i.then_inc(s_hT, 1)
            for e in range(E):
                body(e % 2, e, e == E - 1)

        @block.vector
        def _(dve):
            dve.wait_ge(s_b, 32)
            dve.wait_ge(s_gg, 16 * 2 * E)

            def body(n, e, last):
                dve.wait_ge(s_o, e + 1)
                dve.wait_ge(s_ctr, e)
                for h in range(2):
                    i = dve.tensor_tensor(tmp[:, h], psO[n][:, h], b2s[:, bass.ds(e, 1), :].rearrange("p a c -> p (a c)"), ALU.add)
                i.then_inc(s_t, 1)
                dve.wait_ge(s_t, e + 1)
                for h in range(2):
                    i = dve.tensor_scalar(ctr[:, bass.ds(2 * e + h, 1), :].rearrange("p a c -> p (a c)"), tmp[:, h],
                                          gg[:, bass.ds((2 * E + 1) * e + E * h, 1)], None, ALU.mult)
                i.then_inc(s_ctr, 1)
            for e in range(E):
                body(e % 2, e, e == E - 1)


def skewed(eng, nb, fn):
    for s in range(2):
        fn(s, s % 2)
    if nb > 2:
        with eng.Fori(0, nb // 2 - 1) as i:
            for n in range(2):
                PAIR[0] = i + 1
                fn(2 * i + n + 2, n)
    for s in (nb, nb + 1):
        fn(s, s % 2)


def live(b, nb):
    return not isinstance(b, int) or 0 <= b < nb


def mixer(nc, x_all, xbuf, ident, win, wout, prm, rows, nb):
    with ExitStack() as ctx:
        sb = lambda name, shape, dt: ctx.enter_context(nc.sbuf_tensor("mx_" + name, shape, dt))
        sem = lambda name: ctx.enter_context(nc.semaphore("mx_" + name))
        two = lambda name, shape, dt=F32: [sb(f"{name}{i}", shape, dt) for i in range(2)]
        win_s = sb("win", [P, 2 * C], F32)
        wout_s = sb("wout", [P, C], F32)
        prm_s = sb("prm", [P, 10], F32)
        col = lambda k: prm_s[:, k:k + 1]
        BU, BV, W0, W1, W2, CB, LA, SB, SC, SD = range(10)
        rows_s = sb("rows", [P, 3, TT, C], F32)
        decay = sb("decay", [P, 1], F32)
        decayb = sb("decayb", [P, T], F32)
        bc = sb("bc", [P, 1], F32)
        mhalf = sb("mhalf", [P, TT], F32)
        carry = sb("carry", [P, 1], F32)
        nrm = Norm(lambda a, b_, c_: sb("i" + a, b_, c_))
        nr2 = Norm(lambda a, b_, c_: sb("o" + a, b_, c_))
        rs1 = sb("rs1", [P, TT], F32)
        rs2 = sb("rs2", [P, TT], F32)
        xn, xT, vs, c0, vl, hs, dv, ys, z, xo, ho, hn, t1, t2 = (two(n, s) for n, s in (
            ("xn", [P, TT, C]), ("xT", [P, T]), ("vs", [P, T + 2]), ("c0", [P, T]), ("vl", [P, T]), ("hs", [P, T]),
            ("dv", [P, T]), ("ys", [P, T]), ("z", [P, T]), ("xo", [P, TT, C]), ("ho", [P, TT, C]), ("hn", [P, TT, C]),
            ("t1", [P, TT, C]), ("t2", [P, TT, C])))
        ps = lambda n: ctx.enter_context(nc.psum_tensor("mx_" + n, [P, T], F32))
        psX = ps("psX")
        psU = [ps("psU0"), ps("psU1")]
        psV = [ps("psV0"), ps("psV1")]
        psO = [ps("psO0"), ps("psO1")]
        s_w, s_ea, s_set, s_n1, s_n2, s_r1, s_r2, s_xn, s_tr, s_xT, s_uv, s_vs, s_c0, s_c, s_dv, s_y, s_ys, s_z, s_o, s_xo, \
            s_h, s_hn, s_t1, s_t2, s_x3, s_pre = (sem(n) for n in (
                "weights", "exp_a", "set", "stat1", "stat2", "rstd1", "rstd2", "xn_ready", "turned", "xT_ready", "uv_ready",
                "v_ready", "conv0", "conv", "dv_ready", "y_ready", "silu_y", "z_ready", "out_ready", "xo_ready", "h_ready",
                "hn_ready", "t1_ready", "t2_ready", "x3_ready", "prepared"))
        s_ld = [sem(f"loaded{n}") for n in range(2)]
        block = ctx.enter_context(nc.Block())

        @block.sync
        def _(sp):
            for dst, src in ((win_s[:], win), (wout_s[:], wout), (prm_s[:], prm)):
                sp.dma_start(dst, src).then_inc(s_w, 16)
            for k in range(3):
                for t in range(TT):
                    sp.dma_start(rows_s[:, k, t], rows[k:k + 1].partition_broadcast(P)).then_inc(s_w, 16)

            def load(n, b):
                sp.dma_start(x_all[:, bass.ds(TT * b, TT), :], xbuf[:, bass.ds(TT * b, TT), :]).then_inc(s_ld[n], 16)
            for n in range(2):
                load(n, n)
            with sp.Fori(0, nb // 2 - 1) as i:
                for n in range(2):
                    sp.wait_ge(s_n1, Norm.OPS * (2 * i + n + 1))
                    load(n, 2 * i + n + 2)

        @block.gpsimd
        def _(pool):
            pool.memset(mhalf[:], -0.5).then_inc(s_set, 1)
            for n in range(2):
                pool.memset(vs[n][:], 0.0).then_inc(s_set, 1)
            pool.wait_ge(s_set, 3)
            pool.wait_ge(s_w, 16 * 15)

            def step(s, n):
                m = 1 - n
                if live(s - 2, nb):
                    b = s - 2
                    pool.wait_ge(s_n2, Norm.OPS * b + 8)
                    pool.wait_ge(s_hn, b)
                    pool.tensor_tensor(rs2[:], nr2.veps[:], mhalf[:], ALU.pow).then_inc(s_r2, 1)
                if live(s, nb):
                    pool.wait_ge(s_n1, Norm.OPS * s + 8)
                    pool.wait_ge(s_xn, s)
                    pool.tensor_tensor(rs1[:], nrm.veps[:], mhalf[:], ALU.pow).then_inc(s_r1, 1)
                if live(s - 1, nb):
                    b = s - 1
                    pool.wait_ge(s_c, 3 * b + 2)
                    pool.tensor_tensor(carry[:], mhalf[:, 0:1], mhalf[:, 0:1], ALU.mult)
                    pool.tensor_scalar(dv[m][:], vl[m][:], col(SD), None, ALU.mult).then_inc(s_dv, 1)
                if live(s - 2, nb):
                    b = s - 2
                    pool.wait_ge(s_x3, b)
                    pool.tensor_tensor(t2[n][:], x_all[:, bass.ds(TT * b, TT), :], rows_s[:, 2], ALU.add).then_inc(s_t2, 1)
                    pool.wait_ge(s_hn, b + 1)
                    pool.tensor_tensor(t1[n][:], hn[n][:], rows_s[:, 1], ALU.mult).then_inc(s_t1, 1)
                if live(s, nb):
                    pool.wait_ge(s_xn, s + 1)
                    pool.wait_ge(s_h, s - 1) if not isinstance(s, int) or s >= 2 else None
                    pool.tensor_tensor(xo[n][:], xn[n][:], rows_s[:, 0], ALU.add).then_inc(s_xo, 1)
                    pool.wait_ge(s_vs, s + 1)
                    pool.wait_ge(s_c, 3 * s - 3) if not isinstance(s, int) or s >= 2 else None
                    pool.tensor_tensor(carry[:], mhalf[:, 0:1], mhalf[:, 0:1], ALU.mult)
                    pool.tensor_scalar(c0[n][:], vs[n][:, 1:T + 1], col(W1), col(CB), ALU.mult, ALU.add).then_inc(s_c0, 1)
            skewed(pool, nb, step)

        @block.tensor
        def _(pe):
            pe.wait_ge(s_w, 16 * 15)

            def step(s, n):
                m = 1 - n
                if live(s, nb):
                    pe.wait_ge(s_xn, s + 1)
                    pe.wait_ge(s_xT, s)
                    for t in range(TT):
                        i = pe.transpose(psX[:, P * t:P * t + P], xn[n][:, t], ident[:])
                    i.then_inc(s_tr, 1)
                    pe.wait_ge(s_xT, s + 1)
                    pe.wait_ge(s_vs, s - 1) if not isinstance(s, int) or s >= 2 else None
                    pe.matmul(psV[n][:], win_s[:, C:2 * C], xT[n][:], start=True, stop=True)
                    pe.wait_ge(s_z, s - 1) if not isinstance(s, int) or s >= 2 else None
                    pe.matmul(psU[n][:], win_s[:, 0:C], xT[n][:], start=True, stop=True).then_inc(s_uv, 1)
                if live(s - 1, nb):
                    b = s - 1
                    pe.wait_ge(s_z, b + 1)
                    pe.wait_ge(s_h, b - 1) if not isinstance(b, int) or b >= 2 else None
                    for t in range(TT):
                        i = pe.matmul(psO[m][:, P * t:P * t + P], z[m][:, P * t:P * t + P], wout_s[:], start=True, stop=True)
                    i.then_inc(s_o, 1)
            skewed(pe, nb, step)

        @block.scalar
        def _(act):
            act.wait_ge(s_w, 16 * 15)
            act.wait_ge(s_set, 3)
            act.activation(decay[:], col(LA), ACT.Exp, scale=-1.0).then_inc(s_ea, 1)

            def step(s, n):
                m = 1 - n
                if live(s - 1, nb):
                    b = s - 1
                    act.wait_ge(s_y, b + 1)
                    act.wait_ge(s_z, b - 1) if not isinstance(b, int) or b >= 2 else None
                    act.activation(ys[m][:], hs[m][:], ACT.Silu).then_inc(s_ys, 1)
                if live(s, nb):
                    act.wait_ge(s_tr, s + 1)
                    act.wait_ge(s_uv, s - 1) if not isinstance(s, int) or s >= 2 else None
                    act.activation(xT[n][:], psX[:], ACT.Copy).then_inc(s_xT, 1)
                    act.wait_ge(s_uv, s + 1)
                    act.wait_ge(s_c, 3 * s - 3) if not isinstance(s, int) or s >= 2 else None
                    act.activation(vs[n][:, 1:T + 1], psV[n][:], ACT.Silu, bias=col(BV)).then_inc(s_vs, 1)
            skewed(act, nb, step)

        @block.vector
        def _(dve):
            dve.wait_ge(s_ea, 1)
            dve.tensor_scalar(decay[:], decay[:], 1.0, None, ALU.add).then_inc(s_pre, 1)
            dve.wait_ge(s_pre, 1)
            dve.reciprocal(decay[:], decay[:]).then_inc(s_pre, 1)
            dve.tensor_tensor(bc[:], col(SB), col(SC), ALU.mult).then_inc(s_pre, 1)
            dve.wait_ge(s_pre, 3)
            dve.tensor_copy(decayb[:], decay[:].to_broadcast([P, T])).then_inc(s_pre, 1)
            dve.wait_ge(s_pre, 4)

            def step(s, n):
                m = 1 - n
                if live(s - 2, nb):
                    b = s - 2
                    dve.wait_ge(s_o, b + 1)
                    dve.wait_ge(s_xo, b + 1)
                    dve.wait_ge(s_r2, b)
                    dve.tensor_tensor(ho[n][:], psO[n][:].rearrange("p (t c) -> p t c", t=TT), xo[n][:], ALU.add).then_inc(s_h, 1)
                    dve.wait_ge(s_h, b + 1)
                    nr2.run(dve, lambda t: ho[n][:, t], s_n2, b)
                if live(s, nb):
                    dve.wait_ge(s_ld[n], 16 * (half(s, n) + 1))
                    dve.wait_ge(s_r1, s)
                    nrm.run(dve, lambda t: x_all[:, bass.ds(TT * s + t, 1), :].rearrange("p a c -> p (a c)"), s_n1, s)
                if live(s - 1, nb):
                    b = s - 1
                    dve.wait_ge(s_c0, b + 1)
                    dve.wait_ge(s_c, 3 * b)
                    dve.scalar_tensor_tensor(out=c0[m][:], in0=vs[m][:, 0:T], scalar=col(W0), in1=c0[m][:], op0=ALU.mult, op1=ALU.add)\
                       .then_inc(s_c, 1)
                    dve.wait_ge(s_c, 3 * b + 1)
                    dve.wait_ge(s_dv, b)
                    dve.scalar_tensor_tensor(out=vl[m][:], in0=vs[m][:, 2:T + 2], scalar=col(W2), in1=c0[m][:], op0=ALU.mult, op1=ALU.add)\
                       .then_inc(s_c, 1)
                    dve.wait_ge(s_c, 3 * b + 2)
                    dve.wait_ge(s_ys, b)
                    dve.tensor_tensor_scan(hs[m][:], decayb[:], vl[m][:], 0.0, ALU.mult, ALU.add).then_inc(s_c, 1)
                    dve.wait_ge(s_c, 3 * b + 3)
                    dve.wait_ge(s_dv, b + 1)
                    dve.scalar_tensor_tensor(out=hs[m][:], in0=hs[m][:], scalar=bc[:, 0:1], in1=dv[m][:], op0=ALU.mult, op1=ALU.add)\
                       .then_inc(s_y, 1)
                if live(s - 2, nb):
                    b = s - 2
                    dve.wait_ge(s_r2, b + 1)
                    dve.wait_ge(s_t1, b)
                    for t in range(TT):
                        i = dve.tensor_scalar(hn[n][:, t], ho[n][:, t], nr2.mean[:, t:t + 1], rs2[:, t:t + 1], ALU.subtract, ALU.mult)
                    i.then_inc(s_hn, 1)
                if live(s, nb):
                    dve.wait_ge(s_r1, s + 1)
                    dve.wait_ge(s_tr, s - 1) if not isinstance(s, int) or s >= 2 else None
                    dve.wait_ge(s_xo, s - 1) if not isinstance(s, int) or s >= 2 else None
                    for t in range(TT):
                        i = dve.tensor_scalar(xn[n][:, t], x_all[:, bass.ds(TT * s + t, 1), :].rearrange("p a c -> p (a c)"),
                                              nrm.mean[:, t:t + 1], rs1[:, t:t + 1], ALU.subtract, ALU.mult)
                    i.then_inc(s_xn, 1)
                if live(s - 1, nb):
                    b = s - 1
                    dve.wait_ge(s_ys, b + 1)
                    dve.wait_ge(s_o, b - 1) if not isinstance(b, int) or b >= 2 else None
                    dve.scalar_tensor_tensor(out=z[m][:], in0=psU[m][:], scalar=col(BU), in1=ys[m][:], op0=ALU.add, op1=ALU.mult)\
                       .then_inc(s_z, 1)
                if live(s - 2, nb):
                    b = s - 2
                    dve.wait_ge(s_t1, b + 1)
                    dve.wait_ge(s_t2, b + 1)
                    dve.tensor_tensor(x_all[:, bass.ds(TT * b, TT), :], t1[n][:], t2[n][:], ALU.add).then_inc(s_x3, 1)
            skewed(dve, nb, step)


def gate(nc, x_all, ident, gate_wT, rms_w, w1t, w2t, c_iotae, w1s, w2s, yT_all, acc_a, acc_b, wfull, wT_scr, nb):
    nt = nb * TT
    nj = nt * E // P
    with ExitStack() as ctx:
        sb = lambda name, shape, dt: ctx.enter_context(nc.sbuf_tensor("gt_" + name, shape, dt))
        sem = lambda name: ctx.enter_context(nc.semaphore("gt_" + name))
        gws = sb("gws", [P, E], F32)
        rmsw = sb("rmsw", [P, 1], F32)
        iotae = sb("iotae", [P, nt, E], F32)
        stats = sb("stats", [P, nt, 6], F32)
        a_, b_, mean, var, veps, rstd, rm, r2, ry, mhalf = (sb(n, [P, nt], F32) for n in (
            "a", "b", "mean", "var", "veps", "rstd", "rm", "r2", "ry", "mhalf"))
        y = [sb(f"y{i}", [P, TT, C], F32) for i in range(2)]
        yT = [sb(f"yT{i}", [P, T], F32) for i in range(2)]
        zeros = sb("zeros", [P, T], F32)
        lg = sb("lg", [P, nt, E], F32)
        oh = [sb(f"oh{i}", [P, nt, E], F32) for i in range(2)]
        pen = sb("pen", [P, nt, E], F32)
        top = [sb(f"top{i}", [P, nt], F32) for i in range(2)]
        low, d, ex, wa, wb = (sb(n, [P, nt], F32) for n in ("low", "d", "ex", "wa", "wb"))
        wTs = sb("wTs", [P, nj * P], F32)
        psX = [ctx.enter_context(nc.psum_tensor(f"gt_psX{i}", [P, T], F32)) for i in range(2)]
        psL = [ctx.enter_context(nc.psum_tensor(f"gt_psL{i}", [P, TT, E], F32)) for i in range(2)]
        psW = ctx.enter_context(nc.psum_tensor("gt_psW", [P, nj * P], F32))
        s_w, s_set, s_c, s_p, s_y, s_tr, s_yT, s_lr, s_lg, s_cp, s_ex, s_wf, s_wt, s_wc, s_out = (sem(n) for n in (
            "weights", "set", "chain", "powers", "y_ready", "turned", "yT_ready", "logits_ready", "logits_kept",
            "yT_kept", "exp_ready", "weights_full", "w_turned", "w_copied", "w_stored"))
        block = ctx.enter_context(nc.Block())

        @block.sync
        def _(sp):
            for dst, src in ((gws[:], gate_wT), (rmsw[:], rms_w), (iotae[:], c_iotae[:, 0:nt]), (w1s[:], w1t), (w2s[:], w2t)):
                sp.dma_start(dst, src).then_inc(s_w, 16)
            sp.wait_ge(s_wc, 1)
            sp.dma_start(wT_scr.rearrange("j q p -> q j p"), wTs[:].rearrange("q (j p) -> q j p", p=P)).then_inc(s_out, 16)
            sp.wait_ge(s_out, 16)

        @block.gpsimd
        def _(pool):
            pool.memset(mhalf[:], -0.5).then_inc(s_set, 1)
            pool.memset(zeros[:], 0.0).then_inc(s_set, 1)
            pool.wait_ge(s_set, 2)
            pool.wait_ge(s_c, 6)
            pool.tensor_tensor(rstd[:], veps[:], mhalf[:], ALU.pow).then_inc(s_p, 1)
            pool.wait_ge(s_c, 9)
            pool.tensor_tensor(r2[:], b_[:], mhalf[:], ALU.pow).then_inc(s_p, 1)

            def body(n, b, last):
                pool.wait_ge(s_yT, b + 1)
                pool.tensor_tensor(yT_all[:, bass.ds(T * b, T)], yT[n][:], zeros[:], ALU.add).then_inc(s_cp, 1)
            pairs(pool, nb, body)

        @block.vector
        def _(dve):
            chain = [0]

            def link(ins):
                chain[0] += 1
                ins.then_inc(s_c, 1)
                dve.wait_ge(s_c, chain[0])

            for t in range(nt):
                i = dve.bn_stats(stats[:, t], x_all[:, t])
            link(i)
            me, m2e, mo, m2o = (stats[:, :, k] for k in (1, 2, 4, 5))
            link(dve.tensor_tensor(a_[:], me, mo, ALU.subtract))
            dve.tensor_tensor(b_[:], m2e, m2o, ALU.add)
            link(dve.tensor_tensor(mean[:], me, mo, ALU.add))
            dve.tensor_scalar(mean[:], mean[:], 0.5, None, ALU.mult)
            link(dve.scalar_tensor_tensor(out=a_[:], in0=a_[:], scalar=C / 4.0, in1=a_[:], op0=ALU.mult, op1=ALU.mult))
            link(dve.tensor_tensor(var[:], b_[:], a_[:], ALU.add))
            link(dve.tensor_scalar(veps[:], var[:], 1.0 / C, EPS, ALU.mult, ALU.add))
            dve.wait_ge(s_p, 1)
            dve.tensor_scalar(acc_a[:], rstd[:], 1.0, None, ALU.add)
            link(dve.tensor_tensor(a_[:], var[:], rstd[:], ALU.mult))
            dve.scalar_tensor_tensor(out=acc_b[:], in0=mean[:], scalar=-1.0, in1=rstd[:], op0=ALU.mult, op1=ALU.mult)
            link(dve.tensor_tensor(a_[:], a_[:], rstd[:], ALU.mult))
            link(dve.tensor_scalar(b_[:], a_[:], 1.0 / C, 1e-6, ALU.mult, ALU.add))
            dve.wait_ge(s_w, 16 * 5)
            dve.tensor_scalar(gws[:], gws[:], rmsw[:, 0:1], None, ALU.mult)
            dve.tensor_scalar(w1s[:], w1s[:], rmsw[:, 0:1], None, ALU.mult)
            dve.tensor_scalar(w2s[:], w2s[:], rmsw[:, 0:1], None, ALU.mult).then_inc(s_set, 1)
            dve.wait_ge(s_p, 2)
            link(dve.tensor_tensor(ry[:], rstd[:], r2[:], ALU.mult))
            base = chain[0]

            def make(n, b, used):
                if used is not None:
                    dve.wait_ge(s_tr, used)
                for t in range(TT):
                    k = TT * b + t
                    i = dve.tensor_scalar(y[n][:, t], x_all[:, bass.ds(k, 1), :].rearrange("p a c -> p (a c)"),
                                          mean[:, bass.ds(k, 1)], ry[:, bass.ds(k, 1)], ALU.subtract, ALU.mult)
                i.then_inc(s_y, 1)

            def keep(n, b):
                dve.wait_ge(s_lr, b + 1)
                dve.tensor_copy(lg[:, bass.ds(TT * b, TT), :], psL[n][:]).then_inc(s_lg, 1)
            make(0, 0, None)
            make(1, 1, None)
            with dve.Fori(0, nb // 2 - 1) as i:
                for n in range(2):
                    make(n, 2 * i + n + 2, 2 * i + n + 1)
                    keep(n, 2 * i + n)
            for b in (nb - 2, nb - 1):
                keep(b % 2, b)
            dve.wait_ge(s_lg, nb)
            for k in range(2):
                link(dve.tensor_reduce(top[k][:], lg[:], AX, ALU.max))
                link(dve.tensor_tensor(pen[:], lg[:], top[k][:].unsqueeze(2).to_broadcast([P, nt, E]), ALU.is_equal))
                link(dve.scalar_tensor_tensor(out=pen[:], in0=pen[:], scalar=-100.0, in1=iotae[:], op0=ALU.mult, op1=ALU.add))
                link(dve.tensor_reduce(low[:], pen[:], AX, ALU.min))
                link(dve.tensor_tensor(oh[k][:], pen[:], low[:].unsqueeze(2).to_broadcast([P, nt, E]), ALU.is_equal))
                if k == 0:
                    link(dve.scalar_tensor_tensor(out=lg[:], in0=oh[0][:], scalar=-1e30, in1=lg[:], op0=ALU.mult, op1=ALU.add))
            link(dve.tensor_tensor(d[:], top[1][:], top[0][:], ALU.subtract))
            dve.wait_ge(s_ex, 1)
            link(dve.tensor_scalar(wa[:], ex[:], 1.0, None, ALU.add))
            link(dve.reciprocal(wa[:], wa[:]))
            link(dve.tensor_tensor(wb[:], ex[:], wa[:], ALU.mult))
            bc = lambda a: a[:].unsqueeze(2).to_broadcast([P, nt, E])
            dve.tensor_tensor(oh[0][:], oh[0][:], bc(wa), ALU.mult)
            link(dve.tensor_tensor(oh[1][:], oh[1][:], bc(wb), ALU.mult))
            dve.tensor_tensor(wfull[:], oh[0][:], oh[1][:], ALU.add).then_inc(s_wf, 1)
            gate.chain = chain[0]
            dve.wait_ge(s_wt, 1)
            dve.tensor_copy(wTs[:], psW[:]).then_inc(s_wc, 1)

        @block.tensor
        def _(pe):
            pe.wait_ge(s_set, 3)

            def turn(n, b):
                for t in range(TT):
                    k = pe.transpose(psX[n][:, P * t:P * t + P], y[n][:, t], ident[:])
                k.then_inc(s_tr, 1)

            def logits(n, b):
                for t in range(TT):
                    k = pe.matmul(psL[n][:, t], yT[n][:, P * t:P * t + P], gws[:], start=True, stop=True)
                k.then_inc(s_lr, 1)
            for b in range(2):
                pe.wait_ge(s_y, b + 1)
                turn(b, b)
            with pe.Fori(0, nb // 2 - 1) as i:
                for n in range(2):
                    b = 2 * i + n
                    pe.wait_ge(s_yT, b + 1)
                    pe.wait_ge(s_lg, b)
                    logits(n, b)
                    pe.wait_ge(s_y, b + 3)
                    turn(n, b + 2)
            for b in (nb - 2, nb - 1):
                pe.wait_ge(s_yT, b + 1)
                pe.wait_ge(s_lg, b - 1)
                logits(b % 2, b)
            pe.wait_ge(s_wf, 1)
            for j in range(nj):
                i = pe.transpose(psW[:, P * j:P * j + P], wfull[:, 16 * j:16 * j + 16, :].rearrange("p t e -> p (t e)"), ident[:])
            i.then_inc(s_wt, 1)

        @block.scalar
        def _(act):
            def copy(n, b, used):
                act.wait_ge(s_tr, b + 1)
                if used is not None:
                    act.wait_ge(s_lr, used)
                    act.wait_ge(s_cp, used)
                act.activation(yT[n][:], psX[n][:], ACT.Copy).then_inc(s_yT, 1)
            copy(0, 0, None)
            copy(1, 1, None)
            with act.Fori(0, nb // 2 - 1) as i:
                for n in range(2):
                    copy(n, 2 * i + n + 2, 2 * i + n + 1)
            act.wait_ge(s_c, 9 + 1 + 5 + 1 + 5 + 1)
            act.activation(ex[:], d[:], ACT.Exp).then_inc(s_ex, 1)


def ffn(nc, x_all, ident, w1s, w2s, w3s, w3, yT_all, acc_a, acc_b, wT_scr, out, nb):
    nt = nb * TT
    NC = E * len(FC)
    with ExitStack() as ctx:
        sb = lambda name, shape, dt: ctx.enter_context(nc.sbuf_tensor("ff_" + name, shape, dt))
        sem = lambda name: ctx.enter_context(nc.semaphore("ff_" + name))
        wbc = [sb(f"wbc{i}", [P, TT, P], F32) for i in range(2)]
        up = [sb(f"up{i}", [P, T], F32) for i in range(2)]
        uw = [sb(f"uw{i}", [P, T], F32) for i in range(2)]
        h = [sb(f"h{i}", [P, T], F32) for i in range(3)]
        warm = sb("warm", [P, 1], F32)
        oT = sb("oT", [P, T], F32)
        psU = [ctx.enter_context(nc.psum_tensor(f"ff_psU{i}", [P, T], F32)) for i in range(2)]
        psG = [ctx.enter_context(nc.psum_tensor(f"ff_psG{i}", [P, T], F32)) for i in range(2)]
        psD = ctx.enter_context(nc.psum_tensor("ff_psD", [P, T], F32))
        psT = ctx.enter_context(nc.psum_tensor("ff_psT", [P, T], F32))
        s_up, s_uw, s_h, s_dn = (sem(n) for n in ("silu_done", "weighted", "h_done", "down_done"))
        s_w, s_u, s_g, s_d, s_oT, s_t, s_base, s_out, s_st = (sem(n) for n in (
            "weights", "up_ready", "gate_ready", "down_complete", "oT_copied", "turned", "base", "out_ready", "stored"))
        s_wb = [sem(f"row_loaded{n}") for n in range(2)]
        block = ctx.enter_context(nc.Block())
        AHEAD = 3

        @block.sync
        def _(sp):
            for f, w in enumerate(FC):
                sp.dma_start(w3s[0:w, f], w3[P * f:P * f + w]).then_inc(s_w, 16)
            with sp.Fori(0, nb) as b:
                for e in range(E):
                    sp.wait_ge(s_uw, NC * b + 3 * e + AHEAD - 3)
                    src = wT_scr.rearrange("j (t e) p -> e (j t) p", e=E)[e, bass.ds(TT * b, TT), :]
                    sp.dma_start(wbc[e % 2][:], src.unsqueeze(0).partition_broadcast(P)).then_inc(s_wb[e % 2], 16)

        @block.tensor
        def _(pe):
            pe.wait_ge(s_w, 16 * len(FC))
            with pe.Fori(0, nb) as b:
                ub = NC * b
                rhs = yT_all[:, bass.ds(T * b, T)]
                for k in range(NC + 1):
                    if k < NC:
                        e, f = k // 3, k % 3
                        w = FC[f]
                        pe.wait_ge(s_up, ub + k + AHEAD - 1)
                        pe.matmul(psU[k % 2][0:w], w1s[:, e, P * f:P * f + w], rhs, start=True, stop=True).then_inc(s_u, 1)
                        pe.wait_ge(s_h, ub + k + AHEAD - 1)
                        pe.matmul(psG[k % 2][0:w], w2s[:, e, P * f:P * f + w], rhs, start=True, stop=True).then_inc(s_g, 1)
                    if k >= 1:
                        j = k - 1
                        e, f = j // 3, j % 3
                        w = FC[f]
                        pe.wait_ge(s_h, ub + j + AHEAD + 1)
                        if j == 0:
                            pe.wait_ge(s_oT, b)
                        mm = pe.matmul(psD[:], w3s[0:w, f, e, :], h[j % 3][0:w], start=(j == 0), stop=(j == NC - 1))
                        mm.then_inc(s_dn, 1)
                pe.wait_ge(s_oT, b + 1)
                pe.wait_ge(s_out, b)
                for t in range(TT):
                    mm = pe.transpose(psT[:, P * t:P * t + P], oT[:, P * t:P * t + P], ident[:])
                mm.then_inc(s_t, 1)

        @block.scalar
        def _(act):
            act.activation(warm[:], ident[:, 0:1], ACT.Copy).then_inc(s_up, AHEAD)
            with act.Fori(0, nb) as b:
                ub = NC * b
                for k in range(NC):
                    w = FC[k % 3]
                    act.wait_ge(s_u, ub + k + 1)
                    act.wait_ge(s_uw, ub + k + AHEAD - 1)
                    act.activation(up[k % 2][0:w], psU[k % 2][0:w], ACT.Silu).then_inc(s_up, 1)
                act.wait_ge(s_dn, ub + NC)
                act.wait_ge(s_t, b)
                act.activation(oT[:], psD[:], ACT.Copy).then_inc(s_oT, 1)
                act.wait_ge(s_out, b + 1)
                act.dma_start(out[:, bass.ds(TT * b, TT), :], x_all[:, bass.ds(TT * b, TT), :]).then_inc(s_st, 16)
            act.wait_ge(s_st, 16 * nb)

        @block.gpsimd
        def _(pool):
            pool.memset(uw[0][:], 0.0).then_inc(s_uw, AHEAD)
            pool.wait_ge(s_uw, AHEAD)
            with pool.Fori(0, nb) as b:
                ub = NC * b
                for k in range(NC):
                    e, f = k // 3, k % 3
                    w = FC[f]
                    pool.wait_ge(s_up, ub + k + AHEAD + 1)
                    pool.wait_ge(s_h, ub + k + AHEAD - 1)
                    if f == 0:
                        pool.wait_ge(s_wb[e % 2], 16 * 4 * b + 16 * (e // 2 + 1))
                    pool.tensor_tensor(uw[k % 2][0:w], up[k % 2][0:w], wbc[e % 2][0:w].rearrange("p t c -> p (t c)"), ALU.mult)\
                        .then_inc(s_uw, 1)

        @block.vector
        def _(dve):
            dve.memset(h[0][:], 0.0).then_inc(s_h, AHEAD)
            dve.wait_ge(s_h, AHEAD)
            with dve.Fori(0, nb) as b:
                ub = NC * b
                for t in range(TT):
                    xt = x_all[:, bass.ds(TT * b + t, 1), :].rearrange("p a c -> p (a c)")
                    i = dve.tensor_scalar(xt, xt, acc_a[:, bass.ds(TT * b + t, 1)], acc_b[:, bass.ds(TT * b + t, 1)],
                                          ALU.mult, ALU.add)
                i.then_inc(s_base, 1)
                for k in range(NC):
                    w = FC[k % 3]
                    dve.wait_ge(s_g, ub + k + 1)
                    dve.wait_ge(s_uw, ub + k + AHEAD + 1)
                    if k >= 3:
                        dve.wait_ge(s_dn, ub + k - 2)
                    dve.tensor_tensor(h[k % 3][0:w], psG[k % 2][0:w], uw[k % 2][0:w], ALU.mult).then_inc(s_h, 1)
                dve.wait_ge(s_t, b + 1)
                dve.wait_ge(s_base, b + 1)
                xb = x_all[:, bass.ds(TT * b, TT), :].rearrange("p t c -> p (t c)")
                dve.tensor_tensor(xb, psT[:], xb, ALU.add).then_inc(s_out, 1)


def two_blocks_kernel(nc, x, wattnT, wprojT, rw, rb, w1, b1, w2, b2, win, wout, prm, rows, gwT, rmsw, W1T, W2T, W3T, cst, out):
    nb = NB
    nt = nb * TT

    def dram(name, shape, dt=F32):
        return nc.dram_tensor(name, shape, dt).ap()

    qkv_scr = dram("qkv_scr", [2, 2, P, 3, T], BF16)
    max_scr = dram("max_scr", [G, 2 * HG, T], BF16)
    y_scr = dram("y_scr", [nb, 2 * D, H, T])
    x_scr = dram("x_scr", [P, nt, C])
    norm_tab = dram("norm_tab", [P, nt, C])
    score_tab = dram("score_tab", [P, nt, E])
    wT_scr = dram("wT_scr", [nt * E // P, P, P])
    with ExitStack() as keep:
        def sb(ctx, name, shape, dt=F32):
            return ctx.enter_context(nc.sbuf_tensor(name, shape, dt))

        x_all = sb(keep, "x_all", [P, nt, C])
        ident = sb(keep, "ident", [P, P])
        with ExitStack() as ctx:
            scores = sb(ctx, "sc", [P, nt, E])
            idx = sb(ctx, "idx", [P, 2 * E], I32)
            mean_all = sb(ctx, "mean_all", [P, nt])
            rstd_all = sb(ctx, "rstd_all", [P, nt])
            attention(nc, x_all, ident, x, wattnT, qkv_scr, max_scr, y_scr, cst["c_ident"], cst["c_identb"],
                      cst["c_maskq"], cst["c_maskk"], cst["c_rows"], nb)
            project(nc, x_all, y_scr, wprojT, x_scr, mean_all, rstd_all, nb)
            router(nc, x_all, mean_all, rstd_all, rw, rb, norm_tab, score_tab, scores, ident, nb)
            choose(nc, scores, ident, cst, idx, nb)
            expert_choice(nc, idx, norm_tab, score_tab, w1, b1, w2, b2, x_scr, ident, nb)
            mixer(nc, x_all, x_scr, ident, win, wout, prm, rows, nb)
        with ExitStack() as ctx:
            w1s = sb(ctx, "w1s", [P, E, DE])
            w2s = sb(ctx, "w2s", [P, E, DE])
            w3s = sb(ctx, "w3s", [P, len(FC), E, C])
            yT_all = sb(ctx, "yT_all", [P, nt * P])
            acc_a = sb(ctx, "acc_a", [P, nt])
            acc_b = sb(ctx, "acc_b", [P, nt])
            wfull = sb(ctx, "wfull", [P, nt, E])
            gate(nc, x_all, ident, gwT, rmsw, W1T, W2T, cst["c_iotae"], w1s, w2s, yT_all, acc_a, acc_b, wfull, wT_scr, nb)
            ffn(nc, x_all, ident, w1s, w2s, w3s, W3T, yT_all, acc_a, acc_b, wT_scr, out, nb)


def constants(nt, bf16):
    i = np.arange(P)
    wide = lambda a, shape, dt: np.ascontiguousarray(np.broadcast_to(a, shape)).astype(dt)
    below = np.where(i[None, :] > i[:, None], np.float32(-1e30), np.float32(0))
    start = 2.0 ** (-2.0 ** (-(np.log2(H) - 3)))
    slopes = np.array([start * start ** k for k in range(H)], dtype=np.float32).astype(np.float64)
    rows, rest = [], slopes[:, None] * (np.arange(T) - T / 2)
    for _ in range(3):
        part = rest.astype(np.float32).astype(bf16)
        rows.append(part)
        rest = rest - part.astype(np.float64)
    rows += [np.ones((H, T), bf16)] * 3 + [-np.ones((H, T), bf16)] * 2
    bits = np.arange(BITS - 1, -1, -1)
    return dict(
        c_ident=np.eye(P, dtype=np.float32), c_identb=np.eye(P, dtype=np.float32).astype(bf16),
        c_maskq=wide(below[:, None], (P, HG, P), bf16), c_maskk=wide(below.T[:, None], (P, HG, P), bf16),
        c_rows=np.stack(rows).reshape(8, H * T),
        c_same=(i[:, None] % E == i[None, :] % E).astype(np.float16),
        c_tri=(i[:, None] <= i[None, :]).astype(bf16), c_ones=np.ones((P, P), bf16),
        c_strict=(i[:, None] < i[None, :]).astype(bf16),
        c_pwf=wide(2.0 ** bits, (P, BITS), np.float32), c_pwi=wide((2 ** bits) // 2, (P, BITS), np.int32),
        c_iota=wide(np.arange(float(KTOP)), (P, KTOP), np.float32), c_tileno=wide(i[:, None], (P, E), bf16),
        c_slotno=wide(i[:, None] + 128.0 * (np.arange(2 * E) % 2)[None], (P, 2 * E), np.float32),
        c_iotae=wide(np.arange(float(E)), (P, nt, E), np.float32))


def layout(a):
    nt = NB * TT
    order = np.arange(C).reshape(H, D).T.reshape(-1)
    c = {k: np.asarray(v) for k, v in a.items()}
    return dict(
        x=c["L0_attn_x"].reshape(nt, P, C).transpose(1, 0, 2), wattnT=c["L0_attn_W_attn"].T,
        wprojT=c["L0_attn_W_proj"].T[order], rw=c["L0_ffn_router_w"], rb=c["L0_ffn_router_b"].reshape(1, E),
        w1=c["L0_ffn_w1"], b1=c["L0_ffn_b1"].reshape(E, 4, P).transpose(2, 0, 1),
        w2=c["L0_ffn_w2"].reshape(E, 4, P, C).transpose(0, 2, 1, 3), b2=c["L0_ffn_b2"].reshape(1, E, C),
        win=c["L1_attn_in_proj_w"], wout=c["L1_attn_out_proj_w"],
        prm=np.stack([c["L1_attn_in_proj_b"][:C], c["L1_attn_in_proj_b"][C:], *c["L1_attn_conv_w"][:, 0].T,
                      c["L1_attn_conv_b"], c["L1_attn_logit_a"], c["L1_attn_ssm_b"], c["L1_attn_ssm_c"],
                      c["L1_attn_ssm_d"]], 1),
        rows=np.stack([c["L1_attn_out_proj_b"], c["L1_attn_ln_w"], c["L1_attn_ln_b"]]),
        gwT=c["L1_ffn_gate_w"].T, rmsw=c["L1_ffn_rms_w"].reshape(P, 1), W1T=c["L1_ffn_W1"].transpose(2, 0, 1),
        W2T=c["L1_ffn_W2"].transpose(2, 0, 1), W3T=c["L1_ffn_W3"].transpose(2, 0, 1))


def kernel(**inputs):
    import concourse.bacc as _bacc
    from concourse.bass_utils import run_bass_kernel_spmd as _run

    nt = NB * TT
    nc = _bacc.Bacc("TRN2", target_bir_lowering=False, num_devices=1)
    host = {**layout(inputs), **constants(nt, mybir.dt.np(BF16))}
    arrays, args, cst = {}, {}, {}
    for name, a in host.items():
        a = np.ascontiguousarray(a)
        arrays[name] = a
        ap = nc.dram_tensor(name, a.shape, mybir.dt.from_np(a.dtype), kind="ExternalInput").ap()
        if name[0:2] == "c_":
            cst[name] = ap
        else:
            args[name] = ap
    out = nc.dram_tensor("out", [P, nt, C], F32, kind="ExternalOutput").ap()
    two_blocks_kernel(nc, cst=cst, out=out, **args)
    r = _run(nc, [arrays], core_ids=[0])
    return r.results[0]["out"].transpose(1, 0, 2).reshape(NB, T, C)
```

```python
from contextlib import ExitStack

import numpy as np
import concourse.bass as bass
from concourse import mybir

F32 = mybir.dt.float32
BF16 = mybir.dt.bfloat16
F16 = mybir.dt.float16
I32 = mybir.dt.int32
ALU = mybir.AluOpType
ACT = mybir.ActivationFunctionType
AX = mybir.AxisListType.X

P = 128
C = 128
T = 512
NB = 16
TT = T // P
EPS = 1e-5

H = 16
D = C // H
G = 4
HG = H // G
TERMS = [(0, 0), (1, 0), (2, 0), (0, 1), (1, 1), (0, 2)]
ROW_ALIBI = 8 * len(TERMS)
ROW_MAX = 96
W = [T - P * j for j in range(TT)]

E = 8
KTOP = 256
BITS = 30
DE = 352
FC = [128, 128, 96]
YP = C + E


def attention(nc, x_all, ident, x_in, w_attnT, qkv_scr, max_scr, y_scr, c_ident, c_identb, c_maskq, c_maskk, c_rows, nb=NB):
    with ExitStack() as ctx:
        def sb(name, shape, dt):
            return ctx.enter_context(nc.sbuf_tensor(name, shape, dt))

        def sem(name):
            return ctx.enter_context(nc.semaphore(name))

        qop = [sb(f"qop{i}", [P, H, T], BF16) for i in range(2)]
        kop = [sb(f"kop{i}", [P, H, T], BF16) for i in range(2)]
        vaug = [sb(f"vaug{i}", [P, TT, H, 32], F32) for i in range(2)]
        probs = [[sb(f"probs{i}_{j}", [P, HG, W[j]], F32) for j in range(TT)] for i in range(2)]
        ysb = [sb(f"ysb{i}", [P, T], F32) for i in range(2)]
        identb = sb("identb", [P, P], BF16)
        maskq = sb("maskq", [P, HG, P], BF16)
        maskk = sb("maskk", [P, HG, P], BF16)
        wT = sb("wT", [P, 3, C], F32)
        stats = sb("stats", [P, TT, 6], F32)
        sync6 = sb("sync6", [P, 6], F32)
        mv = sb("mv", [P, TT, 2], F32)
        veps = sb("veps", [P, TT], F32)
        rstd = sb("rstd", [P, TT], F32)
        mhalf = sb("mhalf", [P, TT], F32)
        zeros = sb("zeros", [P, T], F32)
        warm = sb("warm", [P, 1], F32)
        xn = sb("xn", [P, TT, C], F32)
        xT = sb("xT", [P, T], F32)
        parts = [sb(f"parts{n}", [P, 3, T], BF16) for n in range(2)]
        rest = sb("rest", [P, T], F32)
        mx = sb("mx", [P, TT, HG], F32)
        mhl = sb("mhl", [P, TT, 2, HG], BF16)
        mT = sb("mT", [2 * HG, T], BF16)
        psS = [ctx.enter_context(nc.psum_tensor(f"psS{i}", [P, T], F32)) for i in range(2)]
        psE = [ctx.enter_context(nc.psum_tensor(f"psE{i}", [P, 2, T], F32)) for i in range(2)]
        psY = ctx.enter_context(nc.psum_tensor("psY", [P, T], F32))
        psM = ctx.enter_context(nc.psum_tensor("psM", [P, T], F32))
        psMb = psM[:].bitcast(BF16)

        s_first = sem("x_first")
        s_rest = sem("x_rest")
        s_init = [sem(f"init{i}") for i in range(2)]
        s_vzero = sem("vzero")
        s_vinit = sem("vinit")
        s_rows = [sem(f"rows{i}") for i in range(2)]
        s_stat = sem("stat")
        s_rstd = sem("rstd_ready")
        s_xn = sem("xn_ready")
        s_mr = sem("misc_ready")
        s_mf = sem("misc_free")
        s_hi = sem("hi_ready")
        s_mid = sem("mid_ready")
        s_lo = sem("lo_ready")
        s_pw = sem("parts_written")
        s_op = sem("operands")
        s_sr = sem("scores_ready")
        s_su = sem("scores_used")
        s_hl = sem("max_parts")
        s_mw = sem("max_written")
        s_mrow = sem("max_rows")
        s_er = sem("exp_in_ready")
        s_ex = sem("exp_done")
        s_pv = sem("pv_done")
        s_yc = sem("y_copied")
        s_yw = [sem(f"y_written{i}") for i in range(2)]

        UN = 11
        EN = 6
        s_units = []
        for j in range(TT):
            n = [4, 2, 1, 1][j]
            s_units += [(j, h, n) for h in range(0, HG, n)]
        e_units = [(0, 0, 2), (0, 2, 2), (1, 0, 2), (1, 2, 2), (2, 0, 4), (3, 0, 4)]
        ORDER = ["E0", "E1", "S0", "S1", "M", "S2", "E2", "S3", "E3", "S4", "S5", "V0", "S6", "E4", "S7", "V1", "S8",
                 "E5", "S9", "V2", "S10", "V3"]
        REST = 16 * (nb // 2 - 1)
        MISC0 = 4
        MISC = 2 * G

        def use_max(b, st, last):
            if isinstance(b, int) and b == nb:
                return MISC0 - 1 + MISC * (nb - 1) + G
            return MISC0 - 1 + MISC * b + (st if last else (0, 3, 5, 7)[st])

        def use_next(b, k):
            return MISC0 - 1 + MISC * b + (1, 2, 4, 6)[k]

        def there(u):
            return not isinstance(u, int) or 0 <= u < G * nb

        def steps(eng, step, tail):
            def body(n, b, last):
                for st in range(G):
                    step(n, b, st, last)
            for b in range(2):
                body(b, b, False)
            with eng.Fori(1, nb // 2 - 1) as i:
                for n in range(2):
                    body(n, 2 * i + n, False)
            for b in (nb - 2, nb - 1):
                body(b % 2, b, b == nb - 1)
            for st in range(tail):
                step(0, nb, st, True)

        block = ctx.enter_context(nc.Block())

        @block.sync
        def _(sp):
            for dst, src in ((x_all[:, 0:2 * TT, :], x_in[:, 0:2 * TT, :]), (ident[:], c_ident), (identb[:], c_identb),
                             (maskq[:], c_maskq), (maskk[:], c_maskk),
                             (wT[:], w_attnT.rearrange("c (s f) -> c s f", s=3))):
                sp.dma_start(dst, src).then_inc(s_first, 16)
            def constant_rows(n):
                sp.wait_ge(s_init[n], 2)
                for dst, a, b in ((kop[n][ROW_ALIBI:ROW_ALIBI + 3], 0, 3), (qop[n][ROW_ALIBI:ROW_ALIBI + 3], 3, 6),
                                  (kop[n][ROW_MAX:ROW_MAX + 2], 6, 8)):
                    sp.dma_start(dst.rearrange("p h q -> p (h q)"), c_rows[a:b]).then_inc(s_rows[n], 16)

            def place(n, b):
                if not (isinstance(b, int) and b < 2):
                    sp.wait_ge(s_op, 16 * 6 * (b - 1))
                for s in range(2):
                    sp.wait_ge(s_lo, 2 * b + s + 1)
                    sp.dma_start(qkv_scr[n, s].rearrange("a p q -> p a q"), parts[s][:]).then_inc(s_pw, 16)
                sp.wait_ge(s_pw, 32 * b + 32)
                row = 0
                for k in (3, 2, 1):
                    w = 8 * k
                    q_src = qkv_scr[n, 0, 0:k].rearrange("a (d h) q -> (a d) (h q)", d=D)
                    sp.dma_start(qop[n][row:row + w].rearrange("p h q -> p (h q)"), q_src).then_inc(s_op, 16)
                    k_src = qkv_scr[n, 1, 3 - k].rearrange("(d h) q -> d (h q)", d=D)
                    sp.dma_start(kop[n][row:row + w].rearrange("p h q -> p (h q)"), k_src.unsqueeze(0).to_broadcast([k, D, H * T]))\
                        .then_inc(s_op, 16)
                    row += w

            constant_rows(0)
            place(0, 0)
            for b in range(1, nb // 2):
                sp.dma_start(x_all[:, 2 * TT * b:2 * TT * b + 2 * TT, :], x_in[:, 2 * TT * b:2 * TT * b + 2 * TT, :]).then_inc(s_rest, 16)
            constant_rows(1)

            def step(n, b, st, last):
                u = G * b + st - 1
                if there(u):
                    m, g = (n, st - 1) if st else (1 - n, G - 1)
                    sp.wait_ge(s_mf, use_max(b, st, last) + 1)
                    if not isinstance(u, int) or u:
                        sp.wait_ge(s_mrow, 16 * u)
                    sp.dma_start(max_scr[g], mT[:]).then_inc(s_mw, 16)
                    sp.wait_ge(s_mw, 16 * (u + 1))
                    sp.dma_start(qop[m][ROW_MAX:ROW_MAX + 2, HG * g:HG * g + HG],
                                 max_scr[g].rearrange("(p h) q -> p h q", p=2)).then_inc(s_mrow, 16)
                u = G * b + st - 3
                if there(u):
                    bb, g = (b, st - 3) if st == 3 else (b - 1, st + 1)
                    sp.wait_ge(s_yc, u + 2)
                    for h in range(HG):
                        sp.dma_start(y_scr[bass.ds(bb, 1), :, HG * g + h, :].rearrange("b r q -> (b r) q"),
                                     ysb[g % 2][32 * h:32 * h + 2 * D]).then_inc(s_yw[g % 2], 16)
                if st == 2 and not last:
                    place(1 - n, b + 1)
            steps(sp, step, 3)
            for half_ in s_yw:
                sp.wait_ge(half_, 64 * 2 * nb)
            sp.wait_ge(s_rest, REST)

        @block.gpsimd
        def _(pool):
            pool.memset(mhalf[:], -0.5).then_inc(s_vinit, 1)
            pool.memset(zeros[:], 0.0).then_inc(s_vinit, 1)
            pool.wait_ge(s_vinit, 2)

            def clear_v(n):
                pool.memset(vaug[n][:], 0.0).then_inc(s_vzero, 1)
                pool.wait_ge(s_vzero, n + 1)
                pool.memset(vaug[n][:, :, :, D:2 * D], 1.0).then_inc(s_vinit, 1)

            def prepare(b, first=False):
                pool.wait_ge(s_xn, b)
                pool.wait_ge(s_stat, 3 * b + 3)
                pool.tensor_tensor(rstd[:], veps[:], mhalf[:], ALU.pow).then_inc(s_rstd, 1)
                if first:
                    clear_v(0)
                for s in range(2):
                    pool.wait_ge(s_mf, s + 2 if first else MISC0 + MISC * (b - 1) + 2 * s + 2)
                    pool.tensor_tensor(parts[s][:, 1], rest[:], zeros[:], ALU.add).then_inc(s_mid, 1)
                    pool.wait_ge(s_mid, 2 * b + s + 1)
                    pool.tensor_tensor(parts[s][:, 2], rest[:], parts[s][:, 1], ALU.subtract).then_inc(s_lo, 1)

            prepare(0, True)
            clear_v(1)
            if nb > 2:
                with pool.Fori(1, nb - 1) as b:
                    prepare(b)
            prepare(nb - 1)

        @block.tensor
        def _(pe):
            pe.wait_ge(s_first, 96)

            def x_transposes(b, use):
                pe.wait_ge(s_xn, b + 1)
                if not (use is None):
                    pe.wait_ge(s_mf, use)
                for t in range(TT):
                    mm = pe.transpose(psM[:, P * t:P * t + P], xn[:, t], ident[:])
                mm.then_inc(s_mr, 1)

            def project(which, use):
                pe.wait_ge(s_mf, use)
                if which < 2:
                    pe.matmul(psM[:], wT[:, which], xT[:], start=True, stop=True).then_inc(s_mr, 1)
                else:
                    for t in range(TT):
                        mm = pe.matmul(psM[:, P * t:P * t + P], xT[:, P * t:P * t + P], wT[:, 2], start=True, stop=True)
                    mm.then_inc(s_mr, 1)

            x_transposes(0, None)
            for s in range(3):
                if s == 0:
                    pe.wait_ge(s_yc, 1)
                project(s, s + 1)

            def step(n, b, st, last):
                    g = st
                    u_exp = G * b + st - 2
                    m, e = (n, st - 2) if st >= 2 else (1 - n, st + 2)
                    if st == 0 and there(G * b):
                        pe.wait_ge(s_op, 16 * 6 * (b + 1))
                        pe.wait_ge(s_rows[n], 48)
                    if there(u_exp):
                        pe.wait_ge(s_mrow, 16 * (u_exp + 1))
                    for what in ORDER:
                        if what == "S6" and st == 0 and not last:
                            x_transposes(b + 1, use_next(b, 0))
                        k = int(what[1:]) if len(what) > 1 else 0
                        if what[0] == "S" and there(G * b):
                            j, h0, nh = s_units[k]
                            w = P * (j + 1)
                            u = UN * g + k
                            bank = psS[u % 2]
                            pe.wait_ge(s_su, UN * G * b + u)
                            out = bank[:, 0:nh * w].rearrange("p (h k) -> p h k", h=nh)
                            pe.matmul(out[:, :, P * j:w], identb[:], maskq[:, 0:nh, :], start=True, stop=False, skip_group_check=True)
                            for h in range(nh):
                                hh = HG * g + h0 + h
                                mm = pe.matmul(out[:, h, :], qop[n][0:96, hh, P * j:P * j + P], kop[n][0:96, hh, 0:w],
                                               start=False, stop=(h == nh - 1), skip_group_check=True)
                            mm.then_inc(s_sr, 1)
                        if what[0] == "E" and there(u_exp):
                            j, h0, nh = e_units[k]
                            u = k
                            bank = psE[u % 2]
                            per = nh // 2 if j < 3 else 4
                            pe.wait_ge(s_ex, EN * u_exp + u)
                            for h in range(0, nh, per):
                                out = bank[:, h // per, 0:per * W[j]].rearrange("p (h q) -> p h q", h=per)
                                pe.matmul(out[:, :, 0:P], identb[:], maskk[:, 0:per, :], start=True, stop=False, skip_group_check=True)
                                for a in range(per):
                                    hh = HG * e + h0 + h + a
                                    mm = pe.matmul(out[:, a, :], kop[m][:, hh, P * j:P * j + P], qop[m][:, hh, P * j:T],
                                                   start=False, stop=(a == per - 1), skip_group_check=True)
                            mm.then_inc(s_er, 1)
                        if what[0] == "V" and there(u_exp):
                            pe.wait_ge(s_ex, 1 + EN * u_exp + [2, 4, 5, 6][k])
                            if k == 0:
                                pe.wait_ge(s_yc, u_exp + 1)
                            for h in range(HG):
                                mm = pe.matmul(psY[32 * h:32 * h + 32, P * k:T], vaug[m][:, k, HG * e + h, :], probs[e % 2][k][:, h, :],
                                               start=(k == 0), stop=(k == TT - 1), skip_group_check=True)
                            if k == TT - 1:
                                mm.then_inc(s_pv, 1)
                        if what[0] == "M" and there(G * b + st - 1):
                            pe.wait_ge(s_hl, 2 * (G * b + st))
                            pe.wait_ge(s_mf, use_max(b, st, last))
                            for t in range(TT):
                                mm = pe.transpose(psMb[0:2 * HG, P * t:P * t + P],
                                                  mhl[:, t].rearrange("p a h -> p (a h)"), identb[:])
                            mm.then_inc(s_mr, 1)
                    if not last and st < 3:
                        project(st, use_next(b, st + 1))
            steps(pe, step, 2)

        @block.vector
        def _(dve):
            def norm_stats(b):
                for t in range(TT):
                    bn = dve.bn_stats(stats[:, t], x_all[:, bass.ds(TT * b + t, 1), :].rearrange("p a c -> p (a c)"))
                bn.then_inc(s_stat, 1)
                dve.wait_ge(s_stat, 3 * b + 1)
                dve.tensor_copy(sync6[:], stats[:, TT - 1])
                for t in range(TT):
                    bn = dve.bn_aggr(mv[:, t], stats[:, t])
                bn.then_inc(s_stat, 1)
                dve.wait_ge(s_stat, 3 * b + 2)
                dve.tensor_scalar(veps[:], mv[:, :, 1], EPS, None, ALU.add).then_inc(s_stat, 1)

            def norm_apply(b, used):
                dve.wait_ge(s_rstd, b + 1)
                dve.wait_ge(s_mr, used)
                for t in range(TT):
                    i = dve.tensor_scalar(xn[:, t], x_all[:, bass.ds(TT * b + t, 1), :].rearrange("p a c -> p (a c)"),
                                          mv[:, t, 0:1], rstd[:, t:t + 1], ALU.subtract, ALU.mult)
                i.then_inc(s_xn, 1)

            dve.memset(qop[0][:].bitcast(F32), 0.0).then_inc(s_init[0], 1)
            dve.memset(kop[0][:].bitcast(F32), 0.0).then_inc(s_init[0], 1)
            dve.wait_ge(s_first, 96)
            norm_stats(0)
            norm_apply(0, 0)
            dve.memset(sync6[:], 0.0).then_inc(s_su, 1)
            dve.tensor_scalar(wT[:, 0], wT[:, 0], D ** -0.5, None, ALU.mult).then_inc(s_yc, 1)

            def split(b, s):
                dve.wait_ge(s_hi, 2 * b + s + 1)
                dve.wait_ge(s_lo, 2 * b + s)
                dve.tensor_tensor(rest[:], psM[:], parts[s][:, 0], ALU.subtract).then_inc(s_mf, 1)

            for s in range(2):
                split(0, s)
            dve.memset(qop[1][:].bitcast(F32), 0.0).then_inc(s_init[1], 1)
            dve.memset(kop[1][:].bitcast(F32), 0.0).then_inc(s_init[1], 1)

            def step(n, b, st, last):
                g = st
                real = there(G * b)
                if st == 0 and not last:
                    if n == 1:
                        dve.wait_ge(s_rest, REST)
                    norm_stats(b + 1)
                if real and there(G * b + g - 1):
                    dve.wait_ge(s_hl, 2 * (G * b + g))
                for k in range(UN):
                    if k == 2:
                        if there(G * b + st - 1):
                            dve.wait_ge(s_mr, use_max(b, st, last) + 1)
                            if there(G * b + st - 2):
                                dve.wait_ge(s_mw, 16 * (G * b + st - 1))
                            dve.tensor_copy(mT[:], psMb[0:2 * HG, 0:T]).then_inc(s_mf, 1)
                        if st == 0 and not last:
                            norm_apply(b + 1, use_max(b, st, last))
                    if real:
                        j, h0, nh = s_units[k]
                        u = UN * g + k
                        w = P * (j + 1)
                        dve.wait_ge(s_sr, UN * G * b + u + 1)
                        dve.tensor_reduce(mx[:, j, h0:h0 + nh], psS[u % 2][:, 0:nh * w].rearrange("p (h k) -> p h k", h=nh),
                                          AX, ALU.max).then_inc(s_su, 1)
                if real:
                    dve.wait_ge(s_su, 1 + UN * G * b + UN * (g + 1))
                    if there(G * b + st - 1):
                        dve.wait_ge(s_mr, use_max(b, st, last) + 1)
                    dve.tensor_copy(mhl[:, :, 0], mx[:]).then_inc(s_hl, 1)
                    dve.wait_ge(s_hl, 2 * (G * b + g) + 1)
                    dve.tensor_tensor(mhl[:, :, 1], mx[:], mhl[:, :, 0], ALU.subtract).then_inc(s_hl, 1)
                if st in (0, 1) and not last:
                    split(b + 1, st)
            steps(dve, step, 1)

        @block.scalar
        def _(act):
            def copy_x(use):
                act.wait_ge(s_mr, use + 1)
                act.activation(xT[:], psM[:], ACT.Copy).then_inc(s_mf, 1)

            def hi_part(b, s, use):
                act.wait_ge(s_mr, use + 1)
                act.wait_ge(s_pw, 32 * b)
                act.activation(parts[s][:, 0], psM[:], ACT.Copy).then_inc(s_hi, 1)

            def copy_v(n, use):
                act.wait_ge(s_mr, use + 1)
                act.activation(vaug[n][:, :, :, 0:D], psM[:].rearrange("p (t h d) -> p t h d", t=TT, h=H), ACT.Copy)\
                   .then_inc(s_mf, 1)

            copy_x(0)
            for s in range(2):
                hi_part(0, s, s + 1)
            act.wait_ge(s_vinit, 3)
            copy_v(0, 3)
            act.activation(warm[:], ident[:, 0:1], ACT.Exp).then_inc(s_ex, 1)

            def copy_y(u, g):
                act.wait_ge(s_pv, u + 1)
                if there(u - 2):
                    act.wait_ge(s_yw[g % 2], 32 * (u - g % 2))
                act.activation(ysb[g % 2][:], psY[:], ACT.Copy).then_inc(s_yc, 1)

            def step(n, b, st, last):
                u = G * b + st - 2
                if there(u):
                    if there(u - 2):
                        act.wait_ge(s_pv, u - 1)
                    for k in range(EN):
                        j, h0, nh = e_units[k]
                        act.wait_ge(s_er, EN * u + k + 1)
                        bank, pr = psE[k % 2], probs[st % 2][j]
                        if j < 2:
                            src, dst = bank[:, :, 0:W[j]], pr[:, h0:h0 + 2, :]
                        elif j == 2:
                            src, dst = bank[:], pr[:].rearrange("p (a h) q -> p a (h q)", a=2)
                        else:
                            src, dst = bank[:, 0], pr[:].rearrange("p h q -> p (h q)")
                        act.activation(dst, src, ACT.Exp).then_inc(s_ex, 1)
                        if k == 1 and there(u - 1):
                            copy_y(u - 1, st + 1)
                        if k == 3 and st == 0 and not last:
                            copy_x(use_next(b, 0))
                if not last:
                    if st == 0 and not there(u):
                        copy_x(use_next(b, 0))
                    if st in (0, 1):
                        hi_part(b + 1, st, use_next(b, st + 1))
                    if st == 2:
                        if isinstance(b, int) and b == 0:
                            act.wait_ge(s_vinit, 4)
                        copy_v(1 - n, use_next(b, 3))
            steps(act, step, 2)
            copy_y(G * nb - 1, 1)

PAIR = [None]


def half(b, n):
    return b // 2 if isinstance(b, int) else PAIR[0]


def pairs(eng, count, fn):
    for b in range(2):
        fn(b, b, False)
    with eng.Fori(1, count // 2 - 1) as i:
        PAIR[0] = i
        for n in range(2):
            fn(n, 2 * i + n, False)
    for b in (count - 2, count - 1):
        fn(b % 2, b, b == count - 1)


class Norm:
    OPS = 8

    def __init__(self, sb):
        self.stats = sb("stats", [P, TT, 6], F32)
        self.carry = sb("carry", [P, 1], F32)
        self.a = sb("nrm_a", [P, TT], F32)
        self.b = sb("nrm_b", [P, TT], F32)
        self.c = sb("nrm_c", [P, TT], F32)
        self.mean = sb("nrm_mean", [P, TT], F32)
        self.var = sb("nrm_var", [P, TT], F32)
        self.veps = sb("nrm_veps", [P, TT], F32)

    def run(self, dve, src, s, b, eps=EPS):
        st, base = self.stats, self.OPS * b
        me, m2e, mo, m2o = (st[:, :, k] for k in (1, 2, 4, 5))
        dve.wait_ge(s, base)
        dve.memset(self.carry[:], 0.0)
        for t in range(TT):
            i = dve.bn_stats(st[:, t], src(t))
        i.then_inc(s, 1)
        dve.wait_ge(s, base + 1)
        dve.tensor_tensor(self.a[:], me, mo, ALU.subtract).then_inc(s, 1)
        dve.tensor_tensor(self.b[:], m2e, m2o, ALU.add).then_inc(s, 1)
        dve.tensor_tensor(self.mean[:], me, mo, ALU.add).then_inc(s, 1)
        dve.wait_ge(s, base + 4)
        dve.scalar_tensor_tensor(out=self.c[:], in0=self.a[:], scalar=C / 4.0, in1=self.a[:], op0=ALU.mult, op1=ALU.mult)\
            .then_inc(s, 1)
        dve.tensor_scalar(self.mean[:], self.mean[:], 0.5, None, ALU.mult).then_inc(s, 1)
        dve.wait_ge(s, base + 6)
        dve.tensor_tensor(self.var[:], self.b[:], self.c[:], ALU.add).then_inc(s, 1)
        dve.wait_ge(s, base + 7)
        dve.tensor_scalar(self.veps[:], self.var[:], 1.0 / C, eps, ALU.mult, ALU.add).then_inc(s, 1)


def lead_pairs(count, eng, fn, lead=2, tail=2):
    for s in range(lead):
        fn(s % 2, s)
    with eng.Fori(lead // 2, (count - tail) // 2) as i:
        for n in range(2):
            fn(n, 2 * i + n)
    for s in range(count - tail, count):
        fn(s % 2, s)


def project(nc, x_all, y_scr, rec_scr, w_projT, xbuf, rw, rb, tab, sctab, sc, ident, nb):
    nt = nb * TT
    nd = nb * H * T // P
    with ExitStack() as ctx:
        sb = lambda name, shape, dt: ctx.enter_context(nc.sbuf_tensor("pj_" + name, shape, dt))
        sem = lambda name: ctx.enter_context(nc.semaphore("pj_" + name))
        two = lambda name, shape: [sb(f"{name}{i}", shape, F32) for i in range(2)]
        sums = sb("sums", [P, nd], F32)
        num, rec, y, xn, xT = two("num", [P, T]), two("rec", [P, T]), two("y", [P, T]), two("xn", [P, TT, C]), two("xT", [P, T])
        wp = sb("wp", [P, C], F32)
        rws = sb("rws", [P, E], F32)
        rbs = sb("rbs", [P, TT, E], F32)
        mhalf = sb("mhalf", [P, TT], F32)
        rstd = sb("rstd", [P, TT], F32)
        nrm = Norm(sb)
        lg = sb("lg", [P, nt, E], F32)
        ex = sb("ex", [P, nt, E], F32)
        top = sb("top", [P, nt], F32)
        tot = sb("tot", [P, nt], F32)
        psP = [ctx.enter_context(nc.psum_tensor(f"pj_psP{i}", [P, T], F32)) for i in range(2)]
        psX = [ctx.enter_context(nc.psum_tensor(f"pj_psX{i}", [P, T], F32)) for i in range(2)]
        psL = [ctx.enter_context(nc.psum_tensor(f"pj_psL{i}", [P, TT, E], F32)) for i in range(2)]
        s_w, s_sum, s_inv, s_rw, s_y, s_pr, s_x1, s_chain, s_rs, s_x1st, s_set, s_xn, s_tr, s_xT, s_lr, s_lg, s_c, s_ex, s_sc = (
            sem(n) for n in (
                "weights", "sums_loaded", "inverted", "rec_written", "y_ready", "proj_ready", "x1_ready", "chain", "rstd",
                "x1_stored", "mhalf_set", "xn_ready", "turned", "xT_ready", "logits_ready", "logits_kept", "softmax",
                "exp_ready", "sc_stored"))
        s_ld = [sem(f"loaded{n}") for n in range(2)]
        s_st = [sem(f"xn_stored{n}") for n in range(2)]
        block = ctx.enter_context(nc.Block())
        some = lambda s, lo=0, hi=nb: not isinstance(s, int) or lo <= s < hi

        @block.sync
        def _(sp):
            per = H * T // nd
            for b in range(nb):
                sp.dma_start(sums[per * b:per * b + per], y_scr[b, D].rearrange("h q -> (h q)").rearrange("(p q) -> p q", q=nd))\
                    .then_inc(s_sum, 16)
            for dst, src in ((wp[:], w_projT), (rws[:], rw)):
                sp.dma_start(dst, src).then_inc(s_w, 16)
            for t in range(TT):
                sp.dma_start(rbs[:, t], rb.partition_broadcast(P)).then_inc(s_w, 16)
            sp.wait_ge(s_inv, 1)
            sp.dma_start(rec_scr.rearrange("b h q -> (b h q)").rearrange("(p q) -> p q", q=nd), sums[:]).then_inc(s_rw, 16)
            sp.wait_ge(s_rw, 16)

            def load(n, b):
                one = bass.ds(b, 1)
                sp.dma_start(num[n][:], y_scr[one, 0:D].rearrange("b r h q -> (b r h) q")).then_inc(s_ld[n], 16)
                src = rec_scr[one].rearrange("b h q -> b (h q)")
                sp.dma_start(rec[n][:], src.rearrange("b (h q) -> b h q", h=H).to_broadcast([D, H, T])).then_inc(s_ld[n], 16)

            def step(n, s):
                if some(s):
                    if some(s, 2):
                        sp.wait_ge(s_y, s - 1)
                    load(n, s)
                if some(s - 2):
                    sp.wait_ge(s_xn, s - 1)
                    sp.dma_start(tab[:, bass.ds(TT * (s - 2), TT), :], xn[n][:]).then_inc(s_st[n], 16)
            lead_pairs(nb + 2, sp, step, 4)
            for n in range(2):
                sp.wait_ge(s_st[n], 8 * nb)
            sp.wait_ge(s_c, 5)
            sp.dma_start(sctab, sc[:]).then_inc(s_sc, 16)
            sp.wait_ge(s_sc, 16)

        @block.gpsimd
        def _(pool):
            pool.memset(mhalf[:], -0.5).then_inc(s_set, 1)
            pool.wait_ge(s_set, 1)

            def step(n, s):
                if some(s):
                    pool.wait_ge(s_ld[n], 16 * (s - n) + 32)
                    if some(s, 2):
                        pool.wait_ge(s_pr, s - 1)
                    pool.tensor_tensor(y[n][:], num[n][:], rec[n][:], ALU.mult).then_inc(s_y, 1)
                if some(s - 1):
                    pool.wait_ge(s_chain, Norm.OPS * s)
                    if some(s - 1, 1):
                        pool.wait_ge(s_xn, s - 1)
                    pool.tensor_tensor(rstd[:], nrm.veps[:], mhalf[:], ALU.pow).then_inc(s_rs, 1)
            lead_pairs(nb + 2, pool, step, 4)

        @block.tensor
        def _(pe):
            pe.wait_ge(s_w, 16 * 6)

            def step(n, s):
                m = 1 - n
                if some(s):
                    pe.wait_ge(s_y, s + 1)
                    if some(s, 2):
                        pe.wait_ge(s_x1, s - 1)
                    for t in range(TT):
                        i = pe.matmul(psP[n][:, P * t:P * t + P], y[n][:, P * t:P * t + P], wp[:], start=True, stop=True)
                    i.then_inc(s_pr, 1)
                if some(s - 3):
                    pe.wait_ge(s_xT, s - 2)
                    if some(s - 3, 2):
                        pe.wait_ge(s_lg, s - 4)
                    for t in range(TT):
                        i = pe.matmul(psL[m][:, t], xT[m][:, P * t:P * t + P], rws[:], start=True, stop=True)
                    i.then_inc(s_lr, 1)
                if some(s - 2):
                    pe.wait_ge(s_xn, s - 1)
                    for t in range(TT):
                        i = pe.transpose(psX[n][:, P * t:P * t + P], xn[n][:, t], ident[:])
                    i.then_inc(s_tr, 1)
            lead_pairs(nb + 4, pe, step, 6, 4)

        @block.vector
        def _(dve):
            dve.wait_ge(s_sum, 16 * nb)
            dve.reciprocal(sums[:], sums[:]).then_inc(s_inv, 1)
            dve.wait_ge(s_w, 16 * 6)

            def step(n, s):
                m = 1 - n
                if some(s):
                    dve.wait_ge(s_pr, s + 1)
                    xb = x_all[:, bass.ds(TT * s, TT), :].rearrange("p t c -> p (t c)")
                    dve.tensor_tensor(xb, psP[n][:], xb, ALU.add).then_inc(s_x1, 1)
                if some(s - 1):
                    dve.wait_ge(s_rs, s)
                    if some(s - 1, 2):
                        dve.wait_ge(s_st[m], 8 * (s - 1 - m))
                        dve.wait_ge(s_tr, s - 2)
                    for t in range(TT):
                        i = dve.tensor_scalar(xn[m][:, t], x_all[:, bass.ds(TT * (s - 1) + t, 1), :].rearrange("p a c -> p (a c)"),
                                              nrm.mean[:, t:t + 1], rstd[:, t:t + 1], ALU.subtract, ALU.mult)
                    i.then_inc(s_xn, 1)
                if some(s):
                    dve.wait_ge(s_x1, s + 1)
                    if some(s, 1):
                        dve.wait_ge(s_xn, s)
                    nrm.run(dve, lambda t: x_all[:, bass.ds(TT * s + t, 1), :].rearrange("p a c -> p (a c)"), s_chain, s)
                if some(s - 3):
                    dve.wait_ge(s_lr, s - 2)
                    dve.tensor_tensor(lg[:, bass.ds(TT * (s - 3), TT), :], psL[m][:], rbs[:], ALU.add).then_inc(s_lg, 1)
            lead_pairs(nb + 4, dve, step, 6, 4)
            dve.wait_ge(s_lg, nb)
            dve.tensor_reduce(top[:], lg[:], AX, ALU.max).then_inc(s_c, 1)
            dve.wait_ge(s_c, 1)
            dve.tensor_tensor(lg[:], lg[:], top[:].unsqueeze(2).to_broadcast([P, nt, E]), ALU.subtract).then_inc(s_c, 1)
            dve.wait_ge(s_ex, 1)
            dve.tensor_reduce(tot[:], ex[:], AX, ALU.add).then_inc(s_c, 1)
            dve.wait_ge(s_c, 3)
            dve.reciprocal(tot[:], tot[:]).then_inc(s_c, 1)
            dve.wait_ge(s_c, 4)
            dve.tensor_tensor(sc[:], ex[:], tot[:].unsqueeze(2).to_broadcast([P, nt, E]), ALU.mult).then_inc(s_c, 1)

        @block.scalar
        def _(act):
            def step(n, s):
                if some(s):
                    act.wait_ge(s_x1, s + 1)
                    act.dma_start(xbuf[:, bass.ds(TT * s, TT), :], x_all[:, bass.ds(TT * s, TT), :]).then_inc(s_x1st, 16)
                if some(s - 2):
                    act.wait_ge(s_tr, s - 1)
                    if some(s - 2, 2):
                        act.wait_ge(s_lr, s - 3)
                    act.activation(xT[n][:], psX[n][:], ACT.Copy).then_inc(s_xT, 1)
            lead_pairs(nb + 2, act, step, 4)
            act.wait_ge(s_c, 2)
            act.activation(ex[:], lg[:], ACT.Exp).then_inc(s_ex, 1)
            act.wait_ge(s_x1st, 16 * nb)


def choose(nc, sc, ident, cst, idx, nb):
    nt = nb * TT
    nj = nt * E // P
    BITS = 30
    with ExitStack() as ctx:
        sb = lambda name, shape, dt: ctx.enter_context(nc.sbuf_tensor("ch_" + name, shape, dt))
        sem = lambda name: ctx.enter_context(nc.semaphore("ch_" + name))
        scT = sb("scT", [P, nj * P], F32)
        junk = sb("junk", [P, nj * P], BF16)
        junk2 = sb("junk2", [P, 2 * E, P], BF16)
        cnt = sb("cnt", [P, 1], F16)
        bitx = sb("bitx", [P, 1], I32)
        cand = sb("cand", [P, 1], I32)
        thrb = sb("thrb", [P, P], F32)
        thr = sb("thr", [P, E], F32)
        same = sb("same", [P, P], F16)
        tri = sb("tri", [P, P], BF16)
        ones = sb("ones", [P, P], BF16)
        strict = sb("strict", [nt, nt], BF16)
        pwf = sb("pwf", [P, BITS], F32)
        pwi = sb("pwi", [P, BITS], I32)
        iota = sb("iota", [nt, KTOP], F32)
        tileno = sb("tileno", [nt, E], BF16)
        slotno = sb("slotno", [P, 2 * E], F32)
        gt = sb("gt", [P, nt, E], BF16)
        eq = sb("eq", [P, nt, E], BF16)
        sel = sb("sel", [P, nt, E], BF16)
        cgt = sb("cgt", [P, E], F32)
        tots = sb("tots", [P, E, nt], F32)
        incl = sb("incl", [P, E, nt], F32)
        onesf = sb("onesf", [P, nt], F32)
        pe_ = sb("peq", [P, nt, E], F32)
        pin = sb("pin", [nt, E, P], BF16)
        pex2 = sb("pex2", [nt, E, 2], BF16)
        pex = sb("pex", [nt, E], F32)
        pinc = sb("pinc", [nt, E], F32)
        ge = sb("ge", [nt, E, KTOP], BF16)
        oh = sb("oh", [nt, E, KTOP], BF16)
        rr = sb("rr", [P, 2 * E], F32)
        cn = sb("cn", [P, 2 * E], F32)
        til = sb("til", [P, 2 * E], F32)
        psA = ctx.enter_context(nc.psum_tensor("ch_psA", [P, 512], F32))
        psB = ctx.enter_context(nc.psum_tensor("ch_psB", [P, 512], F32))
        psC = ctx.enter_context(nc.psum_tensor("ch_psC", [P, 512], F32))
        psL = ctx.enter_context(nc.psum_tensor("ch_psL", [P, 4, 512], F32))
        psR = ctx.enter_context(nc.psum_tensor("ch_psR", [P, 512], F32))
        s_cst, s_tr, s_cp, s_cnt, s_tot, s_thr, s_thrT, s_masks, s_pre, s_sel, s_pin, s_pinc, s_off, s_oh, s_look, s_c = (
            sem(n) for n in ("consts", "turned", "scT_ready", "counted", "total", "thr_ready", "thr_turned", "masks",
                             "prefixes", "selected", "pin_ready", "pin_copied", "offsets", "onehots", "looked", "chain"))
        block = ctx.enter_context(nc.Block())

        @block.sync
        def _(sp):
            for dst, name in ((same, "c_same"), (tri, "c_tri"), (ones, "c_ones"), (strict, "c_strict"), (pwf, "c_pwf"),
                              (pwi, "c_pwi"), (iota, "c_iota"), (tileno, "c_tileno"), (slotno, "c_slotno")):
                sp.dma_start(dst[:], cst[name][0:dst.shape[0], 0:dst.shape[1]]).then_inc(s_cst, 16)

        @block.tensor
        def _(pe):
            for j in range(nj):
                i = pe.transpose(psA[:, P * j:P * j + P], sc[:, 16 * j:16 * j + 16, :].rearrange("p t e -> p (t e)"), ident[:])
            i.then_inc(s_tr, 1)
            pe.wait_ge(s_cst, 16 * 9)
            with pe.Fori(0, BITS) as k:
                pe.wait_ge(s_cnt, k + 1)
                pe.matmul(psR[:, 0:1], same[:], cnt[:], start=True, stop=True).then_inc(s_tot, 1)
            pe.wait_ge(s_thr, 1)
            pe.transpose(psA[:, 0:P], thrb[:], ident[:]).then_inc(s_thrT, 1)
            pe.wait_ge(s_masks, 1)
            nn = nt * E
            pe.matmul(psA[:, 0:nn], ones[:], gt[:].rearrange("p t e -> p (t e)"), start=True, stop=True)
            pe.matmul(psB[:, 0:nn], tri[:], eq[:].rearrange("p t e -> p (t e)"), start=True, stop=True)
            pe.matmul(psC[:, 0:nn], ones[:], eq[:].rearrange("p t e -> p (t e)"), start=True, stop=True).then_inc(s_pre, 1)
            pe.wait_ge(s_sel, 1)
            for e in range(E):
                i = pe.matmul(psL[0:nt, e // 4, P * (e % 4):P * (e % 4) + P], sel[:, :, e], tri[:], start=True, stop=True)
            i.then_inc(s_pin, 1)
            pe.wait_ge(s_pinc, 1)
            pe.matmul(psR[0:nt, 0:E], strict[:], pin[:, :, P - 1], start=True, stop=True).then_inc(s_off, 1)
            pe.wait_ge(s_oh, 1)
            for k in range(2 * E):
                e, h = k // 2, k % 2
                ohk = oh[:, e, P * h:P * h + P]
                pe.matmul(psL[:, k // 4, P * (k % 4):P * (k % 4) + P], ohk, pin[:, e, :], start=True, stop=True)
                i = pe.matmul(psR[:, 2 * k:2 * k + 2], ohk, pex2[:, e, :], start=True, stop=True)
            i.then_inc(s_look, 1)

        @block.vector
        def _(dve):
            chain = [0]

            def link(ins):
                chain[0] += 1
                ins.then_inc(s_c, 1)
                dve.wait_ge(s_c, chain[0])

            dve.memset(cand[:], 1 << (BITS - 1))
            link(dve.memset(onesf[:], 1.0))
            dve.wait_ge(s_tr, 1)
            dve.tensor_copy(scT[:], psA[:, 0:nj * P]).then_inc(s_cp, 1)
            dve.wait_ge(s_cst, 16 * 9)
            dve.wait_ge(s_cp, 1)
            with dve.Fori(0, BITS) as k:
                dve.tensor_scalar(junk[:], scT[:], cand[:].bitcast(F32), 0.0, ALU.is_ge, ALU.add, accum_out=cnt[:]).then_inc(s_cnt, 1)
                dve.wait_ge(s_tot, k + 1)
                dve.tensor_scalar(bitx[:], psR[:, 0:1], KTOP - 0.5, pwf[:, bass.ds(k, 1)], ALU.is_lt, ALU.mult).then_inc(s_cp, 1)
                dve.wait_ge(s_cp, 2 * k + 2)
                dve.scalar_tensor_tensor(out=cand[:], in0=bitx[:], scalar=pwi[:, bass.ds(k, 1)], in1=cand[:],
                                         op0=ALU.bitwise_xor, op1=ALU.bitwise_xor).then_inc(s_cp, 1)
                dve.wait_ge(s_cp, 2 * k + 3)
            dve.tensor_copy(thrb[:], cand[:].bitcast(F32).to_broadcast([P, P])).then_inc(s_thr, 1)
            dve.wait_ge(s_thrT, 1)
            link(dve.tensor_copy(thr[:], psA[:, 0:E]))
            tb = thr[:].unsqueeze(1).to_broadcast([P, nt, E])
            dve.tensor_tensor(gt[:], sc[:], tb, ALU.is_gt)
            dve.tensor_tensor(eq[:], sc[:], tb, ALU.is_equal).then_inc(s_masks, 1)
            dve.wait_ge(s_pre, 1)
            nn = nt * E
            dve.tensor_reduce(cgt[:], psA[:, 0:nn].rearrange("p (t e) -> p e t", e=E), AX, ALU.add)
            link(dve.tensor_copy(tots[:], psC[:, 0:nn].rearrange("p (t e) -> p e t", e=E)))
            for e in range(E):
                i = dve.tensor_tensor_scan(incl[:, e], onesf[:], tots[:, e], 0.0, ALU.mult, ALU.add)
            link(i)
            link(dve.tensor_tensor(incl[:], incl[:], tots[:], ALU.subtract))
            link(dve.tensor_tensor(pe_[:], psB[:, 0:nn].rearrange("p (t e) -> p t e", e=E), incl[:].rearrange("p e t -> p t e"), ALU.add))
            link(dve.tensor_tensor(pe_[:], pe_[:], cgt[:].unsqueeze(1).to_broadcast([P, nt, E]), ALU.add))
            link(dve.scalar_tensor_tensor(out=pe_[:], in0=pe_[:], scalar=KTOP + 0.5, in1=eq[:], op0=ALU.is_lt, op1=ALU.mult))
            dve.tensor_tensor(sel[:], pe_[:], gt[:], ALU.add).then_inc(s_sel, 1)
            dve.wait_ge(s_pin, 1)
            dve.tensor_copy(pin[:], psL[0:nt, 0:2].rearrange("p a (e k) -> p (a e) k", e=4)).then_inc(s_pinc, 1)
            dve.wait_ge(s_off, 1)
            dve.tensor_copy(pex2[:, :, 0], psR[0:nt, 0:E])
            dve.tensor_copy(pex2[:, :, 1], tileno[:])
            dve.wait_ge(s_pinc, 1)
            dve.tensor_tensor(pinc[:], psR[0:nt, 0:E], pin[:, :, P - 1], ALU.add)
            link(dve.tensor_copy(pex[:], psR[0:nt, 0:E]))
            for e in range(E):
                i = dve.tensor_scalar(ge[:, e], iota[:], pex[:, e:e + 1], None, ALU.is_ge)
            link(i)
            for e in range(E):
                i = dve.scalar_tensor_tensor(out=oh[:, e], in0=iota[:], scalar=pinc[:, e:e + 1], in1=ge[:, e],
                                             op0=ALU.is_lt, op1=ALU.mult)
            i.then_inc(s_oh, 1)
            dve.wait_ge(s_look, 1)
            pr = psR[:, 0:4 * E].rearrange("p (k a) -> p k a", a=2)
            dve.tensor_copy(til[:], pr[:, :, 1])
            link(dve.tensor_tensor(rr[:], slotno[:], pr[:, :, 0], ALU.subtract))
            for k in range(2 * E):
                i = dve.tensor_scalar(junk2[:, k], psL[:, k // 4, P * (k % 4):P * (k % 4) + P], rr[:, k:k + 1], 0.0,
                                      ALU.is_le, ALU.add, accum_out=cn[:, k:k + 1])
            link(i)
            link(dve.scalar_tensor_tensor(out=idx[:], in0=cn[:], scalar=float(nt), in1=til[:], op0=ALU.mult, op1=ALU.add))


def expert_choice(nc, idx, tab, sctab, w1, b1, w2, b2, xbuf, ident, nb):
    nt = nb * TT
    FT = 4
    with ExitStack() as ctx:
        sb = lambda name, shape, dt: ctx.enter_context(nc.sbuf_tensor("ec_" + name, shape, dt))
        sem = lambda name: ctx.enter_context(nc.semaphore("ec_" + name))
        xg = sb("xg", [P, 2 * E, C], F32)
        gg = sb("gg", [P, 2 * E * E], F32)
        w1s = [sb(f"w1s{i}", [P, FT * P], F32) for i in range(2)]
        w2s = [sb(f"w2s{i}", [P, FT, C], F32) for i in range(2)]
        b1s = sb("b1s", [P, E, FT], F32)
        b2s = sb("b2s", [P, E, C], F32)
        xT = [sb(f"xgT{i}", [P, 2 * P], F32) for i in range(2)]
        hT = [sb(f"hT{i}", [P, FT, 2 * P], F32) for i in range(2)]
        ctr = sb("ctr", [P, 2 * E, C], F32)
        tmp = sb("tmp", [P, 2, C], F32)
        psX = [ctx.enter_context(nc.psum_tensor(f"ec_psX{i}", [P, 2 * P], F32)) for i in range(2)]
        psH = [ctx.enter_context(nc.psum_tensor(f"ec_psH{i}", [P, 2, 512], F32)) for i in range(2)]
        psO = [ctx.enter_context(nc.psum_tensor(f"ec_psO{i}", [P, 2, C], F32)) for i in range(2)]
        s_b, s_tr, s_xT, s_h, s_hT, s_o, s_t, s_ctr, s_sc = (sem(n) for n in (
            "biases", "turned", "xT_ready", "h_ready", "hT_ready", "o_ready", "tmp_ready",
            "contrib", "scattered"))
        s_w = [sem(f"weights{n}") for n in range(2)]
        s_xg = [sem(f"rows_gathered{e}") for e in range(3)]
        s_gg = [sem(f"gates_gathered{e}") for e in range(3)]
        block = ctx.enter_context(nc.Block())
        tabr = tab.rearrange("p t c -> (p t) c")
        sctr = sctab.rearrange("p t e -> (p t) e")
        xr = xbuf.rearrange("p t c -> (p t) c")

        @block.gpsimd
        def _(pool):
            def gather(e):
                offs = [bass.IndirectOffsetOnAxis(ap=idx[:, k:k + 1], axis=0) for k in (2 * e, 2 * e + 1)]
                for k, off in zip((2 * e, 2 * e + 1), offs):
                    pool.indirect_dma_start(xg[:, k, :], None, tabr, off).then_inc(s_xg[e % 3], 16)
                for k, off in zip((2 * e, 2 * e + 1), offs):
                    pool.indirect_dma_start(gg[:, E * k:E * k + E], None, sctr, off).then_inc(s_gg[e % 3], 16)

            gather(0)
            gather(1)
            for e in range(E):
                if e + 2 < E:
                    gather(e + 2)
                pool.wait_ge(s_ctr, e + 1)
                if e:
                    pool.wait_ge(s_sc, 32 * e)
                for k in (2 * e, 2 * e + 1):
                    off = bass.IndirectOffsetOnAxis(ap=idx[:, k:k + 1], axis=0)
                    pool.indirect_dma_start(xr, off, ctr[:, k, :], None, compute_op=ALU.add).then_inc(s_sc, 16)
            pool.wait_ge(s_sc, 32 * E)

        @block.sync
        def _(sp):
            sp.dma_start(b1s[:], b1).then_inc(s_b, 16)
            sp.dma_start(b2s[:], b2.partition_broadcast(P)).then_inc(s_b, 16)

            def load(n, e):
                sp.dma_start(w1s[n][:], w1[bass.ds(e, 1)].rearrange("e c f -> (e c) f")).then_inc(s_w[n], 16)
                sp.dma_start(w2s[n][:], w2[bass.ds(e, 1)].rearrange("e f t c -> (e f) t c")).then_inc(s_w[n], 16)
            load(0, 0)
            load(1, 1)
            with sp.Fori(0, E // 2 - 1) as i:
                for n in range(2):
                    sp.wait_ge(s_o, 2 * i + n + 1)
                    load(n, 2 * i + n + 2)

        @block.tensor
        def _(pe):
            def body(n, e, last):
                pe.wait_ge(s_xg[e % 3], 32 * (e // 3 + 1))
                pe.wait_ge(s_xT, e)
                for h in range(2):
                    i = pe.transpose(psX[n][:, P * h:P * h + P], xg[:, bass.ds(2 * e + h, 1), :].rearrange("p a c -> p (a c)"), ident[:])
                i.then_inc(s_tr, 1)
                pe.wait_ge(s_xT, e + 1)
                pe.wait_ge(s_w[n], 32 * (half(e, n) + 1))
                pe.wait_ge(s_hT, e)
                for f in range(FT):
                    i = pe.matmul(psH[n][:, f // 2, 2 * P * (f % 2):2 * P * (f % 2) + 2 * P], w1s[n][:, P * f:P * f + P], xT[n][:],
                                  start=True, stop=True)
                i.then_inc(s_h, 1)
                pe.wait_ge(s_hT, e + 1)
                pe.wait_ge(s_ctr, e)
                for h in range(2):
                    for f in range(FT):
                        i = pe.matmul(psO[n][:, h], hT[n][:, f, P * h:P * h + P], w2s[n][:, f], start=(f == 0), stop=(f == FT - 1))
                i.then_inc(s_o, 1)
            for e in range(E):
                body(e % 2, e, e == E - 1)

        @block.scalar
        def _(act):
            act.wait_ge(s_b, 32)

            def body(n, e, last):
                act.wait_ge(s_tr, e + 1)
                act.activation(xT[n][:], psX[n][:], ACT.Copy).then_inc(s_xT, 1)
                act.wait_ge(s_h, e + 1)
                for f in range(FT):
                    i = act.activation(hT[n][:, f], psH[n][:, f // 2, 2 * P * (f % 2):2 * P * (f % 2) + 2 * P], ACT.Relu,
                                       bias=b1s[:, bass.ds(e, 1), f:f + 1].rearrange("p a b -> p (a b)"))
                i.then_inc(s_hT, 1)
            for e in range(E):
                body(e % 2, e, e == E - 1)

        @block.vector
        def _(dve):
            dve.wait_ge(s_b, 32)

            def body(n, e, last):
                dve.wait_ge(s_o, e + 1)
                dve.wait_ge(s_ctr, e)
                for h in range(2):
                    i = dve.tensor_tensor(tmp[:, h], psO[n][:, h], b2s[:, bass.ds(e, 1), :].rearrange("p a c -> p (a c)"), ALU.add)
                i.then_inc(s_t, 1)
                dve.wait_ge(s_gg[e % 3], 32 * (e // 3 + 1))
                dve.wait_ge(s_t, e + 1)
                for h in range(2):
                    i = dve.tensor_scalar(ctr[:, bass.ds(2 * e + h, 1), :].rearrange("p a c -> p (a c)"), tmp[:, h],
                                          gg[:, bass.ds((2 * E + 1) * e + E * h, 1)], None, ALU.mult)
                i.then_inc(s_ctr, 1)
            for e in range(E):
                body(e % 2, e, e == E - 1)


def skewed(eng, nb, fn):
    for s in range(4):
        fn(s, s % 2)
    with eng.Fori(1, nb // 2 - 1) as i:
        PAIR[0] = i + 1
        for n in range(2):
            fn(2 * i + n + 2, n)
    for s in (nb, nb + 1):
        fn(s, s % 2)


def live(b, nb):
    return not isinstance(b, int) or 0 <= b < nb


def mixer(nc, x_all, xbuf, ident, win, wout, prm, rows, nb):
    with ExitStack() as ctx:
        sb = lambda name, shape, dt: ctx.enter_context(nc.sbuf_tensor("mx_" + name, shape, dt))
        sem = lambda name: ctx.enter_context(nc.semaphore("mx_" + name))
        two = lambda name, shape, dt=F32: [sb(f"{name}{i}", shape, dt) for i in range(2)]
        win_s = sb("win", [P, 2 * C], F32)
        wout_s = sb("wout", [P, C], F32)
        prm_s = sb("prm", [P, 10], F32)
        col = lambda k: prm_s[:, k:k + 1]
        BU, BV, W0, W1, W2, CB, LA, SB, SC, SD = range(10)
        rows_s = sb("rows", [P, 3, TT, C], F32)
        decay = sb("decay", [P, 1], F32)
        decayb = sb("decayb", [P, T], F32)
        bc = sb("bc", [P, 1], F32)
        mhalf = sb("mhalf", [P, TT], F32)
        carry = sb("carry", [P, 1], F32)
        nrm = Norm(lambda a, b_, c_: sb("i" + a, b_, c_))
        nr2 = Norm(lambda a, b_, c_: sb("o" + a, b_, c_))
        rs1 = sb("rs1", [P, TT], F32)
        rs2 = sb("rs2", [P, TT], F32)
        xn, xT, vs, c0, vl, hs, dv, ys, z, xo, ho, hn, t1, t2 = (two(n, s) for n, s in (
            ("xn", [P, TT, C]), ("xT", [P, T]), ("vs", [P, T + 2]), ("c0", [P, T]), ("vl", [P, T]), ("hs", [P, T]),
            ("dv", [P, T]), ("ys", [P, T]), ("z", [P, T]), ("xo", [P, TT, C]), ("ho", [P, TT, C]), ("hn", [P, TT, C]),
            ("t1", [P, TT, C]), ("t2", [P, TT, C])))
        ps = lambda n: ctx.enter_context(nc.psum_tensor("mx_" + n, [P, T], F32))
        psX = ps("psX")
        psU = [ps("psU0"), ps("psU1")]
        psV = [ps("psV0"), ps("psV1")]
        psO = [ps("psO0"), ps("psO1")]
        s_w, s_ea, s_set, s_n1, s_n2, s_r1, s_r2, s_xn, s_tr, s_xT, s_uv, s_vs, s_c0, s_c, s_dv, s_y, s_ys, s_z, s_o, s_xo, \
            s_h, s_hn, s_t1, s_t2, s_x3, s_pre, s_v = (sem(n) for n in (
                "weights", "exp_a", "set", "stat1", "stat2", "rstd1", "rstd2", "xn_ready", "turned", "xT_ready", "uv_ready",
                "v_ready", "conv0", "conv", "dv_ready", "y_ready", "silu_y", "z_ready", "out_ready", "xo_ready", "h_ready",
                "hn_ready", "t1_ready", "t2_ready", "x3_ready", "prepared", "v_product"))
        s_ld = [sem(f"loaded{n}") for n in range(2)]
        block = ctx.enter_context(nc.Block())

        @block.sync
        def _(sp):
            for dst, src in ((win_s[:], win), (wout_s[:], wout), (prm_s[:], prm)):
                sp.dma_start(dst, src).then_inc(s_w, 16)
            for k in range(3):
                for t in range(TT):
                    sp.dma_start(rows_s[:, k, t], rows[k:k + 1].partition_broadcast(P)).then_inc(s_w, 16)

            def load(n, b):
                sp.dma_start(x_all[:, bass.ds(TT * b, TT), :], xbuf[:, bass.ds(TT * b, TT), :]).then_inc(s_ld[n], 16)
            for n in range(2):
                load(n, n)
            with sp.Fori(0, nb // 2 - 1) as i:
                for n in range(2):
                    sp.wait_ge(s_n1, Norm.OPS * (2 * i + n + 1))
                    load(n, 2 * i + n + 2)

        @block.gpsimd
        def _(pool):
            pool.memset(mhalf[:], -0.5).then_inc(s_set, 1)
            for n in range(2):
                pool.memset(vs[n][:], 0.0).then_inc(s_set, 1)
            pool.wait_ge(s_set, 3)
            pool.wait_ge(s_w, 16 * 15)

            def step(s, n):
                m = 1 - n
                if live(s, nb):
                    pool.wait_ge(s_n1, Norm.OPS * s + 8)
                    pool.wait_ge(s_xn, s)
                    pool.tensor_tensor(rs1[:], nrm.veps[:], mhalf[:], ALU.pow).then_inc(s_r1, 1)
                if live(s - 2, nb):
                    b = s - 2
                    pool.wait_ge(s_n2, Norm.OPS * b + 8)
                    pool.wait_ge(s_hn, b)
                    pool.tensor_tensor(rs2[:], nr2.veps[:], mhalf[:], ALU.pow).then_inc(s_r2, 1)
                if live(s - 2, nb):
                    b = s - 2
                    pool.wait_ge(s_x3, b)
                    pool.tensor_tensor(t2[n][:], x_all[:, bass.ds(TT * b, TT), :], rows_s[:, 2], ALU.add).then_inc(s_t2, 1)
                    pool.wait_ge(s_hn, b + 1)
                    pool.tensor_tensor(t1[n][:], hn[n][:], rows_s[:, 1], ALU.mult).then_inc(s_t1, 1)
                if live(s, nb):
                    pool.wait_ge(s_xn, s + 1)
                    pool.wait_ge(s_h, s - 1) if not isinstance(s, int) or s >= 2 else None
                    pool.tensor_tensor(xo[n][:], xn[n][:], rows_s[:, 0], ALU.add).then_inc(s_xo, 1)
            skewed(pool, nb, step)

        @block.tensor
        def _(pe):
            pe.wait_ge(s_w, 16 * 15)

            def step(s, n):
                m = 1 - n
                if live(s, nb):
                    pe.wait_ge(s_xn, s + 1)
                    pe.wait_ge(s_xT, s)
                    for t in range(TT):
                        i = pe.transpose(psX[:, P * t:P * t + P], xn[n][:, t], ident[:])
                    i.then_inc(s_tr, 1)
                if live(s - 1, nb):
                    b = s - 1
                    pe.wait_ge(s_z, b + 1)
                    pe.wait_ge(s_h, b - 1) if not isinstance(b, int) or b >= 2 else None
                    for t in range(TT):
                        i = pe.matmul(psO[m][:, P * t:P * t + P], z[m][:, P * t:P * t + P], wout_s[:], start=True, stop=True)
                    i.then_inc(s_o, 1)
                if live(s, nb):
                    pe.wait_ge(s_xT, s + 1)
                    pe.wait_ge(s_vs, s - 1) if not isinstance(s, int) or s >= 2 else None
                    pe.matmul(psV[n][:], win_s[:, C:2 * C], xT[n][:], start=True, stop=True).then_inc(s_v, 1)
                    pe.wait_ge(s_z, s - 1) if not isinstance(s, int) or s >= 2 else None
                    pe.matmul(psU[n][:], win_s[:, 0:C], xT[n][:], start=True, stop=True).then_inc(s_uv, 1)
            skewed(pe, nb, step)

        @block.scalar
        def _(act):
            act.wait_ge(s_w, 16 * 15)
            act.wait_ge(s_set, 3)
            act.activation(decay[:], col(LA), ACT.Exp, scale=-1.0).then_inc(s_ea, 1)

            def step(s, n):
                m = 1 - n
                if live(s - 1, nb):
                    b = s - 1
                    act.wait_ge(s_c, 3 * b + 2)
                    act.activation(dv[m][:], vl[m][:], ACT.Copy, scale=col(SD)).then_inc(s_dv, 1)
                    act.wait_ge(s_y, b + 1)
                    act.wait_ge(s_z, b - 1) if not isinstance(b, int) or b >= 2 else None
                    act.activation(ys[m][:], hs[m][:], ACT.Silu).then_inc(s_ys, 1)
                if live(s, nb):
                    act.wait_ge(s_tr, s + 1)
                    act.wait_ge(s_uv, s - 1) if not isinstance(s, int) or s >= 2 else None
                    act.activation(xT[n][:], psX[:], ACT.Copy).then_inc(s_xT, 1)
                    act.wait_ge(s_v, s + 1)
                    act.wait_ge(s_c, 3 * s - 3) if not isinstance(s, int) or s >= 2 else None
                    act.activation(vs[n][:, 1:T + 1], psV[n][:], ACT.Silu, bias=col(BV)).then_inc(s_vs, 1)
                    act.wait_ge(s_vs, s + 1)
                    act.activation(c0[n][:], vs[n][:, 1:T + 1], ACT.Identity, bias=col(CB), scale=col(W1)).then_inc(s_c0, 1)
            skewed(act, nb, step)

        @block.vector
        def _(dve):
            dve.wait_ge(s_ea, 1)
            dve.tensor_scalar(decay[:], decay[:], 1.0, None, ALU.add).then_inc(s_pre, 1)
            dve.wait_ge(s_pre, 1)
            dve.reciprocal(decay[:], decay[:]).then_inc(s_pre, 1)
            dve.tensor_tensor(bc[:], col(SB), col(SC), ALU.mult).then_inc(s_pre, 1)
            dve.wait_ge(s_pre, 3)
            dve.tensor_copy(decayb[:], decay[:].to_broadcast([P, T])).then_inc(s_pre, 1)
            dve.wait_ge(s_pre, 4)

            def step(s, n):
                m = 1 - n
                if live(s, nb):
                    dve.wait_ge(s_ld[n], 16 * (half(s, n) + 1))
                    dve.wait_ge(s_r1, s)
                    nrm.run(dve, lambda t: x_all[:, bass.ds(TT * s + t, 1), :].rearrange("p a c -> p (a c)"), s_n1, s)
                if live(s - 2, nb):
                    b = s - 2
                    dve.wait_ge(s_o, b + 1)
                    dve.wait_ge(s_xo, b + 1)
                    dve.wait_ge(s_r2, b)
                    dve.tensor_tensor(ho[n][:], psO[n][:].rearrange("p (t c) -> p t c", t=TT), xo[n][:], ALU.add).then_inc(s_h, 1)
                    dve.wait_ge(s_h, b + 1)
                    nr2.run(dve, lambda t: ho[n][:, t], s_n2, b)
                if live(s - 1, nb):
                    b = s - 1
                    dve.wait_ge(s_c0, b + 1)
                    dve.wait_ge(s_c, 3 * b)
                    dve.scalar_tensor_tensor(out=c0[m][:], in0=vs[m][:, 0:T], scalar=col(W0), in1=c0[m][:], op0=ALU.mult, op1=ALU.add)\
                       .then_inc(s_c, 1)
                    dve.wait_ge(s_c, 3 * b + 1)
                    dve.wait_ge(s_dv, b)
                    dve.scalar_tensor_tensor(out=vl[m][:], in0=vs[m][:, 2:T + 2], scalar=col(W2), in1=c0[m][:], op0=ALU.mult, op1=ALU.add)\
                       .then_inc(s_c, 1)
                    dve.wait_ge(s_c, 3 * b + 2)
                    dve.wait_ge(s_ys, b)
                    dve.tensor_tensor_scan(hs[m][:], decayb[:], vl[m][:], 0.0, ALU.mult, ALU.add).then_inc(s_c, 1)
                    dve.wait_ge(s_c, 3 * b + 3)
                    dve.wait_ge(s_dv, b + 1)
                    dve.scalar_tensor_tensor(out=hs[m][:], in0=hs[m][:], scalar=bc[:, 0:1], in1=dv[m][:], op0=ALU.mult, op1=ALU.add)\
                       .then_inc(s_y, 1)
                if live(s - 2, nb):
                    b = s - 2
                    dve.wait_ge(s_r2, b + 1)
                    dve.wait_ge(s_t1, b)
                    for t in range(TT):
                        i = dve.tensor_scalar(hn[n][:, t], ho[n][:, t], nr2.mean[:, t:t + 1], rs2[:, t:t + 1], ALU.subtract, ALU.mult)
                    i.then_inc(s_hn, 1)
                if live(s, nb):
                    dve.wait_ge(s_r1, s + 1)
                    dve.wait_ge(s_tr, s - 1) if not isinstance(s, int) or s >= 2 else None
                    dve.wait_ge(s_xo, s - 1) if not isinstance(s, int) or s >= 2 else None
                    for t in range(TT):
                        i = dve.tensor_scalar(xn[n][:, t], x_all[:, bass.ds(TT * s + t, 1), :].rearrange("p a c -> p (a c)"),
                                              nrm.mean[:, t:t + 1], rs1[:, t:t + 1], ALU.subtract, ALU.mult)
                    i.then_inc(s_xn, 1)
                if live(s - 1, nb):
                    b = s - 1
                    dve.wait_ge(s_uv, b + 1)
                    dve.wait_ge(s_ys, b + 1)
                    dve.wait_ge(s_o, b - 1) if not isinstance(b, int) or b >= 2 else None
                    dve.scalar_tensor_tensor(out=z[m][:], in0=psU[m][:], scalar=col(BU), in1=ys[m][:], op0=ALU.add, op1=ALU.mult)\
                       .then_inc(s_z, 1)
                if live(s - 2, nb):
                    b = s - 2
                    dve.wait_ge(s_t1, b + 1)
                    dve.wait_ge(s_t2, b + 1)
                    dve.tensor_tensor(x_all[:, bass.ds(TT * b, TT), :], t1[n][:], t2[n][:], ALU.add).then_inc(s_x3, 1)
            skewed(dve, nb, step)


def gate(nc, x_all, ident, gate_wT, rms_w, w1t, w2t, c_iotae, w1s, w2s, mask, ytab, out, nb):
    nt = nb * TT
    with ExitStack() as ctx:
        sb = lambda name, shape, dt: ctx.enter_context(nc.sbuf_tensor("gt_" + name, shape, dt))
        sem = lambda name: ctx.enter_context(nc.semaphore("gt_" + name))
        gws = sb("gws", [P, E], F32)
        rmsw = sb("rmsw", [P, 1], F32)
        iotae = sb("iotae", [P, nt, E], F32)
        stats = sb("stats", [P, nt, 6], F32)
        a_, b_, mean, var, veps, rstd, rm, r2, ry, mhalf = (sb(n, [P, nt], F32) for n in (
            "a", "b", "mean", "var", "veps", "rstd", "rm", "r2", "ry", "mhalf"))
        y = [sb(f"y{i}", [P, TT, C], F32) for i in range(2)]
        rows = sb("rows", [P, nt, YP], F32)
        acc_a, acc_b = (sb(n, [P, nt], F32) for n in ("acc_a", "acc_b"))
        yT = [sb(f"yT{i}", [P, T], F32) for i in range(2)]
        zeros = sb("zeros", [P, YP], F32)
        lg = sb("lg", [P, nt, E], F32)
        oh = [sb(f"oh{i}", [P, nt, E], F32) for i in range(2)]
        pen = sb("pen", [P, nt, E], F32)
        top = [sb(f"top{i}", [P, nt], F32) for i in range(2)]
        low, d, ex, wa, wb = (sb(n, [P, nt], F32) for n in ("low", "d", "ex", "wa", "wb"))
        psX = [ctx.enter_context(nc.psum_tensor(f"gt_psX{i}", [P, T], F32)) for i in range(2)]
        psL = [ctx.enter_context(nc.psum_tensor(f"gt_psL{i}", [P, TT, E], F32)) for i in range(2)]
        s_w, s_set, s_c, s_p, s_y, s_tr, s_yT, s_lr, s_lg, s_base, s_kept, s_ex, s_wf, s_out = (sem(n) for n in (
            "weights", "set", "chain", "powers", "y_ready", "turned", "yT_ready", "logits_ready", "logits_kept",
            "base_ready", "rows_kept", "exp_ready", "weights_full", "stored"))
        block = ctx.enter_context(nc.Block())

        @block.sync
        def _(sp):
            for dst, src in ((gws[:], gate_wT), (rmsw[:], rms_w), (iotae[:], c_iotae[:, 0:nt]), (w1s[:], w1t), (w2s[:], w2t)):
                sp.dma_start(dst, src).then_inc(s_w, 16)
            sp.wait_ge(s_set, 2)
            sp.dma_start(ytab[nt * P:], zeros[:]).then_inc(s_out, 16)
            sp.dma_start(out[nt * P:], zeros[:, 0:C]).then_inc(s_out, 16)
            outp = out[0:nt * P].rearrange("(p t) c -> p t c", p=P)
            q = nt // 4
            for k in range(4):
                sp.wait_ge(s_base, k + 1)
                sp.dma_start(outp[:, q * k:q * k + q], x_all[:, q * k:q * k + q]).then_inc(s_out, 16)
            sp.wait_ge(s_wf, 1)
            sp.dma_start(ytab[0:nt * P].rearrange("(p t) c -> p t c", p=P), rows[:]).then_inc(s_out, 16)
            sp.wait_ge(s_out, 16 * 7)

        @block.gpsimd
        def _(pool):
            pool.memset(mhalf[:], -0.5).then_inc(s_set, 1)
            pool.memset(zeros[:], 0.0).then_inc(s_set, 1)
            pool.wait_ge(s_set, 2)
            pool.wait_ge(s_c, 6)
            pool.tensor_tensor(rstd[:], veps[:], mhalf[:], ALU.pow).then_inc(s_p, 1)
            pool.wait_ge(s_c, 9)
            pool.tensor_tensor(r2[:], b_[:], mhalf[:], ALU.pow).then_inc(s_p, 1)

            def keep(n, b):
                pool.wait_ge(s_y, b + 1)
                pool.tensor_tensor(rows[:, bass.ds(TT * b, TT), 0:C], y[n][:], zeros[:, 0:C].unsqueeze(1).to_broadcast([P, TT, C]),
                                   ALU.add).then_inc(s_kept, 1)
            lead_pairs(nb, pool, keep)

        @block.vector
        def _(dve):
            chain = [0]

            def link(ins):
                chain[0] += 1
                ins.then_inc(s_c, 1)
                dve.wait_ge(s_c, chain[0])

            for t in range(nt):
                i = dve.bn_stats(stats[:, t], x_all[:, t])
            link(i)
            me, m2e, mo, m2o = (stats[:, :, k] for k in (1, 2, 4, 5))
            link(dve.tensor_tensor(a_[:], me, mo, ALU.subtract))
            dve.tensor_tensor(b_[:], m2e, m2o, ALU.add)
            link(dve.tensor_tensor(mean[:], me, mo, ALU.add))
            dve.tensor_scalar(mean[:], mean[:], 0.5, None, ALU.mult)
            link(dve.scalar_tensor_tensor(out=a_[:], in0=a_[:], scalar=C / 4.0, in1=a_[:], op0=ALU.mult, op1=ALU.mult))
            link(dve.tensor_tensor(var[:], b_[:], a_[:], ALU.add))
            link(dve.tensor_scalar(veps[:], var[:], 1.0 / C, EPS, ALU.mult, ALU.add))
            dve.wait_ge(s_p, 1)
            dve.tensor_scalar(acc_a[:], rstd[:], 1.0, None, ALU.add)
            link(dve.tensor_tensor(a_[:], var[:], rstd[:], ALU.mult))
            dve.scalar_tensor_tensor(out=acc_b[:], in0=mean[:], scalar=-1.0, in1=rstd[:], op0=ALU.mult, op1=ALU.mult)
            link(dve.tensor_tensor(a_[:], a_[:], rstd[:], ALU.mult))
            link(dve.tensor_scalar(b_[:], a_[:], 1.0 / C, 1e-6, ALU.mult, ALU.add))
            dve.wait_ge(s_w, 16 * 5)
            dve.tensor_scalar(gws[:], gws[:], rmsw[:, 0:1], None, ALU.mult)
            dve.tensor_scalar(w1s[:], w1s[:], rmsw[:, 0:1], None, ALU.mult)
            dve.tensor_scalar(w2s[:], w2s[:], rmsw[:, 0:1], None, ALU.mult).then_inc(s_set, 1)
            dve.wait_ge(s_p, 2)
            link(dve.tensor_tensor(ry[:], rstd[:], r2[:], ALU.mult))
            base = chain[0]

            def make(n, b, used):
                if used is not None:
                    dve.wait_ge(s_tr, used)
                    dve.wait_ge(s_kept, used)
                for t in range(TT):
                    k = TT * b + t
                    i = dve.tensor_scalar(y[n][:, t], x_all[:, bass.ds(k, 1), :].rearrange("p a c -> p (a c)"),
                                          mean[:, bass.ds(k, 1)], ry[:, bass.ds(k, 1)], ALU.subtract, ALU.mult)
                i.then_inc(s_y, 1)

            def keep(n, b):
                dve.wait_ge(s_lr, b + 1)
                dve.tensor_copy(lg[:, bass.ds(TT * b, TT), :], psL[n][:]).then_inc(s_lg, 1)
            def step(n, s):
                if not isinstance(s, int) or s < nb:
                    make(n, s, s - 1 if not isinstance(s, int) or s >= 2 else None)
                if not isinstance(s, int) or s >= 2:
                    keep(n, s - 2)
            lead_pairs(nb + 2, dve, step, 4)
            dve.wait_ge(s_lg, nb)
            for k in range(4):
                for t in range(nt // 4 * k, nt // 4 * (k + 1)):
                    i = dve.tensor_scalar(x_all[:, t], x_all[:, t], acc_a[:, t:t + 1], acc_b[:, t:t + 1], ALU.mult, ALU.add)
                i.then_inc(s_base, 1)
            for k in range(2):
                link(dve.tensor_reduce(top[k][:], lg[:], AX, ALU.max))
                link(dve.tensor_tensor(pen[:], lg[:], top[k][:].unsqueeze(2).to_broadcast([P, nt, E]), ALU.is_equal))
                link(dve.scalar_tensor_tensor(out=pen[:], in0=pen[:], scalar=-100.0, in1=iotae[:], op0=ALU.mult, op1=ALU.add))
                link(dve.tensor_reduce(low[:], pen[:], AX, ALU.min))
                link(dve.tensor_tensor(oh[k][:], pen[:], low[:].unsqueeze(2).to_broadcast([P, nt, E]), ALU.is_equal))
                if k == 0:
                    link(dve.scalar_tensor_tensor(out=lg[:], in0=oh[0][:], scalar=-1e30, in1=lg[:], op0=ALU.mult, op1=ALU.add))
            link(dve.tensor_tensor(d[:], top[1][:], top[0][:], ALU.subtract))
            dve.wait_ge(s_ex, 1)
            link(dve.tensor_scalar(wa[:], ex[:], 1.0, None, ALU.add))
            link(dve.reciprocal(wa[:], wa[:]))
            link(dve.tensor_tensor(wb[:], ex[:], wa[:], ALU.mult))
            bc = lambda a: a[:].unsqueeze(2).to_broadcast([P, nt, E])
            dve.tensor_tensor(mask[:], oh[0][:], oh[1][:], ALU.add)
            link(dve.tensor_tensor(oh[0][:], oh[0][:], bc(wa), ALU.mult))
            link(dve.tensor_tensor(oh[1][:], oh[1][:], bc(wb), ALU.mult))
            dve.wait_ge(s_kept, nb)
            dve.tensor_tensor(rows[:, :, C:YP], oh[0][:], oh[1][:], ALU.add).then_inc(s_wf, 1)

        @block.tensor
        def _(pe):
            pe.wait_ge(s_set, 3)

            def turn(n, b):
                for t in range(TT):
                    k = pe.transpose(psX[n][:, P * t:P * t + P], y[n][:, t], ident[:])
                k.then_inc(s_tr, 1)

            def logits(n, b):
                for t in range(TT):
                    k = pe.matmul(psL[n][:, t], yT[n][:, P * t:P * t + P], gws[:], start=True, stop=True)
                k.then_inc(s_lr, 1)
            def step(n, s):
                if not isinstance(s, int) or s >= 2:
                    pe.wait_ge(s_yT, s - 1)
                    if not isinstance(s, int) or s >= 4:
                        pe.wait_ge(s_lg, s - 3)
                    logits(n, s - 2)
                if not isinstance(s, int) or s < nb:
                    pe.wait_ge(s_y, s + 1)
                    turn(n, s)
            lead_pairs(nb + 2, pe, step, 4)

        @block.scalar
        def _(act):
            def copy(n, b):
                act.wait_ge(s_tr, b + 1)
                if not isinstance(b, int) or b >= 2:
                    act.wait_ge(s_lr, b - 1)
                act.activation(yT[n][:], psX[n][:], ACT.Copy).then_inc(s_yT, 1)
            lead_pairs(nb, act, copy)
            act.wait_ge(s_c, 9 + 1 + 5 + 1 + 5 + 1)
            act.activation(ex[:], d[:], ACT.Exp).then_inc(s_ex, 1)


def dispatch(nc, mask, c_tri, c_ones, c_strict, c_iota, c_tileno, c_slotno, ghl, first, past, slot, emap, nb):
    nt = nb * TT
    ntl = 2 * nt + E
    with ExitStack() as ctx:
        sb = lambda name, shape, dt=F32: ctx.enter_context(nc.sbuf_tensor("di_" + name, shape, dt))
        sem = lambda name: ctx.enter_context(nc.semaphore("di_" + name))
        tri = sb("tri", [P, P], BF16)
        ones = sb("ones", [P, P], BF16)
        strict = sb("strict", [nt, nt], BF16)
        iota = sb("iota", [P, 2 * P])
        tileno = sb("tileno", [nt, E], BF16)
        jcol = sb("jcol", [P, 2 * E])
        pin = sb("pin", [nt, E, P], BF16)
        rank = sb("rank", [nt, E, P])
        pex, pinc = sb("pex", [nt, E]), sb("pinc", [nt, E])
        cnt, tiles, last, start, onesf = (sb(n, [P, E]) for n in ("cnt", "tiles", "last", "start", "onesf"))
        full = sb("full", [P, E, nt])
        cmp = sb("cmp", [P, ntl, E])
        prod = sb("prod", [P, ntl, E])
        ef, rel, o = (sb(n, [P, ntl]) for n in ("ef", "rel", "o"))
        psA = ctx.enter_context(nc.psum_tensor("di_psA", [P, 512], F32))
        psL = ctx.enter_context(nc.psum_tensor("di_psL", [P, 2, 512], F32))
        psO = ctx.enter_context(nc.psum_tensor("di_psO", [P, 512], F32))
        s_cst, s_pre, s_pin, s_off, s_c = (sem(n) for n in ("consts", "prefixes", "pin_ready", "offsets", "chain"))
        block = ctx.enter_context(nc.Block())

        @block.sync
        def _(sp):
            for dst, src in ((tri, c_tri), (ones, c_ones), (strict, c_strict), (iota, c_iota), (tileno, c_tileno), (jcol, c_slotno)):
                sp.dma_start(dst[:], src[0:dst.shape[0], 0:dst.shape[1]]).then_inc(s_cst, 16)

        @block.tensor
        def _(pe):
            pe.wait_ge(s_cst, 96)
            pe.matmul(psA[:, 0:nt * E], ones[:], mask[:].rearrange("p t e -> p (t e)"), start=True, stop=True)
            for e in range(E):
                i = pe.matmul(psL[0:nt, e // 4, P * (e % 4):P * (e % 4) + P], mask[:, :, e], tri[:], start=True, stop=True)
            i.then_inc(s_pre, 1)
            pe.wait_ge(s_pin, 1)
            pe.matmul(psO[0:nt, 0:E], strict[:], pin[:, :, P - 1], start=True, stop=True).then_inc(s_off, 1)

        @block.vector
        def _(dve):
            chain = [0]

            def link(ins):
                chain[0] += 1
                ins.then_inc(s_c, 1)
                dve.wait_ge(s_c, chain[0])

            def sum_e(dst, src):
                return dve.tensor_reduce(dst, src, AX, ALU.add)
            dve.wait_ge(s_cst, 96)
            dve.memset(onesf[:], 1.0)
            dve.wait_ge(s_pre, 1)
            dve.tensor_copy(pin[:], psL[0:nt, 0:2].rearrange("p a (e k) -> p (a e) k", e=4)).then_inc(s_pin, 1)
            link(dve.tensor_reduce(cnt[:], psA[:, 0:nt * E].rearrange("p (t e) -> p e t", e=E), AX, ALU.add))
            link(dve.tensor_scalar(cnt[:], cnt[:], 1.0 / P, None, ALU.mult))
            link(dve.tensor_tensor(full[:], iota[:, 0:nt].unsqueeze(1).to_broadcast([P, E, nt]),
                                   cnt[:].unsqueeze(2).to_broadcast([P, E, nt]), ALU.is_lt))
            link(sum_e(tiles[:], full[:]))
            link(dve.tensor_tensor_scan(last[:], onesf[:], tiles[:], 0.0, ALU.mult, ALU.add))
            dve.tensor_tensor(start[:], last[:], tiles[:], ALU.subtract)
            tno = iota[:, 0:ntl].unsqueeze(2).to_broadcast([P, ntl, E])
            row = lambda a, n=P: a[0:n].unsqueeze(1).to_broadcast([n, ntl, E])
            link(dve.tensor_tensor(cmp[:], row(last), tno, ALU.is_le))
            link(sum_e(ef[:], cmp[:]))
            link(dve.tensor_scalar(ef[:], ef[:], float(E - 1), None, ALU.min))
            dve.tensor_copy(emap[:], ef[:])
            link(dve.tensor_tensor(cmp[:], row(iota[:, 0:E]), ef[:].unsqueeze(2).to_broadcast([P, ntl, E]), ALU.is_equal))
            link(dve.tensor_tensor(prod[:], cmp[:], row(start), ALU.mult))
            link(sum_e(rel[:], prod[:]))
            link(dve.tensor_tensor(rel[:], iota[:, 0:ntl], rel[:], ALU.subtract))
            dve.tensor_scalar(slot[:], rel[:], float(P), jcol[:, 0:1], ALU.mult, ALU.add)
            link(dve.tensor_scalar(o[:], rel[:], float(P), None, ALU.mult))
            dve.wait_ge(s_off, 1)
            dve.tensor_copy(pex[:], psO[0:nt, 0:E])
            dve.wait_ge(s_pin, 1)
            link(dve.tensor_tensor(pinc[:], psO[0:nt, 0:E], pin[:, :, P - 1], ALU.add))
            for dst, src in ((first, pex), (past, pinc)):
                link(dve.tensor_tensor(prod[0:nt], cmp[0:nt], row(src, nt), ALU.mult))
                link(sum_e(dst[:], prod[0:nt]))
                link(dve.tensor_tensor(dst[:], dst[:], o[0:nt], ALU.subtract))
            link(dve.tensor_tensor(rank[:], pin[:], pex[:].unsqueeze(2).to_broadcast([nt, E, P]), ALU.add))
            link(dve.tensor_copy(ghl[:, 0, :, 0:P], rank[:]))
            dve.tensor_tensor(ghl[:, 1, :, 0:P], rank[:], ghl[:, 0, :, 0:P], ALU.subtract)
            dve.tensor_copy(ghl[:, 0, :, P], tileno[:])
            link(dve.memset(ghl[:, 1, :, P], 0.0))


def experts(nc, ident, w1s, w2s, w3, c_iota, c_slotno, ghl, first, past, slot, emap, ytab, out, nb):
    nt = nb * TT
    ntl = 2 * nt + E
    with ExitStack() as ctx:
        sb = lambda name, shape, dt=F32: ctx.enter_context(nc.sbuf_tensor("ex_" + name, shape, dt))
        sem = lambda name: ctx.enter_context(nc.semaphore("ex_" + name))
        w3s = sb("w3s", [P, len(FC), E, C])
        iota = sb("iota", [nt, P])
        jcol = sb("jcol", [P, 2 * E])
        after = [sb(f"after{i}", [nt, P], BF16) for i in range(2)]
        oh = [sb(f"oh{i}", [nt, P], BF16) for i in range(2)]
        junk = sb("junk", [P, P], BF16)
        carried, waited = sb("carried", [P, 1]), [sb(f"waited{i}", [P, 1]) for i in range(4)]
        place = [sb(f"place{i}", [P, 1]) for i in range(2)]
        pad = [sb(f"pad{i}", [P, 1]) for i in range(2)]
        rowf = [sb(f"rowf{i}", [P, 1]) for i in range(2)]
        idx = [sb(f"idx{i}", [P, 1], I32) for i in range(8)]
        xg = [sb(f"xg{i}", [P, YP]) for i in range(4)]
        w = [sb(f"w{i}", [P, 1]) for i in range(2)]
        xT = [sb(f"xT{i}", [P, P]) for i in range(2)]
        up = [sb(f"up{i}", [P, DE]) for i in range(2)]
        h = [sb(f"h{i}", [P, DE]) for i in range(2)]
        hT = [sb(f"hT{i}", [P, len(FC), P]) for i in range(2)]
        y = [sb(f"y{i}", [P, C]) for i in range(2)]
        ps = lambda n: ctx.enter_context(nc.psum_tensor("ex_" + n, [P, 512], F32))
        psI, psX, psH, psY = ps("psI"), ps("psX"), ps("psH"), ps("psY")
        psU = [ps("psU0"), ps("psU1")]
        psG = [ps("psG0"), ps("psG1")]
        s_cst, s_aft, s_oh, s_rk, s_pl, s_id, s_x, s_xT, s_g, s_s, s_w, s_h, s_ht, s_hc, s_y, s_yc, s_g2, s_carry = (sem(n) for n in (
            "consts", "after", "onehot", "ranks", "place", "index", "turned", "xT_ready", "gate_ready", "silu",
            "weight", "h_ready", "h_turned", "hT_ready", "down_ready", "y_ready", "up_ready", "zero_set"))
        s_gt = [sem(f"gathered{n}") for n in range(4)]
        s_sc = sem("scattered")
        block = ctx.enter_context(nc.Block())
        LOOK = 4
        GATH = 3

        def steps(eng, fn, before, after_, unroll=8):
            lo, hi = unroll, ntl - unroll
            for s in range(-before, lo):
                fn(s, s % unroll)
            with eng.Fori(lo // unroll, hi // unroll) as i:
                for n in range(unroll):
                    fn(unroll * i + n, n)
            for s in range(hi, ntl + after_):
                fn(s, s % unroll)

        def has(t):
            return not isinstance(t, int) or 0 <= t < ntl

        def wait(eng, s, value, since=1):
            if not isinstance(value, int) or value >= since:
                eng.wait_ge(s, value)

        @block.sync
        def _(sp):
            for f, n in enumerate(FC):
                sp.dma_start(w3s[0:n, f], w3[P * f:P * f + n]).then_inc(s_cst, 16)
            sp.dma_start(iota[:], c_iota[0:nt, 0:P]).then_inc(s_cst, 16)
            sp.dma_start(jcol[:], c_slotno).then_inc(s_cst, 16)

        @block.vector
        def _(dve):
            dve.wait_ge(s_cst, 80)

            def onehot(t, k):
                n = k % 2
                dve.tensor_scalar(after[n][:], iota[:], first[:, bass.ds(t, 1)], None, ALU.is_ge).then_inc(s_aft, 1)
                wait(dve, s_aft, t + 1)
                dve.scalar_tensor_tensor(out=oh[n][:], in0=iota[:], scalar=past[:, bass.ds(t, 1)], in1=after[n][:],
                                         op0=ALU.is_lt, op1=ALU.mult).then_inc(s_oh, 1)

            def index(t, k):
                n = k % 2
                wait(dve, s_rk, t + 1)
                dve.tensor_scalar(junk[:], psI[:, 0:P], slot[:, bass.ds(t, 1)], 0.0, ALU.is_le, ALU.add, accum_out=place[n][:])\
                    .then_inc(s_pl, 1)
                wait(dve, s_pl, 3 * t + 1)
                dve.scalar_tensor_tensor(out=pad[n][:], in0=place[n][:], scalar=float(P), in1=jcol[:, 0:1], op0=ALU.is_ge, op1=ALU.mult)\
                   .then_inc(s_pl, 1)
                dve.scalar_tensor_tensor(out=rowf[n][:], in0=place[n][:], scalar=float(nt), in1=psI[:, P:P + 1], op0=ALU.mult,
                                         op1=ALU.add).then_inc(s_pl, 1)
                wait(dve, s_pl, 3 * t + 3)
                dve.tensor_tensor(idx[k % 8][:], rowf[n][:], pad[n][:], ALU.add).then_inc(s_id, 1)

            def step(s, k):
                if has(s):
                    n = k % 2
                    wait(dve, s_g, s + 1)
                    wait(dve, s_s, 2 * s + 2)
                    dve.scalar_tensor_tensor(out=h[n][:], in0=psG[n][:, 0:DE], scalar=w[n][:, 0:1], in1=up[n][:], op0=ALU.mult,
                                             op1=ALU.mult).then_inc(s_h, 1)
                if has(s + LOOK):
                    index(s + LOOK, k + LOOK)
                if has(s + LOOK + 1):
                    onehot(s + LOOK + 1, k + LOOK + 1)
                if has(s - 1):
                    m = (k - 1) % 2
                    wait(dve, s_y, s)
                    wait(dve, s_sc, 16 * (s - 2))
                    dve.tensor_copy(y[m][:], psY[:, 0:C]).then_inc(s_yc, 1)
            steps(dve, step, LOOK + 1, 1)

        @block.gpsimd
        def _(pool):
            pool.memset(carried[:], 0.0).then_inc(s_carry, 4)
            pool.wait_ge(s_carry, 4)

            def carry(s, n):
                if not isinstance(s, int):
                    pool.wait_ge(s_carry, 2 * (s - 8) + n // 2 + 1)
                    pool.tensor_tensor(waited[n][:], carried[:], carried[:], ALU.add).then_inc(s_carry, 1)

            def gather(t, k):
                wait(pool, s_id, t + 1)
                carry(t - GATH, k % 2)
                pool.indirect_dma_start(xg[k % 4][:], None, ytab, bass.IndirectOffsetOnAxis(ap=idx[k % 8][:], axis=0))\
                    .then_inc(s_gt[k % 4], 16)

            def step(s, k):
                if has(s + GATH):
                    gather(s + GATH, k + GATH)
                if has(s - 1):
                    wait(pool, s_yc, s)
                    wait(pool, s_sc, 16 * (s - 1))
                    carry(s, 2 + k % 2)
                    pool.indirect_dma_start(out, bass.IndirectOffsetOnAxis(ap=idx[(k - 1) % 8][:], axis=0), y[(k - 1) % 2][:],
                                            None, compute_op=ALU.add).then_inc(s_sc, 16)
            steps(pool, step, GATH, 1)
            pool.wait_ge(s_sc, 16 * ntl)

        @block.tensor
        def _(pe):
            pe.wait_ge(s_cst, 80)

            regs = [pe.alloc_register(f"expert{k}") for k in range(8)]

            def number(k):
                return bass.ds(pe.snap(regs[k % 8], min_val=0, max_val=E - 1), 1)

            def flat(a):
                return a.rearrange("p a c -> p (a c)")

            def turn(t, k):
                n = k % 4
                wait(pe, s_gt[n], 4 * (t - n) + 16)
                pe.transpose(psX[:, 0:P], xg[n][:, 0:C], ident[:]).then_inc(s_x, 1)

            def step(s, k):
                if has(s - 1):
                    m = (k - 1) % 2
                    wait(pe, s_h, s)
                    for f, wd in enumerate(FC):
                        i = pe.transpose(psH[0:wd, P * f:P * f + P], h[m][:, P * f:P * f + wd], ident[:])
                    i.then_inc(s_ht, 1)
                if has(s):
                    n = k % 2
                    e = number(k)
                    wait(pe, s_xT, s + 1)
                    pe.matmul(psU[n][:, 0:DE], xT[n][:], flat(w1s[:, e, :]), start=True, stop=True).then_inc(s_g2, 1)
                    pe.matmul(psG[n][:, 0:DE], xT[n][:], flat(w2s[:, e, :]), start=True, stop=True).then_inc(s_g, 1)
                if has(s + LOOK):
                    t = s + LOOK
                    pe.reg_load(regs[(k + LOOK) % 8], emap[0:1, bass.ds(t, 1)])
                    e = number(k + LOOK)
                    wait(pe, s_oh, t + 1)
                    for a in range(2):
                        i = pe.matmul(psI[:, 0:P + 1], oh[(k + LOOK) % 2][:], flat(ghl[:, a, e, :]), start=(a == 0), stop=(a == 1))
                    i.then_inc(s_rk, 1)
                if has(s + 1):
                    turn(s + 1, k + 1)
                if has(s - 1):
                    m = (k - 1) % 2
                    e = number(k - 1)
                    wait(pe, s_hc, s)
                    wait(pe, s_yc, s - 1)
                    for f, wd in enumerate(FC):
                        i = pe.matmul(psY[:, 0:C], hT[m][0:wd, f], flat(w3s[0:wd, f, e, :]), start=(f == 0), stop=(f == len(FC) - 1))
                    i.then_inc(s_y, 1)
            steps(pe, step, LOOK, 1)

        @block.scalar
        def _(act):
            def step(s, k):
                if has(s - 1):
                    m = (k - 1) % 2
                    wait(act, s_ht, s)
                    act.activation(hT[m][:, 0:2].rearrange("p a c -> p (a c)"), psH[:, 0:2 * P], ACT.Copy)
                    act.activation(hT[m][0:FC[2], 2], psH[0:FC[2], 2 * P:3 * P], ACT.Copy).then_inc(s_hc, 1)
                if has(s):
                    n = k % 2
                    wait(act, s_g2, s + 1)
                    act.activation(up[n][:], psU[n][:, 0:DE], ACT.Silu).then_inc(s_s, 1)
                    e = bass.ds(act.value_load(emap[0:1, bass.ds(s, 1)], min_val=0, max_val=E - 1) + C, 1)
                    act.activation(w[n][:], xg[k % 4][:, e], ACT.Copy).then_inc(s_s, 1)
                if has(s + 1):
                    m = (k + 1) % 2
                    wait(act, s_x, s + 2)
                    act.activation(xT[m][:], psX[:, 0:P], ACT.Copy).then_inc(s_xT, 1)
            steps(act, step, 1, 1)


def two_blocks_kernel(nc, x, wattnT, wprojT, rw, rb, w1, b1, w2, b2, win, wout, prm, rows, gwT, rmsw, W1T, W2T, W3T, cst, out):
    nb = NB
    nt = nb * TT

    def dram(name, shape, dt=F32):
        return nc.dram_tensor(name, shape, dt).ap()

    qkv_scr = dram("qkv_scr", [2, 2, 3, P, T], BF16)
    max_scr = dram("max_scr", [G, 2 * HG, T], BF16)
    y_scr = dram("y_scr", [nb, 2 * D, H, T])
    rec_scr = dram("rec_scr", [nb, H, T])
    x_scr = dram("x_scr", [P, nt, C])
    norm_tab = dram("norm_tab", [P, nt, C])
    score_tab = dram("score_tab", [P, nt, E])
    expert_tab = dram("expert_tab", [nt * P + P, YP])
    with ExitStack() as keep:
        def sb(ctx, name, shape, dt=F32):
            return ctx.enter_context(nc.sbuf_tensor(name, shape, dt))

        x_all = sb(keep, "x_all", [P, nt, C])
        ident = sb(keep, "ident", [P, P])
        with ExitStack() as ctx:
            scores = sb(ctx, "sc", [P, nt, E])
            idx = sb(ctx, "idx", [P, 2 * E], I32)
            attention(nc, x_all, ident, x, wattnT, qkv_scr, max_scr, y_scr, cst["c_ident"], cst["c_identb"],
                      cst["c_maskq"], cst["c_maskk"], cst["c_rows"], nb)
            project(nc, x_all, y_scr, rec_scr, wprojT, x_scr, rw, rb, norm_tab, score_tab, scores, ident, nb)
            choose(nc, scores, ident, cst, idx, nb)
            expert_choice(nc, idx, norm_tab, score_tab, w1, b1, w2, b2, x_scr, ident, nb)
            mixer(nc, x_all, x_scr, ident, win, wout, prm, rows, nb)
        with ExitStack() as ctx:
            w1s = sb(ctx, "w1s", [P, E, DE])
            w2s = sb(ctx, "w2s", [P, E, DE])
            mask = sb(ctx, "mask", [P, nt, E], BF16)
            ghl = sb(ctx, "ghl", [nt, 2, E, P + 1], BF16)
            first = sb(ctx, "first", [nt, 2 * nt + E])
            past = sb(ctx, "past", [nt, 2 * nt + E])
            slot = sb(ctx, "slot", [P, 2 * nt + E])
            emap = sb(ctx, "emap", [P, 2 * nt + E], I32)
            gate(nc, x_all, ident, gwT, rmsw, W1T, W2T, cst["c_iotae"], w1s, w2s, mask, expert_tab, out, nb)
            dispatch(nc, mask, cst["c_tri"], cst["c_ones"], cst["c_strict"], cst["c_iota"], cst["c_tileno"],
                     cst["c_slotno"], ghl, first, past, slot, emap, nb)
            experts(nc, ident, w1s, w2s, W3T, cst["c_iota"], cst["c_slotno"], ghl, first, past, slot, emap, expert_tab,
                    out, nb)


def constants(nt, bf16):
    i = np.arange(P)
    wide = lambda a, shape, dt: np.ascontiguousarray(np.broadcast_to(a, shape)).astype(dt)
    below = np.where(i[None, :] > i[:, None], np.float32(-1e30), np.float32(0))
    start = 2.0 ** (-2.0 ** (-(np.log2(H) - 3)))
    slopes = np.array([start * start ** k for k in range(H)], dtype=np.float32).astype(np.float64)
    rows, rest = [], slopes[:, None] * (np.arange(T) - T / 2)
    for _ in range(3):
        part = rest.astype(np.float32).astype(bf16)
        rows.append(part)
        rest = rest - part.astype(np.float64)
    rows += [np.ones((H, T), bf16)] * 3 + [-np.ones((H, T), bf16)] * 2
    bits = np.arange(BITS - 1, -1, -1)
    return dict(
        c_ident=np.eye(P, dtype=np.float32), c_identb=np.eye(P, dtype=np.float32).astype(bf16),
        c_maskq=wide(below[:, None], (P, HG, P), bf16), c_maskk=wide(below.T[:, None], (P, HG, P), bf16),
        c_rows=np.stack(rows).reshape(8, H * T),
        c_same=(i[:, None] % E == i[None, :] % E).astype(np.float16),
        c_tri=(i[:, None] <= i[None, :]).astype(bf16), c_ones=np.ones((P, P), bf16),
        c_strict=(i[:, None] < i[None, :]).astype(bf16),
        c_pwf=wide(2.0 ** bits, (P, BITS), np.float32), c_pwi=wide((2 ** bits) // 2, (P, BITS), np.int32),
        c_iota=wide(np.arange(float(KTOP)), (P, KTOP), np.float32), c_tileno=wide(i[:, None], (P, E), bf16),
        c_slotno=wide(i[:, None] + 128.0 * (np.arange(2 * E) % 2)[None], (P, 2 * E), np.float32),
        c_iotae=wide(np.arange(float(E)), (P, nt, E), np.float32))


def layout(a):
    nt = NB * TT
    order = np.arange(C).reshape(H, D).T.reshape(-1)
    c = {k: np.asarray(v) for k, v in a.items()}
    w_attn = c["L0_attn_W_attn"]
    return dict(
        x=c["L0_attn_x"].reshape(nt, P, C).transpose(1, 0, 2), wattnT=np.concatenate([w_attn[0:C][order], w_attn[C:2 * C][order], w_attn[2 * C:]]).T,
        wprojT=c["L0_attn_W_proj"].T[order], rw=c["L0_ffn_router_w"], rb=c["L0_ffn_router_b"].reshape(1, E),
        w1=c["L0_ffn_w1"], b1=c["L0_ffn_b1"].reshape(E, 4, P).transpose(2, 0, 1),
        w2=c["L0_ffn_w2"].reshape(E, 4, P, C).transpose(0, 2, 1, 3), b2=c["L0_ffn_b2"].reshape(1, E, C),
        win=c["L1_attn_in_proj_w"], wout=c["L1_attn_out_proj_w"],
        prm=np.stack([c["L1_attn_in_proj_b"][:C], c["L1_attn_in_proj_b"][C:], *c["L1_attn_conv_w"][:, 0].T,
                      c["L1_attn_conv_b"], c["L1_attn_logit_a"], c["L1_attn_ssm_b"], c["L1_attn_ssm_c"],
                      c["L1_attn_ssm_d"]], 1),
        rows=np.stack([c["L1_attn_out_proj_b"], c["L1_attn_ln_w"], c["L1_attn_ln_b"]]),
        gwT=c["L1_ffn_gate_w"].T, rmsw=c["L1_ffn_rms_w"].reshape(P, 1), W1T=c["L1_ffn_W1"].transpose(2, 0, 1),
        W2T=c["L1_ffn_W2"].transpose(2, 0, 1), W3T=c["L1_ffn_W3"].transpose(2, 0, 1))


def kernel(**inputs):
    import concourse.bacc as _bacc
    from concourse.bass_utils import run_bass_kernel_spmd as _run

    nt = NB * TT
    nc = _bacc.Bacc("TRN2", target_bir_lowering=False, num_devices=1)
    host = {**layout(inputs), **constants(nt, mybir.dt.np(BF16))}
    arrays, args, cst = {}, {}, {}
    for name, a in host.items():
        a = np.ascontiguousarray(a)
        arrays[name] = a
        ap = nc.dram_tensor(name, a.shape, mybir.dt.from_np(a.dtype), kind="ExternalInput").ap()
        if name[0:2] == "c_":
            cst[name] = ap
        else:
            args[name] = ap
    out = nc.dram_tensor("out", [nt * P + P, C], F32, kind="ExternalOutput").ap()
    two_blocks_kernel(nc, cst=cst, out=out, **args)
    r = _run(nc, [arrays], core_ids=[0])
    return r.results[0]["out"][0:nt * P].reshape(P, nt, C).transpose(1, 0, 2).reshape(NB, T, C)
```

```python
from contextlib import ExitStack

import numpy as np
import concourse.bass as bass
from concourse import mybir

F32 = mybir.dt.float32
BF16 = mybir.dt.bfloat16
F16 = mybir.dt.float16
I32 = mybir.dt.int32
U16 = mybir.dt.uint16
ALU = mybir.AluOpType
ACT = mybir.ActivationFunctionType
AX = mybir.AxisListType.X

P = 128
C = 128
T = 512
NB = 16
TT = T // P
EPS = 1e-5
RMS_EPS = 1e-6

H = 16
D = C // H
G = 4
HG = H // G
TERMS = [(0, 0), (1, 0), (2, 0), (0, 1), (1, 1), (0, 2)]
ROW_ALIBI = 8 * len(TERMS)
ROW_MAX = 96
LATE = 2
W = [T - P * j for j in range(TT)]

E = 8
KTOP = 256
DE = 352
FC = [128, 128, 96]
YP = C + E


def sum_rows(of, parts=8):
    return of.rearrange("b h q -> b (h q)").rearrange("b (p q) -> b p q", p=parts)


def attention(nc, x_all, ident, x_in, w_attnT, qkv_scr, max_scr, y_scr, rec_scr, shared, c_ident, c_identb, c_maskq, c_maskk, c_rows, nb=NB):
    with ExitStack() as ctx:
        def sb(name, shape, dt):
            return ctx.enter_context(nc.sbuf_tensor(name, shape, dt))

        def sem(name):
            return ctx.enter_context(nc.semaphore(name))

        qop = [sb(f"qop{i}", [P, H, T], BF16) for i in range(2)]
        kop = [sb(f"kop{i}", [P, H, T], BF16) for i in range(2)]
        vaug = [sb(f"vaug{i}", [P, TT, H, 32], F32) for i in range(2)]
        probs = [[sb(f"probs{i}_{j}", [P, HG, W[j]], F32) for j in range(TT)] for i in range(2)]
        ysb, sums, s_yw, s_sum, s_inv, s_rw, _ = shared
        identb = sb("identb", [P, P], BF16)
        maskq = sb("maskq", [P, HG, P], BF16)
        maskk = sb("maskk", [P, HG, P], BF16)
        wT = sb("wT", [P, 3, C], F32)
        stats = sb("stats", [P, TT, 6], F32)
        sync6 = sb("sync6", [P, 6], F32)
        mv = sb("mv", [P, TT, 2], F32)
        veps = sb("veps", [P, TT], F32)
        rstd = sb("rstd", [P, TT], F32)
        mhalf = sb("mhalf", [P, TT], F32)
        zeros = sb("zeros", [P, T], F32)
        warm = sb("warm", [P, 1], F32)
        xn = sb("xn", [P, TT, C], F32)
        xT = sb("xT", [P, T], F32)
        parts = [sb(f"parts{n}", [P, 3, T], BF16) for n in range(2)]
        rest = sb("rest", [P, T], F32)
        mx = sb("mx", [P, TT, HG], F32)
        mhl = sb("mhl", [P, TT, 2, HG], BF16)
        mT = sb("mT", [2 * HG, T], BF16)
        psS = [ctx.enter_context(nc.psum_tensor(f"psS{i}", [P, T], F32)) for i in range(2)]
        psE = [ctx.enter_context(nc.psum_tensor(f"psE{i}", [P, 2, T], F32)) for i in range(2)]
        psY = ctx.enter_context(nc.psum_tensor("psY", [P, T], F32))
        psM = ctx.enter_context(nc.psum_tensor("psM", [P, T], F32))
        psMb = psM[:].bitcast(BF16)

        s_first = sem("x_first")
        s_rest = sem("x_rest")
        s_init = [sem(f"init{i}") for i in range(2)]
        s_vzero = sem("vzero")
        s_vinit = sem("vinit")
        s_rows = [sem(f"rows{i}") for i in range(2)]
        s_stat = sem("stat")
        s_rstd = sem("rstd_ready")
        s_xn = sem("xn_ready")
        s_mr = sem("misc_ready")
        s_mf = sem("misc_free")
        s_hi = sem("hi_ready")
        s_mid = sem("mid_ready")
        s_lo = sem("lo_ready")
        s_pw = sem("parts_written")
        s_op = sem("operands")
        s_sr = sem("scores_ready")
        s_su = sem("scores_used")
        s_hl = sem("max_parts")
        s_mw = sem("max_written")
        s_mrow = sem("max_rows")
        s_er = sem("exp_in_ready")
        s_ex = sem("exp_done")
        s_pv = sem("pv_done")
        s_yc = sem("y_copied")

        UN = 11
        EN = 6
        s_units = []
        for j in range(TT):
            n = [4, 2, 1, 1][j]
            s_units += [(j, h, n) for h in range(0, HG, n)]
        e_units = [(0, 0, 2), (0, 2, 2), (1, 0, 2), (1, 2, 2), (2, 0, 4), (3, 0, 4)]
        ORDER = ["E0", "S0", "E1", "S1", "M", "S2", "E2", "E3", "S3", "V0", "S4", "S5", "E4", "S6",
                 "E5", "S7", "V1", "S8", "S9", "V2", "V3", "S10"]
        REST = 16 * (nb // 2 - 1)
        MISC0 = 4
        MISC = 2 * G

        def use_max(b, st, last):
            if isinstance(b, int) and b == nb:
                return MISC0 - 1 + MISC * (nb - 1) + G
            return MISC0 - 1 + MISC * b + (st if last else (0, 3, 5, 7)[st])

        def use_next(b, k):
            return MISC0 - 1 + MISC * b + (1, 2, 4, 6)[k]

        def there(u):
            return not isinstance(u, int) or 0 <= u < G * nb

        def steps(eng, step, tail):
            def body(n, b, last):
                for st in range(G):
                    step(n, b, st, last)
            for b in range(2):
                body(b, b, False)
            with eng.Fori(1, nb // 2 - 1) as i:
                for n in range(2):
                    body(n, 2 * i + n, False)
            for b in (nb - 2, nb - 1):
                body(b % 2, b, b == nb - 1)
            for st in range(tail):
                step(0, nb, st, True)

        block = ctx.enter_context(nc.Block())

        @block.sync
        def _(sp):
            for dst, src in ((x_all[:, 0:2 * TT, :], x_in[:, 0:2 * TT, :]), (ident[:], c_ident), (identb[:], c_identb),
                             (maskq[:], c_maskq), (maskk[:], c_maskk),
                             (wT[:], w_attnT.rearrange("c (s f) -> c s f", s=3))):
                sp.dma_start(dst, src).then_inc(s_first, 16)
            def constant_rows(n):
                sp.wait_ge(s_init[n], 2)
                for dst, a, b in ((kop[n][ROW_ALIBI:ROW_ALIBI + 3], 0, 3), (qop[n][ROW_ALIBI:ROW_ALIBI + 3], 3, 6),
                                  (kop[n][ROW_MAX:ROW_MAX + 2], 6, 8)):
                    sp.dma_start(dst.rearrange("p h q -> p (h q)"), c_rows[a:b]).then_inc(s_rows[n], 16)

            def place(n, b):
                if not (isinstance(b, int) and b < 2):
                    sp.wait_ge(s_op, 16 * 6 * (b - 1))
                for s in range(2):
                    sp.wait_ge(s_lo, 2 * b + s + 1)
                    sp.dma_start(qkv_scr[n, s].rearrange("a p q -> p a q"), parts[s][:]).then_inc(s_pw, 16)
                sp.wait_ge(s_pw, 32 * b + 32)
                row = 0
                for k in (3, 2, 1):
                    w = 8 * k
                    q_src = qkv_scr[n, 0, 0:k].rearrange("a (d h) q -> (a d) (h q)", d=D)
                    sp.dma_start(qop[n][row:row + w].rearrange("p h q -> p (h q)"), q_src).then_inc(s_op, 16)
                    k_src = qkv_scr[n, 1, 3 - k].rearrange("(d h) q -> d (h q)", d=D)
                    sp.dma_start(kop[n][row:row + w].rearrange("p h q -> p (h q)"), k_src.unsqueeze(0).to_broadcast([k, D, H * T]))\
                        .then_inc(s_op, 16)
                    row += w

            constant_rows(0)
            place(0, 0)
            for b in range(1, nb // 2):
                sp.dma_start(x_all[:, 2 * TT * b:2 * TT * b + 2 * TT, :], x_in[:, 2 * TT * b:2 * TT * b + 2 * TT, :]).then_inc(s_rest, 16)
            constant_rows(1)

            def step(n, b, st, last):
                u = G * b + st - 1
                if there(u):
                    m, g = (n, st - 1) if st else (1 - n, G - 1)
                    sp.wait_ge(s_mf, use_max(b, st, last) + 1)
                    if not isinstance(u, int) or u:
                        sp.wait_ge(s_mrow, 16 * u)
                    sp.dma_start(max_scr[g], mT[:]).then_inc(s_mw, 16)
                    sp.wait_ge(s_mw, 16 * (u + 1))
                    sp.dma_start(qop[m][ROW_MAX:ROW_MAX + 2, HG * g:HG * g + HG],
                                 max_scr[g].rearrange("(p h) q -> p h q", p=2)).then_inc(s_mrow, 16)
                if isinstance(b, int) and b == nb and st == 2:
                    sp.wait_ge(s_inv, 1)
                    sp.dma_start(sum_rows(rec_scr[0:nb - LATE]), sums[0][:]).then_inc(s_rw, 16)
                u = G * b + st - 3
                if there(u):
                    bb, g = (b, st - 3) if st == 3 else (b - 1, st + 1)
                    sp.wait_ge(s_yc, u + 2)
                    for h in range(HG):
                        sp.dma_start(y_scr[bass.ds(bb, 1), :, HG * g + h, :].rearrange("b r q -> (b r) q"),
                                     ysb[g % 2][32 * h:32 * h + 2 * D]).then_inc(s_yw[g % 2], 16)
                if isinstance(b, int) and b == nb - 1 and st == 0:
                    for half in s_yw:
                        sp.wait_ge(half, 64 * 2 * (nb - LATE))
                    sp.dma_start(sums[0][:], sum_rows(y_scr[0:nb - LATE, D])).then_inc(s_sum, 16)
                if st == 2 and not last:
                    place(1 - n, b + 1)
            steps(sp, step, 3)
            sp.wait_ge(s_rw, 16)
            sp.wait_ge(s_rest, REST)

        @block.gpsimd
        def _(pool):
            pool.memset(mhalf[:], -0.5).then_inc(s_vinit, 1)
            pool.memset(zeros[:], 0.0).then_inc(s_vinit, 1)
            pool.wait_ge(s_vinit, 2)

            def clear_v(n):
                pool.memset(vaug[n][:], 0.0).then_inc(s_vzero, 1)
                pool.wait_ge(s_vzero, n + 1)
                pool.memset(vaug[n][:, :, :, D:2 * D], 1.0).then_inc(s_vinit, 1)

            def prepare(b, first=False):
                pool.wait_ge(s_xn, b)
                pool.wait_ge(s_stat, 3 * b + 3)
                pool.tensor_tensor(rstd[:], veps[:], mhalf[:], ALU.pow).then_inc(s_rstd, 1)
                if first:
                    clear_v(0)
                for s in range(2):
                    pool.wait_ge(s_mf, s + 2 if first else MISC0 + MISC * (b - 1) + 2 * s + 2)
                    pool.tensor_tensor(parts[s][:, 1], rest[:], zeros[:], ALU.add).then_inc(s_mid, 1)
                    pool.wait_ge(s_mid, 2 * b + s + 1)
                    pool.tensor_tensor(parts[s][:, 2], rest[:], parts[s][:, 1], ALU.subtract).then_inc(s_lo, 1)

            prepare(0, True)
            clear_v(1)
            if nb > 2:
                with pool.Fori(1, nb - 1) as b:
                    prepare(b)
            prepare(nb - 1)

        @block.tensor
        def _(pe):
            pe.wait_ge(s_first, 96)

            def x_transposes(b, use):
                pe.wait_ge(s_xn, b + 1)
                if not (use is None):
                    pe.wait_ge(s_mf, use)
                for t in range(TT):
                    mm = pe.transpose(psM[:, P * t:P * t + P], xn[:, t], ident[:])
                mm.then_inc(s_mr, 1)

            def project(which, use):
                pe.wait_ge(s_mf, use)
                if which < 2:
                    pe.matmul(psM[:], wT[:, which], xT[:], start=True, stop=True).then_inc(s_mr, 1)
                else:
                    for t in range(TT):
                        mm = pe.matmul(psM[:, P * t:P * t + P], xT[:, P * t:P * t + P], wT[:, 2], start=True, stop=True)
                    mm.then_inc(s_mr, 1)

            x_transposes(0, None)
            for s in range(3):
                if s == 0:
                    pe.wait_ge(s_yc, 1)
                project(s, s + 1)

            def step(n, b, st, last):
                    g = st
                    u_exp = G * b + st - 2
                    m, e = (n, st - 2) if st >= 2 else (1 - n, st + 2)
                    if st == 0 and there(G * b):
                        pe.wait_ge(s_op, 16 * 6 * (b + 1))
                        pe.wait_ge(s_rows[n], 48)
                    if there(u_exp):
                        pe.wait_ge(s_mrow, 16 * (u_exp + 1))
                    for what in ORDER:
                        if what == "S6" and st == 0 and not last:
                            x_transposes(b + 1, use_next(b, 0))
                        k = int(what[1:]) if len(what) > 1 else 0
                        if what[0] == "S" and there(G * b):
                            j, h0, nh = s_units[k]
                            w = P * (j + 1)
                            u = UN * g + k
                            bank = psS[u % 2]
                            pe.wait_ge(s_su, UN * G * b + u)
                            out = bank[:, 0:nh * w].rearrange("p (h k) -> p h k", h=nh)
                            pe.matmul(out[:, :, P * j:w], identb[:], maskq[:, 0:nh, :], start=True, stop=False, skip_group_check=True)
                            for h in range(nh):
                                hh = HG * g + h0 + h
                                mm = pe.matmul(out[:, h, :], qop[n][0:96, hh, P * j:P * j + P], kop[n][0:96, hh, 0:w],
                                               start=False, stop=(h == nh - 1), skip_group_check=True)
                            mm.then_inc(s_sr, 1)
                        if what[0] == "E" and there(u_exp):
                            j, h0, nh = e_units[k]
                            u = k
                            bank = psE[u % 2]
                            per = nh // 2 if j < 3 else 4
                            pe.wait_ge(s_ex, EN * u_exp + u)
                            for h in range(0, nh, per):
                                out = bank[:, h // per, 0:per * W[j]].rearrange("p (h q) -> p h q", h=per)
                                pe.matmul(out[:, :, 0:P], identb[:], maskk[:, 0:per, :], start=True, stop=False, skip_group_check=True)
                                for a in range(per):
                                    hh = HG * e + h0 + h + a
                                    mm = pe.matmul(out[:, a, :], kop[m][:, hh, P * j:P * j + P], qop[m][:, hh, P * j:T],
                                                   start=False, stop=(a == per - 1), skip_group_check=True)
                            mm.then_inc(s_er, 1)
                        if what[0] == "V" and there(u_exp):
                            pe.wait_ge(s_ex, 1 + EN * u_exp + [2, 4, 5, 6][k])
                            if k == 0:
                                pe.wait_ge(s_yc, u_exp + 1)
                            for h in range(HG):
                                mm = pe.matmul(psY[32 * h:32 * h + 32, P * k:T], vaug[m][:, k, HG * e + h, :], probs[e % 2][k][:, h, :],
                                               start=(k == 0), stop=(k == TT - 1), skip_group_check=True)
                            if k == TT - 1:
                                mm.then_inc(s_pv, 1)
                        if what[0] == "M" and there(G * b + st - 1):
                            pe.wait_ge(s_hl, 2 * (G * b + st))
                            pe.wait_ge(s_mf, use_max(b, st, last))
                            for t in range(TT):
                                mm = pe.transpose(psMb[0:2 * HG, P * t:P * t + P],
                                                  mhl[:, t].rearrange("p a h -> p (a h)"), identb[:])
                            mm.then_inc(s_mr, 1)
                    if not last and st < 3:
                        project(st, use_next(b, st + 1))
            steps(pe, step, 2)

        @block.vector
        def _(dve):
            def norm_stats(b):
                for t in range(TT):
                    bn = dve.bn_stats(stats[:, t], x_all[:, bass.ds(TT * b + t, 1), :].rearrange("p a c -> p (a c)"))
                bn.then_inc(s_stat, 1)
                dve.wait_ge(s_stat, 3 * b + 1)
                dve.tensor_copy(sync6[:], stats[:, TT - 1])
                for t in range(TT):
                    bn = dve.bn_aggr(mv[:, t], stats[:, t])
                bn.then_inc(s_stat, 1)
                dve.wait_ge(s_stat, 3 * b + 2)
                dve.tensor_scalar(veps[:], mv[:, :, 1], EPS, None, ALU.add).then_inc(s_stat, 1)

            def norm_apply(b, used):
                dve.wait_ge(s_rstd, b + 1)
                dve.wait_ge(s_mr, used)
                for t in range(TT):
                    i = dve.tensor_scalar(xn[:, t], x_all[:, bass.ds(TT * b + t, 1), :].rearrange("p a c -> p (a c)"),
                                          mv[:, t, 0:1], rstd[:, t:t + 1], ALU.subtract, ALU.mult)
                i.then_inc(s_xn, 1)

            dve.memset(qop[0][:].bitcast(F32), 0.0).then_inc(s_init[0], 1)
            dve.memset(kop[0][:].bitcast(F32), 0.0).then_inc(s_init[0], 1)
            dve.wait_ge(s_first, 96)
            norm_stats(0)
            norm_apply(0, 0)
            dve.memset(sync6[:], 0.0).then_inc(s_su, 1)
            dve.tensor_scalar(wT[:, 0], wT[:, 0], D ** -0.5, None, ALU.mult).then_inc(s_yc, 1)

            def split(b, s):
                dve.wait_ge(s_hi, 2 * b + s + 1)
                dve.wait_ge(s_lo, 2 * b + s)
                dve.tensor_tensor(rest[:], psM[:], parts[s][:, 0], ALU.subtract).then_inc(s_mf, 1)

            for s in range(2):
                split(0, s)
            dve.memset(qop[1][:].bitcast(F32), 0.0).then_inc(s_init[1], 1)
            dve.memset(kop[1][:].bitcast(F32), 0.0).then_inc(s_init[1], 1)

            def step(n, b, st, last):
                g = st
                real = there(G * b)
                if st == 0 and not last:
                    if n == 1:
                        dve.wait_ge(s_rest, REST)
                    norm_stats(b + 1)
                if real and there(G * b + g - 1):
                    dve.wait_ge(s_hl, 2 * (G * b + g))
                for k in range(UN):
                    if k == 2:
                        if there(G * b + st - 1):
                            dve.wait_ge(s_mr, use_max(b, st, last) + 1)
                            if there(G * b + st - 2):
                                dve.wait_ge(s_mw, 16 * (G * b + st - 1))
                            dve.tensor_copy(mT[:], psMb[0:2 * HG, 0:T]).then_inc(s_mf, 1)
                        if st == 0 and not last:
                            norm_apply(b + 1, use_max(b, st, last))
                    if real:
                        j, h0, nh = s_units[k]
                        u = UN * g + k
                        w = P * (j + 1)
                        dve.wait_ge(s_sr, UN * G * b + u + 1)
                        dve.tensor_reduce(mx[:, j, h0:h0 + nh], psS[u % 2][:, 0:nh * w].rearrange("p (h k) -> p h k", h=nh),
                                          AX, ALU.max).then_inc(s_su, 1)
                if real:
                    dve.wait_ge(s_su, 1 + UN * G * b + UN * (g + 1))
                    if there(G * b + st - 1):
                        dve.wait_ge(s_mr, use_max(b, st, last) + 1)
                    dve.tensor_copy(mhl[:, :, 0], mx[:]).then_inc(s_hl, 1)
                    dve.wait_ge(s_hl, 2 * (G * b + g) + 1)
                    dve.tensor_tensor(mhl[:, :, 1], mx[:], mhl[:, :, 0], ALU.subtract).then_inc(s_hl, 1)
                if st in (0, 1) and not last:
                    split(b + 1, st)
            steps(dve, step, 1)
            dve.wait_ge(s_sum, 16)
            dve.reciprocal(sums[0][:], sums[0][:]).then_inc(s_inv, 1)

        @block.scalar
        def _(act):
            def copy_x(use):
                act.wait_ge(s_mr, use + 1)
                act.activation(xT[:], psM[:], ACT.Copy).then_inc(s_mf, 1)

            def hi_part(b, s, use):
                act.wait_ge(s_mr, use + 1)
                act.wait_ge(s_pw, 32 * b)
                act.activation(parts[s][:, 0], psM[:], ACT.Copy).then_inc(s_hi, 1)

            def copy_v(n, use):
                act.wait_ge(s_mr, use + 1)
                act.activation(vaug[n][:, :, :, 0:D], psM[:].rearrange("p (t h d) -> p t h d", t=TT, h=H), ACT.Copy)\
                   .then_inc(s_mf, 1)

            copy_x(0)
            for s in range(2):
                hi_part(0, s, s + 1)
            act.wait_ge(s_vinit, 3)
            copy_v(0, 3)
            act.activation(warm[:], ident[:, 0:1], ACT.Exp).then_inc(s_ex, 1)

            def copy_y(u, g):
                act.wait_ge(s_pv, u + 1)
                if there(u - 2):
                    act.wait_ge(s_yw[g % 2], 32 * (u - g % 2))
                act.activation(ysb[g % 2][:], psY[:], ACT.Copy).then_inc(s_yc, 1)

            def step(n, b, st, last):
                u = G * b + st - 2
                if there(u):
                    if there(u - 2):
                        act.wait_ge(s_pv, u - 1)
                    for k in range(EN):
                        j, h0, nh = e_units[k]
                        act.wait_ge(s_er, EN * u + k + 1)
                        bank, pr = psE[k % 2], probs[st % 2][j]
                        if j < 2:
                            src, dst = bank[:, :, 0:W[j]], pr[:, h0:h0 + 2, :]
                        elif j == 2:
                            src, dst = bank[:], pr[:].rearrange("p (a h) q -> p a (h q)", a=2)
                        else:
                            src, dst = bank[:, 0], pr[:].rearrange("p h q -> p (h q)")
                        act.activation(dst, src, ACT.Exp).then_inc(s_ex, 1)
                        if k == 1 and there(u - 1):
                            copy_y(u - 1, st + 1)
                        if k == 3 and st == 0 and not last:
                            copy_x(use_next(b, 0))
                if not last:
                    if st == 0 and not there(u):
                        copy_x(use_next(b, 0))
                    if st in (0, 1):
                        hi_part(b + 1, st, use_next(b, st + 1))
                    if st == 2:
                        if isinstance(b, int) and b == 0:
                            act.wait_ge(s_vinit, 4)
                        copy_v(1 - n, use_next(b, 3))
            steps(act, step, 2)
            copy_y(G * nb - 1, 1)


def pairs(eng, count, fn):
    for b in range(2):
        fn(b, b, False)
    with eng.Fori(1, count // 2 - 1) as i:
        for n in range(2):
            fn(n, 2 * i + n, False)
    for b in (count - 2, count - 1):
        fn(b % 2, b, b == count - 1)


class Norm:
    OPS = 8

    def __init__(self, sb, tiles=TT, means=1):
        self.stats = sb("stats", [P, tiles, 6], F32)
        self.carry = sb("carry", [P, 2], F32)
        self.a = sb("nrm_a", [P, tiles], F32)
        self.b = sb("nrm_b", [P, tiles], F32)
        self.c = sb("nrm_c", [P, tiles], F32)
        self.mean = [sb(f"nrm_mean{n}", [P, tiles], F32) for n in range(means)]
        self.var = sb("nrm_var", [P, tiles], F32)
        self.veps = sb("nrm_veps", [P, tiles], F32)

    def run(self, dve, groups, s, u, n=0, between=None, eps=EPS):
        base = self.OPS * u
        for k, (lo, hi, src, ready) in enumerate(groups):
            dve.wait_ge(*ready())
            dve.memset(self.carry[:, k:k + 1], 0.0)
            for t in range(lo, hi):
                i = dve.bn_stats(self.stats[:, t], src(t))
        i.then_inc(s, 1)
        cols = slice(groups[0][0], groups[-1][1])
        me, m2e, mo, m2o = (self.stats[:, cols, k] for k in (1, 2, 4, 5))
        a, b, c, mean, var, veps = (t[:, cols] for t in (self.a, self.b, self.c, self.mean[n], self.var, self.veps))
        fill = between or (lambda k: None)
        fill(0)
        dve.wait_ge(s, base + 1)
        dve.tensor_tensor(a, me, mo, ALU.subtract).then_inc(s, 1)
        dve.tensor_tensor(b, m2e, m2o, ALU.add).then_inc(s, 1)
        dve.tensor_tensor(mean, me, mo, ALU.add).then_inc(s, 1)
        fill(1)
        dve.wait_ge(s, base + 4)
        dve.scalar_tensor_tensor(out=c, in0=a, scalar=C / 4.0, in1=a, op0=ALU.mult, op1=ALU.mult).then_inc(s, 1)
        dve.tensor_scalar(mean, mean, 0.5, None, ALU.mult).then_inc(s, 1)
        fill(2)
        dve.wait_ge(s, base + 6)
        dve.tensor_tensor(var, b, c, ALU.add).then_inc(s, 1)
        fill(3)
        dve.wait_ge(s, base + 7)
        dve.tensor_scalar(veps, var, 1.0 / C, eps, ALU.mult, ALU.add).then_inc(s, 1)


def lead_pairs(count, eng, fn, lead=2, tail=2):
    for s in range(lead):
        fn(s % 2, s)
    with eng.Fori(lead // 2, (count - tail) // 2) as i:
        for n in range(2):
            fn(n, 2 * i + n)
    for s in range(count - tail, count):
        fn(s % 2, s)


def project(nc, x_all, y_scr, rec_scr, shared, w_projT, xbuf, rw, rb, tab, sctab, sc, ident, nb):
    nt = nb * TT
    with ExitStack() as ctx:
        sb = lambda name, shape, dt: ctx.enter_context(nc.sbuf_tensor("pj_" + name, shape, dt))
        sem = lambda name: ctx.enter_context(nc.semaphore("pj_" + name))
        two = lambda name, shape: [sb(f"{name}{i}", shape, F32) for i in range(2)]
        ysb, sums, s_yw, s_sum, s_inv, s_rw, s_sc = shared
        num, rec, y, xn, xT = two("num", [P, T]), two("rec", [P, T]), two("y", [P, T]), two("xn", [P, TT, C]), two("xT", [P, T])
        wp = sb("wp", [P, C], F32)
        rws = sb("rws", [P, E], F32)
        rbs = sb("rbs", [P, TT, E], F32)
        mhalf = sb("mhalf", [P, TT], F32)
        rstd = sb("rstd", [P, TT], F32)
        nrm = Norm(sb, means=2)
        lg = sb("lg", [P, nt, E], F32)
        ex = sb("ex", [P, nt, E], F32)
        top = sb("top", [P, nt], F32)
        tot = sb("tot", [P, nt], F32)
        psP = [ctx.enter_context(nc.psum_tensor(f"pj_psP{i}", [P, T], F32)) for i in range(2)]
        psX = [ctx.enter_context(nc.psum_tensor(f"pj_psX{i}", [P, T], F32)) for i in range(2)]
        psL = [ctx.enter_context(nc.psum_tensor(f"pj_psL{i}", [P, TT, E], F32)) for i in range(2)]
        s_w, s_y, s_pr, s_x1, s_chain, s_rs, s_x1st, s_set, s_xn, s_tr, s_xT, s_lr, s_lg, s_c, s_ex = (
            sem(n) for n in (
                "weights", "y_ready", "proj_ready", "x1_ready", "chain", "rstd",
                "x1_stored", "mhalf_set", "xn_ready", "turned", "xT_ready", "logits_ready", "logits_kept", "softmax",
                "exp_ready"))
        s_ld = [sem(f"loaded{n}") for n in range(2)]
        s_st = [sem(f"xn_stored{n}") for n in range(2)]
        block = ctx.enter_context(nc.Block())
        some = lambda s, lo=0, hi=nb: not isinstance(s, int) or lo <= s < hi

        @block.sync
        def _(sp):
            def load(n, b):
                one = bass.ds(b, 1)
                sp.dma_start(num[n][:], y_scr[one, 0:D].rearrange("b r h q -> (b r h) q")).then_inc(s_ld[n], 16)
                src = rec_scr[one].rearrange("b h q -> b (h q)")
                sp.dma_start(rec[n][:], src.rearrange("b (h q) -> b h q", h=H).to_broadcast([D, H, T])).then_inc(s_ld[n], 16)

            for n in range(2):
                load(n, n)
            for half in s_yw:
                sp.wait_ge(half, 64 * 2 * nb)
            sp.dma_start(sums[1][:], sum_rows(y_scr[nb - LATE:nb, D], P // LATE)).then_inc(s_sum, 16)

            def step(n, s):
                if isinstance(s, int) and s == 3:
                    sp.wait_ge(s_inv, 2)
                    sp.dma_start(sum_rows(rec_scr[nb - LATE:nb], P // LATE), sums[1][:]).then_inc(s_rw, 16)
                if isinstance(s, int) and s == nb - LATE:
                    sp.wait_ge(s_rw, 32)
                if some(s, 2):
                    sp.wait_ge(s_y, s - 1)
                    load(n, s)
            lead_pairs(nb, sp, step, 4, LATE)
            sp.wait_ge(s_c, 5)
            sp.dma_start(sctab, sc[:]).then_inc(s_sc, 16)

        @block.gpsimd
        def _(pool):
            pool.memset(mhalf[:], -0.5).then_inc(s_set, 1)
            pool.wait_ge(s_set, 1)

            def step(n, s):
                if some(s):
                    pool.wait_ge(s_ld[n], 16 * (s - n) + 32)
                    if some(s, 2):
                        pool.wait_ge(s_pr, s - 1)
                    pool.tensor_tensor(y[n][:], num[n][:], rec[n][:], ALU.mult).then_inc(s_y, 1)
                if some(s - 1):
                    pool.wait_ge(s_chain, Norm.OPS * s)
                    if some(s - 1, 1):
                        pool.wait_ge(s_xn, s - 1)
                    pool.tensor_tensor(rstd[:], nrm.veps[:], mhalf[:], ALU.pow).then_inc(s_rs, 1)
            lead_pairs(nb + 2, pool, step, 4)

        @block.tensor
        def _(pe):
            pe.wait_ge(s_w, 16 * 3)

            def step(n, s):
                m = 1 - n
                if some(s):
                    pe.wait_ge(s_y, s + 1)
                    if some(s, 2):
                        pe.wait_ge(s_x1, s - 1)
                    for t in range(TT):
                        i = pe.matmul(psP[n][:, P * t:P * t + P], y[n][:, P * t:P * t + P], wp[:], start=True, stop=True)
                    i.then_inc(s_pr, 1)
                if some(s - 3):
                    pe.wait_ge(s_xT, s - 2)
                    if some(s - 3, 2):
                        pe.wait_ge(s_lg, s - 4)
                    for t in range(TT):
                        i = pe.matmul(psL[m][:, t], xT[m][:, P * t:P * t + P], rws[:], start=True, stop=True)
                    i.then_inc(s_lr, 1)
                if some(s - 2):
                    pe.wait_ge(s_xn, s - 1)
                    for t in range(TT):
                        i = pe.transpose(psX[n][:, P * t:P * t + P], xn[n][:, t], ident[:])
                    i.then_inc(s_tr, 1)
            lead_pairs(nb + 4, pe, step, 6, 4)

        @block.vector
        def _(dve):
            dve.wait_ge(s_w, 16 * 3)

            def step(n, s):
                m = 1 - n
                if some(s):
                    dve.wait_ge(s_pr, s + 1)
                    xb = x_all[:, bass.ds(TT * s, TT), :].rearrange("p t c -> p (t c)")
                    dve.tensor_tensor(xb, psP[n][:], xb, ALU.add).then_inc(s_x1, 1)
                def normalise(t):
                    if some(s - 1):
                        i = dve.tensor_scalar(xn[m][:, t], x_all[:, bass.ds(TT * (s - 1) + t, 1), :].rearrange("p a c -> p (a c)"),
                                              nrm.mean[m][:, t:t + 1], rstd[:, t:t + 1], ALU.subtract, ALU.mult)
                        if t == TT - 1:
                            i.then_inc(s_xn, 1)
                if some(s - 1):
                    dve.wait_ge(s_rs, s)
                    if some(s - 1, 2):
                        dve.wait_ge(s_st[m], 8 * (s - 1 - m))
                        dve.wait_ge(s_tr, s - 2)
                    normalise(0)
                if some(s):
                    nrm.run(dve, [(0, TT, lambda t: x_all[:, bass.ds(TT * s + t, 1), :].rearrange("p a c -> p (a c)"), lambda: (s_x1, s + 1))],
                            s_chain, s, n, lambda k: k and normalise(k))
                else:
                    for t in range(1, TT):
                        normalise(t)
                if isinstance(s, int) and s == 1:
                    dve.wait_ge(s_sum, 32)
                    dve.reciprocal(sums[1][:], sums[1][:]).then_inc(s_inv, 1)
                if some(s - 3):
                    dve.wait_ge(s_lr, s - 2)
                    dve.tensor_tensor(lg[:, bass.ds(TT * (s - 3), TT), :], psL[m][:], rbs[:], ALU.add).then_inc(s_lg, 1)
            lead_pairs(nb + 4, dve, step, 6, 4)
            dve.wait_ge(s_lg, nb)
            dve.tensor_reduce(top[:], lg[:], AX, ALU.max).then_inc(s_c, 1)
            dve.wait_ge(s_c, 1)
            dve.tensor_tensor(lg[:], lg[:], top[:].unsqueeze(2).to_broadcast([P, nt, E]), ALU.subtract).then_inc(s_c, 1)
            dve.wait_ge(s_ex, 1)
            dve.tensor_reduce(tot[:], ex[:], AX, ALU.add).then_inc(s_c, 1)
            dve.wait_ge(s_c, 3)
            dve.reciprocal(tot[:], tot[:]).then_inc(s_c, 1)
            dve.wait_ge(s_c, 4)
            dve.tensor_tensor(sc[:], ex[:], tot[:].unsqueeze(2).to_broadcast([P, nt, E]), ALU.mult).then_inc(s_c, 1)

        @block.scalar
        def _(act):
            for dst, src in ((wp[:], w_projT), (rws[:], rw), (rbs[:], rb.partition_broadcast(P).to_broadcast([P, TT, E]))):
                act.dma_start(dst, src).then_inc(s_w, 16)

            def step(n, s):
                if some(s):
                    act.wait_ge(s_x1, s + 1)
                    act.dma_start(xbuf[:, bass.ds(TT * s, TT), :], x_all[:, bass.ds(TT * s, TT), :]).then_inc(s_x1st, 16)
                if some(s - 2):
                    act.wait_ge(s_xn, s - 1)
                    act.dma_start(tab[:, bass.ds(TT * (s - 2), TT), :], xn[n][:]).then_inc(s_st[n], 16)
                    act.wait_ge(s_tr, s - 1)
                    if some(s - 2, 2):
                        act.wait_ge(s_lr, s - 3)
                    act.activation(xT[n][:], psX[n][:], ACT.Copy).then_inc(s_xT, 1)
            lead_pairs(nb + 2, act, step, 4)
            act.wait_ge(s_c, 2)
            act.activation(ex[:], lg[:], ACT.Exp).then_inc(s_ex, 1)
            act.wait_ge(s_x1st, 16 * nb)
            for n in range(2):
                act.wait_ge(s_st[n], 8 * nb)


def choose(nc, sc, s_sc, ident, cst, idx, nb):
    nt = nb * TT
    nj = nt * E // P
    DIGITS = 8
    with ExitStack() as ctx:
        sb = lambda name, shape, dt: ctx.enter_context(nc.sbuf_tensor("ch_" + name, shape, dt))
        sem = lambda name: ctx.enter_context(nc.semaphore("ch_" + name))
        scT = sb("scT", [P, nj * P], F32)
        high, low, key = (sb(n, [P, nj * P], U16) for n in ("high", "low", "key"))
        lowf = sb("lowf", [P, nj * P], F32)
        above = sb("above", [P, nj * P], F32)
        junk = [sb(f"counted{j}", [P, nj * P], BF16) for j in range(3)]
        junk2 = sb("junk2", [P, 2 * E, P], BF16)
        cnt = sb("cnt", [P, 3], F16)
        junk3 = sb("junk3", [P, 3], F32)
        digit = sb("digit", [P, 1], F32)
        base = [sb(f"base{i}", [P, 1], F32) for i in range(2)]
        cand = sb("cand", [P, 3], F32)
        bits = sb("bits", [P, 2], U16)
        thrb = sb("thrb", [P, P], F32)
        thr = sb("thr", [P, E], F32)
        same = sb("same", [P, P], F16)
        tri = sb("tri", [P, P], BF16)
        ones = sb("ones", [P, P], BF16)
        strict = sb("strict", [nt, nt], BF16)
        step = sb("step", [P, DIGITS + 1, 4], F32)
        iota = sb("iota", [nt, KTOP], F32)
        tileno = sb("tileno", [nt, E], BF16)
        slotno = sb("slotno", [P, 2 * E], F32)
        gt = sb("gt", [P, nt, E], BF16)
        eq = sb("eq", [P, nt, E], BF16)
        sel = sb("sel", [P, nt, E], BF16)
        cgt = sb("cgt", [P, E], F32)
        tots = sb("tots", [P, E, nt], F32)
        incl = sb("incl", [P, E, nt], F32)
        onesf = sb("onesf", [P, nt], F32)
        pe_ = sb("peq", [P, nt, E], F32)
        pin = sb("pin", [nt, E, P], BF16)
        pex2 = sb("pex2", [nt, E, 2], BF16)
        pex = sb("pex", [nt, E], F32)
        pinc = sb("pinc", [nt, E], F32)
        ge = sb("ge", [nt, E, KTOP], BF16)
        oh = sb("oh", [nt, E, KTOP], BF16)
        rr = sb("rr", [P, 2 * E], F32)
        cn = sb("cn", [P, 2 * E], F32)
        til = sb("til", [P, 2 * E], F32)
        psA = ctx.enter_context(nc.psum_tensor("ch_psA", [P, 512], F32))
        psB = ctx.enter_context(nc.psum_tensor("ch_psB", [P, 512], F32))
        psC = ctx.enter_context(nc.psum_tensor("ch_psC", [P, 512], F32))
        psL = ctx.enter_context(nc.psum_tensor("ch_psL", [P, 4, 512], F32))
        psR = ctx.enter_context(nc.psum_tensor("ch_psR", [P, 512], F32))
        s_cst, s_tr, s_cp, s_cnt, s_tot, s_thr, s_thrT, s_masks, s_pre, s_sel, s_pin, s_pinc, s_off, s_oh, s_look, s_c = (
            sem(n) for n in ("consts", "turned", "scT_ready", "counted", "total", "thr_ready", "thr_turned", "masks",
                             "prefixes", "selected", "pin_ready", "pin_copied", "offsets", "onehots", "looked", "chain"))
        block = ctx.enter_context(nc.Block())

        @block.sync
        def _(sp):
            for dst, name in ((same, "c_same"), (tri, "c_tri"), (ones, "c_ones"), (strict, "c_strict"), (iota, "c_iota"), (tileno, "c_tileno"), (slotno, "c_slotno")):
                sp.dma_start(dst[:], cst[name][0:dst.shape[0], 0:dst.shape[1]]).then_inc(s_cst, 16)
            sp.dma_start(step[:], cst["c_step"]).then_inc(s_cst, 16)
            sp.wait_ge(s_sc, 16)

        @block.tensor
        def _(pe):
            for j in range(nj):
                i = pe.transpose(psA[:, P * j:P * j + P], sc[:, 16 * j:16 * j + 16, :].rearrange("p t e -> p (t e)"), ident[:])
            i.then_inc(s_tr, 1)
            pe.wait_ge(s_cst, 16 * 8)
            with pe.Fori(0, 2 * DIGITS - 1) as k:
                pe.wait_ge(s_cnt, k + 1)
                pe.matmul(psR[:, 0:3], same[:], cnt[:], start=True, stop=True).then_inc(s_tot, 1)
            pe.wait_ge(s_thr, 1)
            pe.transpose(psA[:, 0:P], thrb[:], ident[:]).then_inc(s_thrT, 1)
            pe.wait_ge(s_masks, 1)
            nn = nt * E
            pe.matmul(psA[:, 0:nn], ones[:], gt[:].rearrange("p t e -> p (t e)"), start=True, stop=True)
            pe.matmul(psB[:, 0:nn], tri[:], eq[:].rearrange("p t e -> p (t e)"), start=True, stop=True)
            pe.matmul(psC[:, 0:nn], ones[:], eq[:].rearrange("p t e -> p (t e)"), start=True, stop=True).then_inc(s_pre, 1)
            pe.wait_ge(s_sel, 1)
            for e in range(E):
                i = pe.matmul(psL[0:nt, e // 4, P * (e % 4):P * (e % 4) + P], sel[:, :, e], tri[:], start=True, stop=True)
            i.then_inc(s_pin, 1)
            pe.wait_ge(s_pinc, 1)
            pe.matmul(psR[0:nt, 0:E], strict[:], pin[:, :, P - 1], start=True, stop=True).then_inc(s_off, 1)
            pe.wait_ge(s_oh, 1)
            for k in range(2 * E):
                e, h = k // 2, k % 2
                ohk = oh[:, e, P * h:P * h + P]
                pe.matmul(psL[:, k // 4, P * (k % 4):P * (k % 4) + P], ohk, pin[:, e, :], start=True, stop=True)
                i = pe.matmul(psR[:, 2 * k:2 * k + 2], ohk, pex2[:, e, :], start=True, stop=True)
            i.then_inc(s_look, 1)

        @block.vector
        def _(dve):
            chain = [0]

            def link(ins):
                chain[0] += 1
                ins.then_inc(s_c, 1)
                dve.wait_ge(s_c, chain[0])

            dve.memset(base[0][:], 0.0)
            dve.memset(base[1][:], 0.0)
            link(dve.memset(onesf[:], 1.0))
            dve.wait_ge(s_tr, 1)
            dve.tensor_copy(scT[:], psA[:, 0:nj * P]).then_inc(s_cp, 1)
            dve.wait_ge(s_cst, 16 * 8)
            dve.wait_ge(s_cp, 1)
            halves = scT[:].bitcast(U16).rearrange("p (n two) -> p n two", two=2)
            dve.tensor_copy(low[:], halves[:, :, 0])
            dve.tensor_copy(cand[:], step[:, 1, 1:4])
            link(dve.tensor_copy(high[:], halves[:, :, 1]))

            def find(keys, found, k, rounds):
                for j in range(3):
                    i = dve.tensor_scalar(junk[j][:], keys[:], cand[:, j:j + 1], 0.0, ALU.is_ge, ALU.add, accum_out=cnt[:, j:j + 1])
                i.then_inc(s_cnt, 1)
                dve.wait_ge(s_tot, rounds + 1)
                dve.tensor_scalar(junk3[:], psR[:, 0:3], KTOP - 0.5, 0.0, ALU.is_ge, ALU.add, accum_out=digit[:]).then_inc(s_cp, 1)
                dve.wait_ge(s_cp, 3 * rounds + 2)
                dve.scalar_tensor_tensor(out=found[:], in0=step[:, bass.ds(k, 1), 0], scalar=digit[:, 0:1], in1=found[:],
                                         op0=ALU.mult, op1=ALU.add).then_inc(s_cp, 1)
                dve.wait_ge(s_cp, 3 * rounds + 3)
                dve.tensor_scalar(cand[:], step[:, bass.ds(k + 1, 1), 1:4].rearrange("p a c -> p (a c)"), found[:, 0:1], None,
                                  ALU.add).then_inc(s_cp, 1)
                dve.wait_ge(s_cp, 3 * rounds + 4)
            with dve.Fori(1, DIGITS) as k:
                find(high, base[0], k, k - 1)
            dve.tensor_scalar(above[:], high[:], base[0][:, 0:1], 65535.0, ALU.is_gt, ALU.mult)
            dve.tensor_copy(cand[:], step[:, 0, 1:4])
            link(dve.scalar_tensor_tensor(out=lowf[:], in0=high[:], scalar=base[0][:, 0:1], in1=low[:], op0=ALU.is_equal, op1=ALU.mult))
            link(dve.tensor_tensor(key[:], lowf[:], above[:], ALU.add))
            with dve.Fori(0, DIGITS) as k:
                find(key, base[1], k, k + DIGITS - 1)
            dve.tensor_copy(bits[:, 0:1], base[1][:])
            link(dve.tensor_copy(bits[:, 1:2], base[0][:]))
            dve.tensor_copy(thrb[:], bits[:].bitcast(F32).to_broadcast([P, P])).then_inc(s_thr, 1)
            dve.wait_ge(s_thrT, 1)
            link(dve.tensor_copy(thr[:], psA[:, 0:E]))
            tb = thr[:].unsqueeze(1).to_broadcast([P, nt, E])
            dve.tensor_tensor(gt[:], sc[:], tb, ALU.is_gt)
            dve.tensor_tensor(eq[:], sc[:], tb, ALU.is_equal).then_inc(s_masks, 1)
            dve.wait_ge(s_pre, 1)
            nn = nt * E
            dve.tensor_reduce(cgt[:], psA[:, 0:nn].rearrange("p (t e) -> p e t", e=E), AX, ALU.add)
            link(dve.tensor_copy(tots[:], psC[:, 0:nn].rearrange("p (t e) -> p e t", e=E)))
            for e in range(E):
                i = dve.tensor_tensor_scan(incl[:, e], onesf[:], tots[:, e], 0.0, ALU.mult, ALU.add)
            link(i)
            link(dve.tensor_tensor(incl[:], incl[:], tots[:], ALU.subtract))
            link(dve.tensor_tensor(pe_[:], psB[:, 0:nn].rearrange("p (t e) -> p t e", e=E), incl[:].rearrange("p e t -> p t e"), ALU.add))
            link(dve.tensor_tensor(pe_[:], pe_[:], cgt[:].unsqueeze(1).to_broadcast([P, nt, E]), ALU.add))
            link(dve.scalar_tensor_tensor(out=pe_[:], in0=pe_[:], scalar=KTOP + 0.5, in1=eq[:], op0=ALU.is_lt, op1=ALU.mult))
            dve.tensor_tensor(sel[:], pe_[:], gt[:], ALU.add).then_inc(s_sel, 1)
            dve.wait_ge(s_pin, 1)
            dve.tensor_copy(pin[:], psL[0:nt, 0:2].rearrange("p a (e k) -> p (a e) k", e=4)).then_inc(s_pinc, 1)
            dve.wait_ge(s_off, 1)
            dve.tensor_copy(pex2[:, :, 0], psR[0:nt, 0:E])
            dve.tensor_copy(pex2[:, :, 1], tileno[:])
            dve.wait_ge(s_pinc, 1)
            dve.tensor_tensor(pinc[:], psR[0:nt, 0:E], pin[:, :, P - 1], ALU.add)
            link(dve.tensor_copy(pex[:], psR[0:nt, 0:E]))
            for e in range(E):
                i = dve.tensor_scalar(ge[:, e], iota[:], pex[:, e:e + 1], None, ALU.is_ge)
            link(i)
            for e in range(E):
                i = dve.scalar_tensor_tensor(out=oh[:, e], in0=iota[:], scalar=pinc[:, e:e + 1], in1=ge[:, e],
                                             op0=ALU.is_lt, op1=ALU.mult)
            i.then_inc(s_oh, 1)
            dve.wait_ge(s_look, 1)
            pr = psR[:, 0:4 * E].rearrange("p (k a) -> p k a", a=2)
            dve.tensor_copy(til[:], pr[:, :, 1])
            link(dve.tensor_tensor(rr[:], slotno[:], pr[:, :, 0], ALU.subtract))
            for k in range(2 * E):
                i = dve.tensor_scalar(junk2[:, k], psL[:, k // 4, P * (k % 4):P * (k % 4) + P], rr[:, k:k + 1], 0.0,
                                      ALU.is_le, ALU.add, accum_out=cn[:, k:k + 1])
            link(i)
            link(dve.scalar_tensor_tensor(out=idx[:], in0=cn[:], scalar=float(nt), in1=til[:], op0=ALU.mult, op1=ALU.add))


def expert_choice(nc, idx, tab, sctab, w1, b1, w2, b2, xbuf, ident, nb):
    nt = nb * TT
    FT = 4
    with ExitStack() as ctx:
        sb = lambda name, shape, dt: ctx.enter_context(nc.sbuf_tensor("ec_" + name, shape, dt))
        sem = lambda name: ctx.enter_context(nc.semaphore("ec_" + name))
        xg = sb("xg", [P, 2 * E, C], F32)
        gg = sb("gg", [P, 2 * E * E], F32)
        w1s = [sb(f"w1s{i}", [P, FT * P], F32) for i in range(2)]
        w2s = [sb(f"w2s{i}", [P, FT, C], F32) for i in range(2)]
        b1s = sb("b1s", [P, E, FT], F32)
        b2s = sb("b2s", [P, E, C], F32)
        xT = [sb(f"xgT{i}", [P, 2 * P], F32) for i in range(2)]
        hT = [sb(f"hT{i}", [P, FT, 2 * P], F32) for i in range(2)]
        ctr = sb("ctr", [P, 2 * E, C], F32)
        tmp = sb("tmp", [P, 2, C], F32)
        psX = [ctx.enter_context(nc.psum_tensor(f"ec_psX{i}", [P, 2 * P], F32)) for i in range(2)]
        psH = [ctx.enter_context(nc.psum_tensor(f"ec_psH{i}", [P, 2, 512], F32)) for i in range(2)]
        psO = [ctx.enter_context(nc.psum_tensor(f"ec_psO{i}", [P, 2, C], F32)) for i in range(2)]
        s_b, s_tr, s_xT, s_h, s_hT, s_o, s_t, s_ctr, s_sc = (sem(n) for n in (
            "biases", "turned", "xT_ready", "h_ready", "hT_ready", "o_ready", "tmp_ready",
            "contrib", "scattered"))
        s_w = [sem(f"weights{n}") for n in range(2)]
        s_xg = [sem(f"rows_gathered{e}") for e in range(3)]
        s_gg = [sem(f"gates_gathered{e}") for e in range(3)]
        block = ctx.enter_context(nc.Block())
        tabr = tab.rearrange("p t c -> (p t) c")
        sctr = sctab.rearrange("p t e -> (p t) e")
        xr = xbuf.rearrange("p t c -> (p t) c")

        @block.gpsimd
        def _(pool):
            def gather(e):
                offs = [bass.IndirectOffsetOnAxis(ap=idx[:, k:k + 1], axis=0) for k in (2 * e, 2 * e + 1)]
                for k, off in zip((2 * e, 2 * e + 1), offs):
                    pool.indirect_dma_start(xg[:, k, :], None, tabr, off).then_inc(s_xg[e % 3], 16)
                for k, off in zip((2 * e, 2 * e + 1), offs):
                    pool.indirect_dma_start(gg[:, E * k:E * k + E], None, sctr, off).then_inc(s_gg[e % 3], 16)

            gather(0)
            gather(1)
            for e in range(E):
                if e + 2 < E:
                    gather(e + 2)
                pool.wait_ge(s_ctr, e + 1)
                if e:
                    pool.wait_ge(s_sc, 32 * e)
                for k in (2 * e, 2 * e + 1):
                    off = bass.IndirectOffsetOnAxis(ap=idx[:, k:k + 1], axis=0)
                    pool.indirect_dma_start(xr, off, ctr[:, k, :], None, compute_op=ALU.add).then_inc(s_sc, 16)
            pool.wait_ge(s_sc, 32 * E)

        @block.sync
        def _(sp):
            sp.dma_start(b1s[:], b1).then_inc(s_b, 16)
            sp.dma_start(b2s[:], b2.partition_broadcast(P)).then_inc(s_b, 16)

            def load(n, e):
                sp.dma_start(w1s[n][:], w1[bass.ds(e, 1)].rearrange("e c f -> (e c) f")).then_inc(s_w[n], 16)
                sp.dma_start(w2s[n][:], w2[bass.ds(e, 1)].rearrange("e f t c -> (e f) t c")).then_inc(s_w[n], 16)
            load(0, 0)
            load(1, 1)
            with sp.Fori(0, E // 2 - 1) as i:
                for n in range(2):
                    sp.wait_ge(s_o, 2 * i + n + 1)
                    load(n, 2 * i + n + 2)

        @block.tensor
        def _(pe):
            def body(n, e, last):
                pe.wait_ge(s_xg[e % 3], 32 * (e // 3 + 1))
                pe.wait_ge(s_xT, e)
                for h in range(2):
                    i = pe.transpose(psX[n][:, P * h:P * h + P], xg[:, bass.ds(2 * e + h, 1), :].rearrange("p a c -> p (a c)"), ident[:])
                i.then_inc(s_tr, 1)
                pe.wait_ge(s_xT, e + 1)
                pe.wait_ge(s_w[n], 16 * (e - n) + 32)
                pe.wait_ge(s_hT, e)
                for f in range(FT):
                    i = pe.matmul(psH[n][:, f // 2, 2 * P * (f % 2):2 * P * (f % 2) + 2 * P], w1s[n][:, P * f:P * f + P], xT[n][:],
                                  start=True, stop=True)
                i.then_inc(s_h, 1)
                pe.wait_ge(s_hT, e + 1)
                pe.wait_ge(s_ctr, e)
                for h in range(2):
                    for f in range(FT):
                        i = pe.matmul(psO[n][:, h], hT[n][:, f, P * h:P * h + P], w2s[n][:, f], start=(f == 0), stop=(f == FT - 1))
                i.then_inc(s_o, 1)
            for e in range(E):
                body(e % 2, e, e == E - 1)

        @block.scalar
        def _(act):
            act.wait_ge(s_b, 32)

            def body(n, e, last):
                act.wait_ge(s_tr, e + 1)
                act.activation(xT[n][:], psX[n][:], ACT.Copy).then_inc(s_xT, 1)
                act.wait_ge(s_h, e + 1)
                for f in range(FT):
                    i = act.activation(hT[n][:, f], psH[n][:, f // 2, 2 * P * (f % 2):2 * P * (f % 2) + 2 * P], ACT.Relu,
                                       bias=b1s[:, bass.ds(e, 1), f:f + 1].rearrange("p a b -> p (a b)"))
                i.then_inc(s_hT, 1)
            for e in range(E):
                body(e % 2, e, e == E - 1)

        @block.vector
        def _(dve):
            dve.wait_ge(s_b, 32)

            def body(n, e, last):
                dve.wait_ge(s_o, e + 1)
                dve.wait_ge(s_ctr, e)
                for h in range(2):
                    i = dve.tensor_tensor(tmp[:, h], psO[n][:, h], b2s[:, bass.ds(e, 1), :].rearrange("p a c -> p (a c)"), ALU.add)
                i.then_inc(s_t, 1)
                dve.wait_ge(s_gg[e % 3], 32 * (e // 3 + 1))
                dve.wait_ge(s_t, e + 1)
                for h in range(2):
                    i = dve.tensor_scalar(ctr[:, bass.ds(2 * e + h, 1), :].rearrange("p a c -> p (a c)"), tmp[:, h],
                                          gg[:, bass.ds((2 * E + 1) * e + E * h, 1)], None, ALU.mult)
                i.then_inc(s_ctr, 1)
            for e in range(E):
                body(e % 2, e, e == E - 1)


def skewed(eng, nb, fn):
    for s in range(4):
        fn(s, s % 2)
    with eng.Fori(1, nb // 2 - 2) as i:
        for n in range(2):
            fn(2 * i + n + 2, n)
    for s in range(nb - 2, nb + 2):
        fn(s, s % 2)


def live(b, nb):
    return not isinstance(b, int) or 0 <= b < nb


def mixer(nc, x_all, xbuf, ident, win, wout, prm, rows, loads, nb):
    with ExitStack() as ctx:
        sb = lambda name, shape, dt: ctx.enter_context(nc.sbuf_tensor("mx_" + name, shape, dt))
        sem = lambda name: ctx.enter_context(nc.semaphore("mx_" + name))
        two = lambda name, shape, dt=F32: [sb(f"{name}{i}", shape, dt) for i in range(2)]
        win_s = sb("win", [P, 2 * C], F32)
        wout_s = sb("wout", [P, C], F32)
        prm_s = sb("prm", [P, 10], F32)
        col = lambda k: prm_s[:, k:k + 1]
        BU, BV, W0, W1, W2, CB, LA, SB, SC, SD = range(10)
        rows_s = sb("rows", [P, 3, TT, C], F32)
        decay = sb("decay", [P, 1], F32)
        decayb = sb("decayb", [P, T], F32)
        bc = sb("bc", [P, 1], F32)
        waited = sb("waited", [P, 1], F32)
        mhalf = sb("mhalf", [P, 2 * TT], F32)
        nrm = Norm(sb, 2 * TT)
        rstd = sb("rstd", [P, 2 * TT], F32)
        xn, xT, vs, c0, vl, hs, dv, ys, z, xo, ho, hn = (two(n, s) for n, s in (
            ("xn", [P, TT, C]), ("xT", [P, T]), ("vs", [P, T + 2]), ("c0", [P, T]), ("vl", [P, T]), ("hs", [P, T]),
            ("dv", [P, T]), ("ys", [P, T]), ("z", [P, T]), ("xo", [P, TT, C]), ("ho", [P, TT, C]), ("hn", [P, TT, C])))
        t1, t2 = sb("t1", [P, TT, C], F32), sb("t2", [P, TT, C], F32)
        ps = lambda n: ctx.enter_context(nc.psum_tensor("mx_" + n, [P, T], F32))
        psX = ps("psX")
        psU = [ps("psU0"), ps("psU1")]
        psV = [ps("psV0"), ps("psV1")]
        psO = [ps("psO0"), ps("psO1")]
        s_w, s_prm, s_ea, s_set, s_n, s_r, s_xn, s_tr, s_xT, s_uv, s_vs, s_c0, s_c, s_dv, s_y, s_ys, s_z, s_o, s_xo, \
            s_h, s_hn, s_t1, s_x3, s_pre, s_v, s_ahead = (sem(n) for n in (
                "weights", "params", "exp_a", "set", "stat", "rstd", "xn_ready", "turned", "xT_ready", "uv_ready",
                "v_ready", "conv0", "conv", "dv_ready", "y_ready", "silu_y", "z_ready", "out_ready", "xo_ready", "h_ready",
                "hn_ready", "t1_ready", "x3_ready", "prepared", "v_product", "loaded_ahead"))
        s_ld = [sem(f"loaded{n}") for n in range(2)]
        block = ctx.enter_context(nc.Block())

        @block.sync
        def _(sp):
            sp.dma_start(prm_s[:], prm).then_inc(s_prm, 16)

            def load(n, b):
                sp.dma_start(x_all[:, bass.ds(TT * b, TT), :], xbuf[:, bass.ds(TT * b, TT), :]).then_inc(s_ld[n], 16)
            for n in range(2):
                load(n, n)
            for dst, src in ((win_s[:], win), (wout_s[:], wout)):
                sp.dma_start(dst, src).then_inc(s_w, 16)
            with sp.Fori(0, nb // 2 - 1) as i:
                for n in range(2):
                    sp.wait_ge(s_n, Norm.OPS * (2 * i + n + 1))
                    load(n, 2 * i + n + 2)
            for dst, src in loads:
                sp.dma_start(dst, src).then_inc(s_ahead, 16)
            sp.wait_ge(s_ahead, 16 * len(loads))

        @block.gpsimd
        def _(pool):
            pool.memset(mhalf[:], -0.5).then_inc(s_set, 1)
            for n in range(2):
                pool.memset(vs[n][:], 0.0).then_inc(s_set, 1)
            pool.wait_ge(s_set, 3)
            pool.wait_ge(s_w, 16 * (TT + 2))

            def factors(s, lo, hi):
                pool.wait_ge(s_n, Norm.OPS * s + 16)
                cols = slice(lo, hi)
                pool.tensor_tensor(rstd[:, cols], nrm.veps[:, cols], mhalf[:, cols], ALU.pow).then_inc(s_r, 1)

            factors(-1, 0, TT)

            def step(s, n):
                b = s - 2
                if live(s + 1, nb) or live(b, nb):
                    if live(s, nb):
                        pool.wait_ge(s_xn, s + 1)
                    if live(b, nb):
                        if not isinstance(b, int) or b:
                            pool.wait_ge(s_hn, b)
                            pool.wait_ge(s_x3, b)
                    factors(s, 0 if live(s + 1, nb) else TT, 2 * TT if live(b, nb) else TT)
                if live(b, nb):
                    pool.tensor_tensor(t2[:], x_all[:, bass.ds(TT * b, TT), :], rows_s[:, 2], ALU.add)
                if live(s, nb):
                    pool.wait_ge(s_xn, s + 1)
                    if not isinstance(s, int) or s >= 2:
                        pool.wait_ge(s_h, s - 1)
                    pool.tensor_tensor(xo[n][:], xn[n][:], rows_s[:, 0], ALU.add).then_inc(s_xo, 1)
                if live(b, nb):
                    pool.wait_ge(s_hn, b + 1)
                    pool.tensor_tensor(t1[:], hn[n][:], rows_s[:, 1], ALU.mult).then_inc(s_t1, 1)
                    pool.wait_ge(s_t1, b + 1)
                    pool.tensor_tensor(waited[:], mhalf[:, 0:1], mhalf[:, 0:1], ALU.add)
                    pool.tensor_tensor(x_all[:, bass.ds(TT * b, TT), :], t1[:], t2[:], ALU.add).then_inc(s_x3, 1)
            skewed(pool, nb, step)

        @block.tensor
        def _(pe):
            pe.wait_ge(s_w, 16 * (TT + 2))

            def step(s, n):
                b = s - 2
                if live(b, nb):
                    pe.wait_ge(s_z, b + 1)
                    if not isinstance(b, int) or b >= 2:
                        pe.wait_ge(s_h, b - 1)
                    for t in range(TT):
                        i = pe.matmul(psO[n][:, P * t:P * t + P], z[n][:, P * t:P * t + P], wout_s[:], start=True, stop=True)
                    i.then_inc(s_o, 1)
                if live(s, nb):
                    pe.wait_ge(s_xn, s + 1)
                    if not isinstance(s, int) or s:
                        pe.wait_ge(s_xT, s)
                    for t in range(TT):
                        i = pe.transpose(psX[:, P * t:P * t + P], xn[n][:, t], ident[:])
                    i.then_inc(s_tr, 1)
                    pe.wait_ge(s_xT, s + 1)
                    if not isinstance(s, int) or s >= 2:
                        pe.wait_ge(s_vs, s - 1)
                    pe.matmul(psV[n][:], win_s[:, C:2 * C], xT[n][:], start=True, stop=True).then_inc(s_v, 1)
                    if not isinstance(s, int) or s >= 2:
                        pe.wait_ge(s_z, s - 1)
                    pe.matmul(psU[n][:], win_s[:, 0:C], xT[n][:], start=True, stop=True).then_inc(s_uv, 1)
            skewed(pe, nb, step)

        @block.scalar
        def _(act):
            for t in range(TT):
                act.dma_start(rows_s[:, :, t], rows.partition_broadcast(P)).then_inc(s_w, 16)
            act.wait_ge(s_prm, 16)
            act.wait_ge(s_set, 3)
            act.activation(decay[:], col(LA), ACT.Exp, scale=-1.0).then_inc(s_ea, 1)

            def step(s, n):
                m = 1 - n
                if live(s, nb):
                    act.wait_ge(s_tr, s + 1)
                    if not isinstance(s, int) or s >= 2:
                        act.wait_ge(s_uv, s - 1)
                    act.activation(xT[n][:], psX[:], ACT.Copy).then_inc(s_xT, 1)
                if live(s - 1, nb):
                    b = s - 1
                    act.wait_ge(s_c, 3 * b + 2)
                    act.activation(dv[m][:], vl[m][:], ACT.Copy, scale=col(SD)).then_inc(s_dv, 1)
                if live(s, nb):
                    act.wait_ge(s_v, s + 1)
                    if not isinstance(s, int) or s >= 2:
                        act.wait_ge(s_c, 3 * s - 3)
                    act.activation(vs[n][:, 1:T + 1], psV[n][:], ACT.Silu, bias=col(BV)).then_inc(s_vs, 1)
                    act.wait_ge(s_vs, s + 1)
                    act.activation(c0[n][:], vs[n][:, 1:T + 1], ACT.Identity, bias=col(CB), scale=col(W1)).then_inc(s_c0, 1)
                if live(s - 1, nb):
                    b = s - 1
                    act.wait_ge(s_y, b + 1)
                    if not isinstance(b, int) or b >= 2:
                        act.wait_ge(s_z, b - 1)
                    act.activation(ys[m][:], hs[m][:], ACT.Silu).then_inc(s_ys, 1)
            skewed(act, nb, step)

        @block.vector
        def _(dve):
            dve.wait_ge(s_ea, 1)
            dve.tensor_scalar(decay[:], decay[:], 1.0, None, ALU.add).then_inc(s_pre, 1)
            dve.wait_ge(s_pre, 1)
            dve.reciprocal(decay[:], decay[:]).then_inc(s_pre, 1)
            dve.tensor_tensor(bc[:], col(SB), col(SC), ALU.mult).then_inc(s_pre, 1)
            dve.wait_ge(s_pre, 3)
            dve.tensor_copy(decayb[:], decay[:].to_broadcast([P, T])).then_inc(s_pre, 1)
            dve.wait_ge(s_pre, 4)

            def x_tile(s, t):
                return x_all[:, bass.ds(TT * s + t, 1), :].rearrange("p a c -> p (a c)")

            def x_group(s, n):
                return 0, TT, lambda t: x_tile(s, t), lambda: (s_ld[n], 8 * (s - n) + 16)

            nrm.run(dve, [x_group(0, 0)], s_n, 0)

            def step(s, n):
                m = 1 - n
                if live(s, nb):
                    dve.wait_ge(s_r, s + 1)
                    if not isinstance(s, int) or s >= 2:
                        dve.wait_ge(s_tr, s - 1)
                        dve.wait_ge(s_xo, s - 1)
                    for t in range(TT):
                        i = dve.tensor_scalar(xn[n][:, t], x_tile(s, t), nrm.mean[0][:, t:t + 1], rstd[:, t:t + 1], ALU.subtract, ALU.mult)
                    i.then_inc(s_xn, 1)

                def tap(k):
                    if live(s - 1, nb):
                        b = s - 1
                        if k == 0:
                            dve.wait_ge(s_c0, b + 1)
                        elif not isinstance(b, int) or b:
                            dve.wait_ge(s_dv, b)
                        if not isinstance(b, int) or b or k:
                            dve.wait_ge(s_c, 3 * b + k // 2)
                        dve.scalar_tensor_tensor(out=(vl if k else c0)[m][:], in0=vs[m][:, k:T + k], scalar=col(W2 if k else W0),
                                                 in1=c0[m][:], op0=ALU.mult, op1=ALU.add).then_inc(s_c, 1)

                def add_out():
                    b = s - 2
                    tap(0)
                    dve.wait_ge(s_o, b + 1)
                    dve.wait_ge(s_xo, b + 1)
                    dve.tensor_tensor(ho[n][:], psO[n][:].rearrange("p (t c) -> p t c", t=TT), xo[n][:], ALU.add).then_inc(s_h, 1)
                    tap(2)
                    return s_h, b + 1
                groups = []
                if live(s + 1, nb):
                    groups += [x_group(s + 1, m)]
                if live(s - 2, nb):
                    groups += [(TT, 2 * TT, lambda t: ho[n][:, t - TT], add_out)]
                else:
                    tap(0)
                    tap(2)
                if groups:
                    dve.wait_ge(s_r, s + 1)
                    nrm.run(dve, groups, s_n, s + 1)
                if live(s - 1, nb):
                    b = s - 1
                    dve.wait_ge(s_c, 3 * b + 2)
                    dve.wait_ge(s_ys, b)
                    dve.tensor_tensor_scan(hs[m][:], decayb[:], vl[m][:], 0.0, ALU.mult, ALU.add).then_inc(s_c, 1)
                    dve.wait_ge(s_c, 3 * b + 3)
                    dve.wait_ge(s_dv, b + 1)
                    dve.scalar_tensor_tensor(out=hs[m][:], in0=hs[m][:], scalar=bc[:, 0:1], in1=dv[m][:], op0=ALU.mult, op1=ALU.add)\
                       .then_inc(s_y, 1)
                if live(s - 2, nb):
                    b = s - 2
                    dve.wait_ge(s_r, s + 2)
                    if not isinstance(b, int) or b:
                        dve.wait_ge(s_t1, b)
                    for t in range(TT):
                        u = TT + t
                        i = dve.tensor_scalar(hn[n][:, t], ho[n][:, t], nrm.mean[0][:, u:u + 1], rstd[:, u:u + 1], ALU.subtract, ALU.mult)
                    i.then_inc(s_hn, 1)
                if live(s - 1, nb):
                    b = s - 1
                    dve.wait_ge(s_uv, b + 1)
                    dve.wait_ge(s_ys, b + 1)
                    if not isinstance(b, int) or b >= 2:
                        dve.wait_ge(s_o, b - 1)
                    dve.scalar_tensor_tensor(out=z[m][:], in0=psU[m][:], scalar=col(BU), in1=ys[m][:], op0=ALU.add, op1=ALU.mult)\
                       .then_inc(s_z, 1)
            skewed(dve, nb, step)


OUT_DMAS = 9


def ahead_loads(nc, ctx, nb, gwT, rmsw, W1T, W2T, W3T, cst):
    nt = nb * TT
    shapes = dict(gate_w=([P, E], F32), rms_w=([P, 1], F32), iotae=([P, nt, E], F32), w1s=([P, E, DE], F32),
                  w2s=([P, E, DE], F32), w3s=([P, len(FC), E, C], F32), tri=([P, P], BF16), ones=([P, P], BF16),
                  strict=([nt, nt], BF16), iota=([P, 2 * P], F32), tileno=([nt, E], BF16), jcol=([P, 2 * E], F32))
    a = {name: ctx.enter_context(nc.sbuf_tensor("ah_" + name, shape, dt)) for name, (shape, dt) in shapes.items()}
    loads = [(a["gate_w"][:], gwT), (a["rms_w"][:], rmsw), (a["iotae"][:], cst["c_iotae"][:, 0:nt]), (a["w1s"][:], W1T),
             (a["w2s"][:], W2T), (a["tri"][:], cst["c_tri"]), (a["ones"][:], cst["c_ones"]),
             (a["strict"][:], cst["c_strict"][0:nt, 0:nt]), (a["iota"][:], cst["c_iota"]),
             (a["tileno"][:], cst["c_tileno"][0:nt]), (a["jcol"][:], cst["c_slotno"])]
    loads += [(a["w3s"][0:w, f], W3T[P * f:P * f + w]) for f, w in enumerate(FC)]
    return a, loads


def gate(nc, x_all, ident, ahead, mask, rows, zeros, ytab, s_out, out, nb):
    nt = nb * TT
    with ExitStack() as ctx:
        sb = lambda name, shape, dt: ctx.enter_context(nc.sbuf_tensor("gt_" + name, shape, dt))
        sem = lambda name: ctx.enter_context(nc.semaphore("gt_" + name))
        gws, rmsw, iotae, w1s, w2s = (ahead[n] for n in ("gate_w", "rms_w", "iotae", "w1s", "w2s"))
        stats = sb("stats", [P, nt, 6], F32)
        a_, b_, mean, minus, var, veps, vrms, rstd, ry, mhalf, one = (sb(n, [P, nt], F32) for n in (
            "a", "b", "mean", "minus_mean", "var", "veps", "vrms", "rstd", "ry", "mhalf", "one"))
        warm = sb("warm", [P, 1], F32)
        y = [sb(f"y{i}", [P, TT, C], F32) for i in range(2)]
        acc_a, acc_b = (sb(n, [P, nt], F32) for n in ("acc_a", "acc_b"))
        scaled = sb("scaled", [P, TT, C], F32)
        yT = [sb(f"yT{i}", [P, T], F32) for i in range(2)]
        lg = sb("lg", [P, nt, E], F32)
        oh = [sb(f"oh{i}", [P, nt, E], F32) for i in range(2)]
        pen = sb("pen", [P, nt, E], F32)
        top = [sb(f"top{i}", [P, nt], F32) for i in range(2)]
        low, d, ex, wa, wb = (sb(n, [P, nt], F32) for n in ("low", "d", "ex", "wa", "wb"))
        psX = [ctx.enter_context(nc.psum_tensor(f"gt_psX{i}", [P, T], F32)) for i in range(2)]
        psL = [ctx.enter_context(nc.psum_tensor(f"gt_psL{i}", [P, TT, E], F32)) for i in range(2)]
        s_set, s_c, s_p, s_y, s_tr, s_yT, s_lr, s_lg, s_kept, s_ex, s_wf, s_mul, s_acc, s_scaled = (sem(n) for n in (
            "set", "chain", "powers", "y_ready", "turned", "yT_ready", "logits_ready", "logits_kept",
            "rows_kept", "exp_ready", "weights_full", "multiplied", "factors", "matrices_scaled"))
        s_base = [sem(f"base{n}") for n in range(2)]
        block = ctx.enter_context(nc.Block())

        @block.sync
        def _(sp):
            sp.wait_ge(s_set, 3)
            for r in (nt * P, nt * P + P):
                sp.dma_start(ytab[r:r + P], zeros[:]).then_inc(s_out, 16)
                sp.dma_start(out[r:r + P], zeros[:, 0:C]).then_inc(s_out, 16)
            outp = out[0:nt * P].rearrange("(p t) c -> p t c", p=P)
            q = nt // 4
            for n, by in ((0, 0), (2, 1), (1, 0), (3, 1)):
                sp.wait_ge(s_base[by], nb // 4 * (n % 2 + 1))
                sp.dma_start(outp[:, q * n:q * n + q], x_all[:, q * n:q * n + q]).then_inc(s_out, 16)
            sp.wait_ge(s_wf, 1)
            sp.dma_start(ytab[0:nt * P].rearrange("(p t) c -> p t c", p=P), rows[:]).then_inc(s_out, 16)

        @block.gpsimd
        def _(pool):
            pool.memset(mhalf[:], -0.5).then_inc(s_set, 1)
            pool.memset(zeros[:], 0.0).then_inc(s_set, 1)
            pool.memset(one[:], 1.0).then_inc(s_set, 1)
            pool.wait_ge(s_set, 3)
            for k in range(2):
                part = slice(nt // 2 * k, nt // 2 * (k + 1))
                pool.wait_ge(s_c, 6 * (k + 1))
                pool.tensor_tensor(ry[:, part], vrms[:, part], mhalf[:, part], ALU.pow).then_inc(s_p, 1)
            pool.tensor_tensor(rstd[:], veps[:], mhalf[:], ALU.pow).then_inc(s_p, 1)
            pool.wait_ge(s_p, 3)
            pool.tensor_tensor(acc_a[:], rstd[:], one[:], ALU.add).then_inc(s_acc, 1)
            pool.tensor_tensor(acc_b[:], rstd[:], minus[:], ALU.mult).then_inc(s_acc, 1)
            pool.wait_ge(s_acc, 2)
            pool.wait_ge(s_y, nb // 2)
            for b in range(nb // 2):
                one_seq = slice(TT * b, TT * b + TT)
                wide = lambda a: a[:, one_seq].unsqueeze(2).to_broadcast([P, TT, C])
                if b:
                    pool.wait_ge(s_base[0], b)
                pool.tensor_tensor(scaled[:], x_all[:, one_seq, :], wide(acc_a), ALU.mult).then_inc(s_mul, 1)
                pool.wait_ge(s_mul, b + 1)
                pool.tensor_tensor(x_all[:, one_seq, :], scaled[:], wide(acc_b), ALU.add).then_inc(s_base[0], 1)

        @block.vector
        def _(dve):
            chain = [0]

            def link(ins):
                chain[0] += 1
                ins.then_inc(s_c, 1)
                dve.wait_ge(s_c, chain[0])

            for k in range(2):
                h = nt // 2
                part = slice(h * k, h * (k + 1))
                for t in range(h * k, h * (k + 1)):
                    i = dve.bn_stats(stats[:, t], x_all[:, t])
                link(i)
                me, m2e, mo, m2o = (stats[:, part, j] for j in (1, 2, 4, 5))
                link(dve.tensor_tensor(a_[:, part], me, mo, ALU.subtract))
                dve.tensor_tensor(b_[:, part], m2e, m2o, ALU.add)
                link(dve.tensor_tensor(mean[:, part], me, mo, ALU.add))
                dve.tensor_scalar(minus[:, part], mean[:, part], -0.5, None, ALU.mult)
                link(dve.scalar_tensor_tensor(out=a_[:, part], in0=a_[:, part], scalar=C / 4.0, in1=a_[:, part], op0=ALU.mult,
                                              op1=ALU.mult))
                dve.tensor_scalar(mean[:, part], mean[:, part], 0.5, None, ALU.mult)
                link(dve.tensor_tensor(var[:, part], b_[:, part], a_[:, part], ALU.add))
                dve.tensor_scalar(veps[:, part], var[:, part], 1.0 / C, EPS, ALU.mult, ALU.add)
                link(dve.tensor_scalar(vrms[:, part], var[:, part], (1.0 + RMS_EPS) / C, RMS_EPS * EPS, ALU.mult, ALU.add))
            dve.tensor_scalar(gws[:], gws[:], rmsw[:, 0:1], None, ALU.mult).then_inc(s_scaled, 1)

            def make(n, b):
                if not isinstance(b, int) or b >= 2:
                    dve.wait_ge(s_tr, b - 1)
                    dve.wait_ge(s_kept, b - 1)
                for t in range(TT):
                    k = TT * b + t
                    i = dve.tensor_scalar(y[n][:, t], x_all[:, bass.ds(k, 1), :].rearrange("p a c -> p (a c)"),
                                          mean[:, bass.ds(k, 1)], ry[:, bass.ds(k, 1)], ALU.subtract, ALU.mult)
                i.then_inc(s_y, 1)

            def keep(n, b):
                dve.wait_ge(s_lr, b + 1)
                dve.tensor_copy(lg[:, bass.ds(TT * b, TT), :], psL[n][:]).then_inc(s_lg, 1)

            def step(n, s):
                if not isinstance(s, int) or s < nb:
                    make(n, s)
                if not isinstance(s, int) or s >= 2:
                    keep(n, s - 2)
            dve.wait_ge(s_p, 1)
            for s in range(2):
                step(s, s)
            with dve.Fori(1, nb // 4) as i:
                for n in range(2):
                    step(n, 2 * i + n)
            dve.wait_ge(s_p, 2)
            with dve.Fori(nb // 4, nb // 2) as i:
                for n in range(2):
                    step(n, 2 * i + n)
            for s in range(nb, nb + 2):
                step(s % 2, s)
            dve.wait_ge(s_lg, nb)
            for k in range(2):
                link(dve.tensor_reduce(top[k][:], lg[:], AX, ALU.max))
                link(dve.tensor_tensor(pen[:], lg[:], top[k][:].unsqueeze(2).to_broadcast([P, nt, E]), ALU.is_equal))
                link(dve.scalar_tensor_tensor(out=pen[:], in0=pen[:], scalar=-100.0, in1=iotae[:], op0=ALU.mult, op1=ALU.add))
                link(dve.tensor_reduce(low[:], pen[:], AX, ALU.min))
                link(dve.tensor_tensor(oh[k][:], pen[:], low[:].unsqueeze(2).to_broadcast([P, nt, E]), ALU.is_equal))
                if k == 0:
                    link(dve.scalar_tensor_tensor(out=lg[:], in0=oh[0][:], scalar=-1e30, in1=lg[:], op0=ALU.mult, op1=ALU.add))
            link(dve.tensor_tensor(d[:], top[1][:], top[0][:], ALU.subtract))
            dve.wait_ge(s_ex, 1)
            link(dve.tensor_scalar(wa[:], ex[:], 1.0, None, ALU.add))
            link(dve.reciprocal(wa[:], wa[:]))
            link(dve.tensor_tensor(wb[:], ex[:], wa[:], ALU.mult))
            bc = lambda a: a[:].unsqueeze(2).to_broadcast([P, nt, E])
            dve.tensor_tensor(mask[:], oh[0][:], oh[1][:], ALU.add)
            link(dve.tensor_tensor(oh[0][:], oh[0][:], bc(wa), ALU.mult))
            link(dve.tensor_tensor(oh[1][:], oh[1][:], bc(wb), ALU.mult))
            dve.tensor_tensor(rows[:, :, C:YP], oh[0][:], oh[1][:], ALU.add).then_inc(s_wf, 1)

        @block.tensor
        def _(pe):
            pe.wait_ge(s_scaled, 1)

            def turn(n, b):
                for t in range(TT):
                    k = pe.transpose(psX[n][:, P * t:P * t + P], y[n][:, t], ident[:])
                k.then_inc(s_tr, 1)

            def logits(n, b):
                for t in range(TT):
                    k = pe.matmul(psL[n][:, t], yT[n][:, P * t:P * t + P], gws[:], start=True, stop=True)
                k.then_inc(s_lr, 1)
            def step(n, s):
                if not isinstance(s, int) or s >= 2:
                    pe.wait_ge(s_yT, s - 1)
                    if not isinstance(s, int) or s >= 4:
                        pe.wait_ge(s_lg, s - 3)
                    logits(n, s - 2)
                if not isinstance(s, int) or s < nb:
                    pe.wait_ge(s_y, s + 1)
                    turn(n, s)
            lead_pairs(nb + 2, pe, step, 4)

        @block.scalar
        def _(act):
            def copy(n, b):
                act.wait_ge(s_y, b + 1)
                act.activation(rows[:, bass.ds(TT * b, TT), 0:C], y[n][:], ACT.Copy).then_inc(s_kept, 1)
                act.wait_ge(s_tr, b + 1)
                if not isinstance(b, int) or b >= 2:
                    act.wait_ge(s_lr, b - 1)
                act.activation(yT[n][:], psX[n][:], ACT.Copy).then_inc(s_yT, 1)

            act.activation(warm[:], rmsw[:, 0:1], ACT.Exp)
            for w in (w1s, w2s):
                act.activation(w[:], w[:], ACT.Copy, scale=rmsw[:, 0:1])
            lead_pairs(nb, act, copy)

            def raise_x(b):
                for t in range(TT):
                    k = TT * b + t
                    x = x_all[:, bass.ds(k, 1), :].rearrange("p a c -> p (a c)")
                    i = act.activation(x, x, ACT.Identity, bias=acc_b[:, bass.ds(k, 1)], scale=acc_a[:, bass.ds(k, 1)])
                i.then_inc(s_base[1], 1)

            act.wait_ge(s_acc, 2)
            with act.Fori(nb // 2, nb - 2) as b:
                raise_x(b)
            act.wait_ge(s_c, 12 + 6 + 5 + 1)
            act.activation(ex[:], d[:], ACT.Exp).then_inc(s_ex, 1)
            with act.Fori(nb - 2, nb) as b:
                raise_x(b)


def dispatch(nc, mask, ahead, s_out, ghl, first, past, slot, emap, nb):
    nt = nb * TT
    ntl = 2 * nt + 2 * E
    with ExitStack() as ctx:
        sb = lambda name, shape, dt=F32: ctx.enter_context(nc.sbuf_tensor("di_" + name, shape, dt))
        sem = lambda name: ctx.enter_context(nc.semaphore("di_" + name))
        tri, ones, strict, iota, tileno, jcol = (ahead[n] for n in ("tri", "ones", "strict", "iota", "tileno", "jcol"))
        pin = sb("pin", [nt, E, P], BF16)
        rank = sb("rank", [nt, E, P])
        pex, pinc = sb("pex", [nt, E]), sb("pinc", [nt, E])
        cnt, tiles, last, start, onesf = (sb(n, [P, E]) for n in ("cnt", "tiles", "last", "start", "onesf"))
        full = sb("full", [P, E, nt])
        cmp = sb("cmp", [P, ntl, E])
        prod = sb("prod", [P, ntl, E])
        ef, rel, o = (sb(n, [P, ntl]) for n in ("ef", "rel", "o"))
        psA = ctx.enter_context(nc.psum_tensor("di_psA", [P, 512], F32))
        psL = ctx.enter_context(nc.psum_tensor("di_psL", [P, 2, 512], F32))
        psO = ctx.enter_context(nc.psum_tensor("di_psO", [P, 512], F32))
        s_pre, s_kept, s_rank, s_c = (sem(n) for n in ("prefixes", "kept", "ranks", "chain"))
        block = ctx.enter_context(nc.Block())

        @block.sync
        def _(sp):
            sp.wait_ge(s_out, 16 * OUT_DMAS)

        @block.tensor
        def _(pe):
            pe.matmul(psA[:, 0:nt * E], ones[:], mask[:].rearrange("p t e -> p (t e)"), start=True, stop=True)
            for e in range(E):
                i = pe.matmul(psL[0:nt, e // 4, P * (e % 4):P * (e % 4) + P], mask[:, :, e], tri[:], start=True, stop=True)
            i.then_inc(s_pre, 1)
            pe.wait_ge(s_kept, 1)
            pe.matmul(psO[0:nt, 0:E], strict[:], pin[:, :, P - 1], start=True, stop=True).then_inc(s_pre, 1)

        @block.vector
        def _(dve):
            chain = [0]

            def link(ins):
                chain[0] += 1
                ins.then_inc(s_c, 1)
                dve.wait_ge(s_c, chain[0])

            def sum_e(dst, src):
                return dve.tensor_reduce(dst, src, AX, ALU.add)
            dve.memset(onesf[:], 1.0)
            dve.wait_ge(s_pre, 1)
            dve.tensor_copy(pin[:], psL[0:nt, 0:2].rearrange("p a (e k) -> p (a e) k", e=4)).then_inc(s_kept, 1)
            link(dve.tensor_reduce(cnt[:], psA[:, 0:nt * E].rearrange("p (t e) -> p e t", e=E), AX, ALU.add))
            link(dve.tensor_scalar(cnt[:], cnt[:], 1.0 / P, None, ALU.mult))
            dve.wait_ge(s_pre, 2)
            dve.tensor_copy(pex[:], psO[0:nt, 0:E]).then_inc(s_kept, 1)
            link(dve.tensor_tensor(full[:], iota[:, 0:nt].unsqueeze(1).to_broadcast([P, E, nt]),
                                   cnt[:].unsqueeze(2).to_broadcast([P, E, nt]), ALU.is_lt))
            link(sum_e(tiles[:], full[:]))
            link(dve.tensor_scalar(tiles[:], tiles[:], 1.0, None, ALU.add))
            link(dve.tensor_tensor_scan(last[:], onesf[:], tiles[:], 0.0, ALU.mult, ALU.add))
            dve.tensor_tensor(start[:], last[:], tiles[:], ALU.subtract)
            tno = iota[:, 0:ntl].unsqueeze(2).to_broadcast([P, ntl, E])
            row = lambda a, n=P: a[0:n].unsqueeze(1).to_broadcast([n, ntl, E])
            link(dve.tensor_tensor(cmp[:], row(last), tno, ALU.is_le))
            link(sum_e(ef[:], cmp[:]))
            link(dve.tensor_scalar(ef[:], ef[:], float(E - 1), None, ALU.min))
            dve.tensor_copy(emap[:], ef[:])
            link(dve.tensor_tensor(cmp[:], row(iota[:, 0:E]), ef[:].unsqueeze(2).to_broadcast([P, ntl, E]), ALU.is_equal))
            link(dve.tensor_tensor(prod[:], cmp[:], row(start), ALU.mult))
            link(sum_e(rel[:], prod[:]))
            link(dve.tensor_tensor(rel[:], iota[:, 0:ntl], rel[:], ALU.subtract))
            dve.tensor_scalar(slot[:], rel[:], float(P), jcol[:, 0:1], ALU.mult, ALU.add)
            link(dve.tensor_scalar(o[:], rel[:], float(P), None, ALU.mult))
            dve.wait_ge(s_kept, 2)
            link(dve.tensor_tensor(pinc[:], psO[0:nt, 0:E], pin[:, :, P - 1], ALU.add))
            for dst, src in ((first, pex), (past, pinc)):
                link(dve.tensor_tensor(prod[0:nt], cmp[0:nt], row(src, nt), ALU.mult))
                link(sum_e(dst[:], prod[0:nt]))
                link(dve.tensor_tensor(dst[:], dst[:], o[0:nt], ALU.subtract))
            dve.tensor_copy(ghl[:, 0, :, P], tileno[:])
            link(dve.memset(ghl[:, 1, :, P], 0.0))

        @block.gpsimd
        def _(pool):
            counts = pex[:].unsqueeze(2).to_broadcast([nt, E, P])
            pool.wait_ge(s_kept, 2)
            pool.tensor_tensor(rank[:], pin[:], counts, ALU.add).then_inc(s_rank, 1)
            pool.tensor_tensor(ghl[:, 0, :, 0:P], pin[:], counts, ALU.add).then_inc(s_rank, 1)
            pool.wait_ge(s_rank, 2)
            pool.tensor_tensor(ghl[:, 1, :, 0:P], rank[:], ghl[:, 0, :, 0:P], ALU.subtract).then_inc(s_rank, 1)


def experts(nc, ident, ahead, ghl, first, past, slot, emap, ytab, out, nb):
    nt = nb * TT
    ntl = 2 * nt + 2 * E
    with ExitStack() as ctx:
        sb = lambda name, shape, dt=F32: ctx.enter_context(nc.sbuf_tensor("ex_" + name, shape, dt))
        sem = lambda name: ctx.enter_context(nc.semaphore("ex_" + name))
        w1s, w2s, w3s, jcol = (ahead[n] for n in ("w1s", "w2s", "w3s", "jcol"))
        iota = ahead["iota"][0:nt, 0:P]
        after = [sb(f"after{i}", [nt, P], BF16) for i in range(2)]
        oh = [sb(f"oh{i}", [nt, P], BF16) for i in range(2)]
        junk = sb("junk", [P, P], BF16)
        carried, waited = sb("carried", [P, 1]), [sb(f"waited{i}", [P, 1]) for i in range(4)]
        place = [sb(f"place{i}", [P, 1]) for i in range(2)]
        pad = [sb(f"pad{i}", [P, 1]) for i in range(2)]
        rowf = [sb(f"rowf{i}", [P, 1]) for i in range(2)]
        idx = [sb(f"idx{i}", [P, 1], I32) for i in range(8)]
        xg = [sb(f"xg{i}", [P, YP]) for i in range(4)]
        w = [sb(f"w{i}", [P, 1]) for i in range(2)]
        xT = [sb(f"xT{i}", [P, P]) for i in range(2)]
        up = [sb(f"up{i}", [P, DE]) for i in range(2)]
        h = [sb(f"h{i}", [P, DE]) for i in range(2)]
        hT = [sb(f"hT{i}", [P, len(FC), P]) for i in range(2)]
        y = [sb(f"y{i}", [P, C]) for i in range(2)]
        ps = lambda n: ctx.enter_context(nc.psum_tensor("ex_" + n, [P, 512], F32))
        psI, psX, psH, psY = ps("psI"), ps("psX"), ps("psH"), ps("psY")
        psU = [ps("psU0"), ps("psU1")]
        psG = [ps("psG0"), ps("psG1")]
        s_aft, s_oh, s_rk, s_pl, s_id, s_x, s_xT, s_g, s_s, s_w, s_h, s_ht, s_hc, s_y, s_yc, s_g2, s_carry = (sem(n) for n in (
            "after", "onehot", "ranks", "place", "index", "turned", "xT_ready", "gate_ready", "silu",
            "weight", "h_ready", "h_turned", "hT_ready", "down_ready", "y_ready", "up_ready", "zero_set"))
        s_gt = [sem(f"gathered{n}") for n in range(4)]
        s_sc = [sem(f"scattered{n}") for n in range(2)]
        block = ctx.enter_context(nc.Block())
        LOOK = 4
        GATH = 3

        def steps(eng, fn, before, after_, unroll=8):
            lo, hi = unroll, ntl - unroll
            for s in range(-before, lo):
                fn(s, s % unroll)
            with eng.Fori(lo // unroll, hi // unroll) as i:
                for n in range(unroll):
                    fn(unroll * i + n, n)
            for s in range(hi, ntl + after_):
                fn(s, s % unroll)

        def has(t):
            return not isinstance(t, int) or 0 <= t < ntl

        def wait(eng, s, value, since=1):
            if not isinstance(value, int) or value >= since:
                eng.wait_ge(s, value)

        @block.vector
        def _(dve):
            def onehot(t, k):
                n = k % 2
                dve.tensor_scalar(after[n][:], iota, first[:, bass.ds(t, 1)], None, ALU.is_ge).then_inc(s_aft, 1)
                wait(dve, s_aft, t + 1)
                dve.scalar_tensor_tensor(out=oh[n][:], in0=iota, scalar=past[:, bass.ds(t, 1)], in1=after[n][:],
                                         op0=ALU.is_lt, op1=ALU.mult).then_inc(s_oh, 1)

            def index(t, k):
                n = k % 2
                wait(dve, s_rk, t + 1)
                dve.tensor_scalar(junk[:], psI[:, 0:P], slot[:, bass.ds(t, 1)], 0.0, ALU.is_le, ALU.add, accum_out=place[n][:])\
                    .then_inc(s_pl, 1)
                wait(dve, s_pl, 3 * t + 1)
                dve.scalar_tensor_tensor(out=pad[n][:], in0=place[n][:], scalar=float(P), in1=jcol[:, n:n + 1], op0=ALU.is_ge, op1=ALU.mult)\
                   .then_inc(s_pl, 1)
                dve.scalar_tensor_tensor(out=rowf[n][:], in0=place[n][:], scalar=float(nt), in1=psI[:, P:P + 1], op0=ALU.mult,
                                         op1=ALU.add).then_inc(s_pl, 1)
                wait(dve, s_pl, 3 * t + 3)
                dve.tensor_tensor(idx[k % 8][:], rowf[n][:], pad[n][:], ALU.add).then_inc(s_id, 1)

            def step(s, k):
                if has(s):
                    n = k % 2
                    wait(dve, s_g, s + 1)
                    wait(dve, s_s, 2 * s + 2)
                    dve.scalar_tensor_tensor(out=h[n][:], in0=psG[n][:, 0:DE], scalar=w[n][:, 0:1], in1=up[n][:], op0=ALU.mult,
                                             op1=ALU.mult).then_inc(s_h, 1)
                if has(s + LOOK):
                    index(s + LOOK, k + LOOK)
                if has(s + LOOK + 1):
                    onehot(s + LOOK + 1, k + LOOK + 1)
                if has(s - 1):
                    m = (k - 1) % 2
                    wait(dve, s_y, s)
                    wait(dve, s_sc[m], 8 * (s - 1 - m))
                    dve.tensor_copy(y[m][:], psY[:, 0:C]).then_inc(s_yc, 1)
            steps(dve, step, LOOK + 1, 1)

        @block.gpsimd
        def _(pool):
            pool.memset(carried[:], 0.0).then_inc(s_carry, 4)
            pool.wait_ge(s_carry, 4)

            def carry(s, n):
                if not isinstance(s, int):
                    pool.wait_ge(s_carry, 2 * (s - 8) + n // 2 + 1)
                    pool.tensor_tensor(waited[n][:], carried[:], carried[:], ALU.add).then_inc(s_carry, 1)

            def gather(t, k):
                wait(pool, s_id, t + 1)
                carry(t - GATH, k % 2)
                pool.indirect_dma_start(xg[k % 4][:], None, ytab, bass.IndirectOffsetOnAxis(ap=idx[k % 8][:], axis=0))\
                    .then_inc(s_gt[k % 4], 16)

            def step(s, k):
                if has(s + GATH):
                    gather(s + GATH, k + GATH)
                if has(s - 1):
                    m = (k - 1) % 2
                    wait(pool, s_yc, s)
                    wait(pool, s_sc[m], 8 * (s - 1 - m))
                    carry(s, 2 + k % 2)
                    pool.indirect_dma_start(out, bass.IndirectOffsetOnAxis(ap=idx[(k - 1) % 8][:], axis=0), y[(k - 1) % 2][:],
                                            None, compute_op=ALU.add).then_inc(s_sc[m], 16)
            steps(pool, step, GATH, 1)
            for n in range(2):
                pool.wait_ge(s_sc[n], 8 * ntl)

        @block.tensor
        def _(pe):
            regs = [pe.alloc_register(f"expert{k}") for k in range(8)]

            def number(k):
                return bass.ds(pe.snap(regs[k % 8], min_val=0, max_val=E - 1), 1)

            def flat(a):
                return a.rearrange("p a c -> p (a c)")

            def turn(t, k):
                n = k % 4
                wait(pe, s_gt[n], 4 * (t - n) + 16)
                pe.transpose(psX[:, 0:P], xg[n][:, 0:C], ident[:]).then_inc(s_x, 1)

            def step(s, k):
                if has(s - 1):
                    m = (k - 1) % 2
                    wait(pe, s_h, s)
                    for f, wd in enumerate(FC):
                        i = pe.transpose(psH[0:wd, P * f:P * f + P], h[m][:, P * f:P * f + wd], ident[:])
                    i.then_inc(s_ht, 1)
                if has(s):
                    n = k % 2
                    e = number(k)
                    wait(pe, s_xT, s + 1)
                    pe.matmul(psU[n][:, 0:DE], xT[n][:], flat(w1s[:, e, :]), start=True, stop=True).then_inc(s_g2, 1)
                    pe.matmul(psG[n][:, 0:DE], xT[n][:], flat(w2s[:, e, :]), start=True, stop=True).then_inc(s_g, 1)
                if has(s + LOOK):
                    t = s + LOOK
                    pe.reg_load(regs[(k + LOOK) % 8], emap[0:1, bass.ds(t, 1)])
                    e = number(k + LOOK)
                    wait(pe, s_oh, t + 1)
                    for a in range(2):
                        i = pe.matmul(psI[:, 0:P + 1], oh[(k + LOOK) % 2][:], flat(ghl[:, a, e, :]), start=(a == 0), stop=(a == 1))
                    i.then_inc(s_rk, 1)
                if has(s + 1):
                    turn(s + 1, k + 1)
                if has(s - 1):
                    m = (k - 1) % 2
                    e = number(k - 1)
                    wait(pe, s_hc, s)
                    wait(pe, s_yc, s - 1)
                    for f, wd in enumerate(FC):
                        i = pe.matmul(psY[:, 0:C], hT[m][0:wd, f], flat(w3s[0:wd, f, e, :]), start=(f == 0), stop=(f == len(FC) - 1))
                    i.then_inc(s_y, 1)
            steps(pe, step, LOOK, 1)

        @block.scalar
        def _(act):
            def step(s, k):
                if has(s - 1):
                    m = (k - 1) % 2
                    wait(act, s_ht, s)
                    act.activation(hT[m][:, 0:2].rearrange("p a c -> p (a c)"), psH[:, 0:2 * P], ACT.Copy)
                    act.activation(hT[m][0:FC[2], 2], psH[0:FC[2], 2 * P:3 * P], ACT.Copy).then_inc(s_hc, 1)
                if has(s):
                    n = k % 2
                    wait(act, s_g2, s + 1)
                    act.activation(up[n][:], psU[n][:, 0:DE], ACT.Silu).then_inc(s_s, 1)
                    e = bass.ds(act.value_load(emap[0:1, bass.ds(s, 1)], min_val=0, max_val=E - 1) + C, 1)
                    act.activation(w[n][:], xg[k % 4][:, e], ACT.Copy).then_inc(s_s, 1)
                if has(s + 1):
                    m = (k + 1) % 2
                    wait(act, s_x, s + 2)
                    act.activation(xT[m][:], psX[:, 0:P], ACT.Copy).then_inc(s_xT, 1)
            steps(act, step, 1, 1)


def two_blocks_kernel(nc, x, wattnT, wprojT, rw, rb, w1, b1, w2, b2, win, wout, prm, rows, gwT, rmsw, W1T, W2T, W3T, cst, out):
    nb = NB
    nt = nb * TT

    def dram(name, shape, dt=F32):
        return nc.dram_tensor(name, shape, dt).ap()

    qkv_scr = dram("qkv_scr", [2, 2, 3, P, T], BF16)
    max_scr = dram("max_scr", [G, 2 * HG, T], BF16)
    y_scr = dram("y_scr", [nb, 2 * D, H, T])
    rec_scr = dram("rec_scr", [nb, H, T])
    x_scr = dram("x_scr", [P, nt, C])
    norm_tab = dram("norm_tab", [P, nt, C])
    score_tab = dram("score_tab", [P, nt, E])
    expert_tab = dram("expert_tab", [nt * P + 2 * P, YP])
    with ExitStack() as keep:
        def sb(ctx, name, shape, dt=F32):
            return ctx.enter_context(nc.sbuf_tensor(name, shape, dt))

        x_all = sb(keep, "x_all", [P, nt, C])
        ident = sb(keep, "ident", [P, P])
        with ExitStack() as ctx:
            scores = sb(ctx, "sc", [P, nt, E])
            idx = sb(ctx, "idx", [P, 2 * E], I32)
            shared = ([sb(ctx, f"ysb{i}", [P, T]) for i in range(2)],
                      [sb(ctx, "sums0", [(nb - LATE) * 8, H * T // 8]), sb(ctx, "sums1", [P, LATE * H * T // P])],
                      [ctx.enter_context(nc.semaphore(f"y_written{i}")) for i in range(2)],
                      ctx.enter_context(nc.semaphore("sums_loaded")),
                      ctx.enter_context(nc.semaphore("sums_inverted")),
                      ctx.enter_context(nc.semaphore("rec_written")),
                      ctx.enter_context(nc.semaphore("scores_stored")))
            attention(nc, x_all, ident, x, wattnT, qkv_scr, max_scr, y_scr, rec_scr, shared, cst["c_ident"], cst["c_identb"],
                      cst["c_maskq"], cst["c_maskk"], cst["c_rows"], nb)
            project(nc, x_all, y_scr, rec_scr, shared, wprojT, x_scr, rw, rb, norm_tab, score_tab, scores, ident, nb)
            choose(nc, scores, shared[-1], ident, cst, idx, nb)
            expert_choice(nc, idx, norm_tab, score_tab, w1, b1, w2, b2, x_scr, ident, nb)
        with ExitStack() as ctx:
            ahead, loads = ahead_loads(nc, ctx, nb, gwT, rmsw, W1T, W2T, W3T, cst)
            mixer(nc, x_all, x_scr, ident, win, wout, prm, rows, loads, nb)
            mask = sb(ctx, "mask", [P, nt, E], BF16)
            ghl = sb(ctx, "ghl", [nt, 2, E, P + 1], BF16)
            first = sb(ctx, "first", [nt, 2 * nt + 2 * E])
            past = sb(ctx, "past", [nt, 2 * nt + 2 * E])
            slot = sb(ctx, "slot", [P, 2 * nt + 2 * E])
            emap = sb(ctx, "emap", [P, 2 * nt + 2 * E], I32)
            with nc.semaphore("experts_ready") as s_out:
                rows_sb = sb(ctx, "table_rows", [P, nt, YP])
                zeros = sb(ctx, "table_zeros", [P, YP])
                gate(nc, x_all, ident, ahead, mask, rows_sb, zeros, expert_tab, s_out, out, nb)
                dispatch(nc, mask, ahead, s_out, ghl, first, past, slot, emap, nb)
            experts(nc, ident, ahead, ghl, first, past, slot, emap, expert_tab, out, nb)


def constants(nt, bf16):
    i = np.arange(P)
    wide = lambda a, shape, dt: np.ascontiguousarray(np.broadcast_to(a, shape)).astype(dt)
    below = np.where(i[None, :] > i[:, None], np.float32(-1e30), np.float32(0))
    start = 2.0 ** (-2.0 ** (-(np.log2(H) - 3)))
    slopes = np.array([start * start ** k for k in range(H)], dtype=np.float32).astype(np.float64)
    rows, rest = [], slopes[:, None] * (np.arange(T) - T / 2)
    for _ in range(3):
        part = rest.astype(np.float32).astype(bf16)
        rows.append(part)
        rest = rest - part.astype(np.float64)
    rows += [np.ones((H, T), bf16)] * 3 + [-np.ones((H, T), bf16)] * 2
    digits = np.array([[4.0 ** (7 - k) * j for j in (1, 1, 2, 3)] for k in range(9)])
    return dict(
        c_ident=np.eye(P, dtype=np.float32), c_identb=np.eye(P, dtype=np.float32).astype(bf16),
        c_maskq=wide(below[:, None], (P, HG, P), bf16), c_maskk=wide(below.T[:, None], (P, HG, P), bf16),
        c_rows=np.stack(rows).reshape(8, H * T),
        c_same=(i[:, None] % E == i[None, :] % E).astype(np.float16),
        c_tri=(i[:, None] <= i[None, :]).astype(bf16), c_ones=np.ones((P, P), bf16),
        c_strict=(i[:, None] < i[None, :]).astype(bf16),
        c_step=wide(digits, (P, 9, 4), np.float32),
        c_iota=wide(np.arange(float(KTOP)), (P, KTOP), np.float32), c_tileno=wide(i[:, None], (P, E), bf16),
        c_slotno=wide(i[:, None] + 128.0 * (np.arange(2 * E) % 2)[None], (P, 2 * E), np.float32),
        c_iotae=wide(np.arange(float(E)), (P, nt, E), np.float32))


def layout(a):
    nt = NB * TT
    order = np.arange(C).reshape(H, D).T.reshape(-1)
    c = {k: np.asarray(v) for k, v in a.items()}
    w_attn = c["L0_attn_W_attn"]
    return dict(
        x=c["L0_attn_x"].reshape(nt, P, C).transpose(1, 0, 2), wattnT=np.concatenate([w_attn[0:C][order], w_attn[C:2 * C][order], w_attn[2 * C:]]).T,
        wprojT=c["L0_attn_W_proj"].T[order], rw=c["L0_ffn_router_w"], rb=c["L0_ffn_router_b"].reshape(1, E),
        w1=c["L0_ffn_w1"], b1=c["L0_ffn_b1"].reshape(E, 4, P).transpose(2, 0, 1),
        w2=c["L0_ffn_w2"].reshape(E, 4, P, C).transpose(0, 2, 1, 3), b2=c["L0_ffn_b2"].reshape(1, E, C),
        win=c["L1_attn_in_proj_w"], wout=c["L1_attn_out_proj_w"],
        prm=np.stack([c["L1_attn_in_proj_b"][:C], c["L1_attn_in_proj_b"][C:], *c["L1_attn_conv_w"][:, 0].T,
                      c["L1_attn_conv_b"], c["L1_attn_logit_a"], c["L1_attn_ssm_b"], c["L1_attn_ssm_c"],
                      c["L1_attn_ssm_d"]], 1),
        rows=np.stack([c["L1_attn_out_proj_b"], c["L1_attn_ln_w"], c["L1_attn_ln_b"]]),
        gwT=c["L1_ffn_gate_w"].T, rmsw=c["L1_ffn_rms_w"].reshape(P, 1), W1T=c["L1_ffn_W1"].transpose(2, 0, 1),
        W2T=c["L1_ffn_W2"].transpose(2, 0, 1), W3T=c["L1_ffn_W3"].transpose(2, 0, 1))


def kernel(**inputs):
    import concourse.bacc as _bacc
    from concourse.bass_utils import run_bass_kernel_spmd as _run

    nt = NB * TT
    nc = _bacc.Bacc("TRN2", target_bir_lowering=False, num_devices=1)
    host = {**layout(inputs), **constants(nt, mybir.dt.np(BF16))}
    arrays, args, cst = {}, {}, {}
    for name, a in host.items():
        a = np.ascontiguousarray(a)
        arrays[name] = a
        ap = nc.dram_tensor(name, a.shape, mybir.dt.from_np(a.dtype), kind="ExternalInput").ap()
        if name[0:2] == "c_":
            cst[name] = ap
        else:
            args[name] = ap
    out = nc.dram_tensor("out", [nt * P + 2 * P, C], F32, kind="ExternalOutput").ap()
    two_blocks_kernel(nc, cst=cst, out=out, **args)
    r = _run(nc, [arrays], core_ids=[0])
    return r.results[0]["out"][0:nt * P].reshape(P, nt, C).transpose(1, 0, 2).reshape(NB, T, C)
```
